# Optimizing a Trainium2 kernel written in Bass

```python
import numpy as np
import jax
import jax.numpy as jnp

def _softmax(x, axis=-1):
    return jax.nn.softmax(x, axis=axis)

def _gelu(x):
    return jax.nn.gelu(x, approximate=True)

def _silu(x):
    return jax.nn.silu(x)

def _sigmoid(x):
    return jax.nn.sigmoid(x)

def _layernorm(x, axis=-1, eps=1e-05):
    m = jnp.mean(x, axis=axis, keepdims=True)
    v = jnp.var(x, axis=axis, keepdims=True)
    return (x - m) / jnp.sqrt(v + eps)

def _scatter_add(tgt, idx, src, axis=0):
    return tgt.at[idx].add(src)

def _segment_sum(src, seg, n):
    return jax.ops.segment_sum(src, seg, n)
kernel_name = 'mk_early_fusion_embed_d2_tok_img1024_r4_03e2ab'

def setup_inputs(seed: int=0):
    np.random.seed(seed)
    _w = jnp.asarray

    def _rec_inputs():
        import jax
        import jax.numpy as jnp
        _rk = jax.random.key(seed)
        x = -0.000392918 + 0.999932 * jax.random.normal(jax.random.fold_in(_rk, 1), (16, 256, 256, 1), jnp.float32)
        x_txt = jax.random.randint(jax.random.fold_in(_rk, 51), (16, 32), 0, 12564, jnp.int32)
        return (x, x_txt)
    x, x_txt = _rec_inputs()

    def _L0_tok_setup():
        import jax, jax.numpy as jnp
        import numpy as np
        INV_SQRT2 = 0.7071067811865476
        LEVEL = 3

        def _split(x, axis):
            ax = axis % x.ndim
            sl0 = [slice(None)] * x.ndim
            sl0[ax] = slice(0, None, 2)
            sl1 = [slice(None)] * x.ndim
            sl1[ax] = slice(1, None, 2)
            x0, x1 = (x[tuple(sl0)], x[tuple(sl1)])
            return ((x0 + x1) * INV_SQRT2, (x0 - x1) * INV_SQRT2)

        def _merge(lo, hi, axis):
            ax = axis % lo.ndim
            e = (lo + hi) * INV_SQRT2
            o = (lo - hi) * INV_SQRT2
            s = jnp.stack([e, o], axis=ax + 1)
            shape = list(lo.shape)
            shape[ax] *= 2
            return s.reshape(shape)

        def _dwt2(x):
            lo, hi = _split(x, -1)
            a, h = _split(lo, -2)
            v, d = _split(hi, -2)
            return (a, h, v, d)

        def _idwt2(a, h, v, d):
            lo = _merge(a, h, -2)
            hi = _merge(v, d, -2)
            return _merge(lo, hi, -1)
        key = jax.random.key(seed)
        ks = jax.random.split(key, 8)
        B, H, W = (16, 256, 256)
        x = jax.random.normal(ks[0], (B, H, W, 1), dtype=jnp.float32)
        na = H // 8 * (W // 8)
        n2 = H // 4 * (W // 4)
        n1 = H // 2 * (W // 2)
        scale = 0.02
        Wa = jax.random.normal(ks[1], (na, 1), dtype=jnp.float32) * scale
        ba = jnp.zeros((1,), jnp.float32)
        Wd1 = jax.random.normal(ks[2], (3 * na, 3), dtype=jnp.float32) * scale
        bd1 = jnp.zeros((3,), jnp.float32)
        Wd2 = jax.random.normal(ks[3], (3 * n2, 3), dtype=jnp.float32) * scale
        bd2 = jnp.zeros((3,), jnp.float32)
        Wd3 = jax.random.normal(ks[4], (3 * n1, 3), dtype=jnp.float32) * scale
        bd3 = jnp.zeros((3,), jnp.float32)
        return {'x': x, 'Wa': Wa, 'ba': ba, 'Wd1': Wd1, 'bd1': bd1, 'Wd2': Wd2, 'bd2': bd2, 'Wd3': Wd3, 'bd3': bd3}
    _L0_tok_all = _L0_tok_setup()
    _L0_tok_in = {k: v for k, v in _L0_tok_all.items() if k in ('Wa', 'ba', 'Wd1', 'bd1', 'Wd2', 'bd2', 'Wd3', 'bd3')}
    del _L0_tok_all

    def _L0_txt_setup():
        import jax, jax.numpy as jnp
        import numpy as np
        NUM_EMB = 50257
        EMB_DIM = 256
        RANK = 8
        ALPHA = 16.0
        SCALING = ALPHA / RANK
        key = jax.random.key(seed)
        k1, k2, k3, k4 = jax.random.split(key, 4)
        x = jax.random.randint(k1, (8, 512), 0, NUM_EMB, dtype=jnp.int64)
        weight = jax.random.normal(k2, (NUM_EMB, EMB_DIM), dtype=jnp.float32)
        lora_A = jax.random.normal(k3, (NUM_EMB, RANK), dtype=jnp.float32)
        lora_B = jax.random.normal(k4, (RANK, EMB_DIM), dtype=jnp.float32)
        return {'x': x, 'weight': weight, 'lora_A': lora_A, 'lora_B': lora_B}
    _L0_txt_all = _L0_txt_setup()
    _L0_txt_in = {k: v for k, v in _L0_txt_all.items() if k in ('weight', 'lora_A', 'lora_B')}
    del _L0_txt_all

    def _L0_attn_setup():
        import jax, jax.numpy as jnp
        import numpy as np
        NUM_HEADS = 16
        HIDDEN = 256
        ATTN_DIM = 64
        HEAD_OUT = 64
        OUT_DIM = 256
        BATCH, SEQ = (2, 512)

        def _split_heads(y, h):
            b, s, _ = y.shape
            return y.reshape(b, s, h, -1).transpose(0, 2, 1, 3)
        key = jax.random.key(seed)
        ks = jax.random.split(key, 9)
        s_in = 1.0 / np.sqrt(HIDDEN)
        s_o = 1.0 / np.sqrt(NUM_HEADS * HEAD_OUT)
        return {'x': jax.random.normal(ks[0], (BATCH, SEQ, HIDDEN), dtype=jnp.float32), 'Wq': jax.random.uniform(ks[1], (HIDDEN, NUM_HEADS * ATTN_DIM), jnp.float32, -s_in, s_in), 'bq': jax.random.uniform(ks[2], (NUM_HEADS * ATTN_DIM,), jnp.float32, -s_in, s_in), 'Wk': jax.random.uniform(ks[3], (HIDDEN, NUM_HEADS * ATTN_DIM), jnp.float32, -s_in, s_in), 'bk': jax.random.uniform(ks[4], (NUM_HEADS * ATTN_DIM,), jnp.float32, -s_in, s_in), 'Wv': jax.random.uniform(ks[5], (HIDDEN, NUM_HEADS * HEAD_OUT), jnp.float32, -s_in, s_in), 'bv': jax.random.uniform(ks[6], (HIDDEN, NUM_HEADS * HEAD_OUT)[1:], jnp.float32, -s_in, s_in), 'Wo': jax.random.uniform(ks[7], (NUM_HEADS * HEAD_OUT, OUT_DIM), jnp.float32, -s_o, s_o), 'bo': jax.random.uniform(ks[8], (OUT_DIM,), jnp.float32, -s_o, s_o)}
    _L0_attn_all = _L0_attn_setup()
    _L0_attn_in = {k: v for k, v in _L0_attn_all.items() if k in ('Wq', 'bq', 'Wk', 'bk', 'Wv', 'bv', 'Wo', 'bo')}
    del _L0_attn_all

    def _L0_ffn_setup():
        import jax, jax.numpy as jnp
        import numpy as np
        EMB = 256
        HEADS = 16
        SEQ = 512
        LATENT = 128
        N_EXP = 8
        TOP_K = 2
        EXP_DIM = 512
        BATCH = 2
        EPS = 1e-06

        def _rmsnorm(x, g):
            return x * jax.lax.rsqrt(jnp.mean(x * x, axis=-1, keepdims=True) + EPS) * g

        def _mla(h, Wq, Wdkv, Wuk, Wuv, Wo):
            B, S, D = h.shape
            hd = D // HEADS
            q = (h @ Wq).reshape(B, S, HEADS, hd)
            c = h @ Wdkv
            k = (c @ Wuk).reshape(B, S, HEADS, hd)
            v = (c @ Wuv).reshape(B, S, HEADS, hd)
            scores = jnp.einsum('bqhd,bkhd->bhqk', q, k) / jnp.sqrt(jnp.asarray(hd, h.dtype))
            causal = jnp.tril(jnp.ones((S, S), bool))
            scores = jnp.where(causal, scores, jnp.asarray(-1000000000.0, h.dtype))
            a = jax.nn.softmax(scores, axis=-1)
            out = jnp.einsum('bhqk,bkhd->bqhd', a, v).reshape(B, S, D)
            return out @ Wo

        def _moe(h, gate_w, w1, w2):
            B, S, D = h.shape
            t = h.reshape(B * S, D)
            logits = t @ gate_w
            top_v, top_i = jax.lax.top_k(logits, TOP_K)
            gates = jax.nn.softmax(top_v, axis=-1)
            T = t.shape[0]
            combine = jnp.zeros((T, N_EXP), t.dtype).at[jnp.arange(T)[:, None], top_i].add(gates)
            hid = jax.nn.silu(jnp.einsum('td,edh->teh', t, w1))
            ye = jnp.einsum('teh,ehd->ted', hid, w2)
            out = jnp.einsum('te,ted->td', combine, ye)
            return out.reshape(B, S, D)
        key = jax.random.key(seed)
        ks = jax.random.split(key, 12)
        s = 0.02
        return {'x': jax.random.normal(ks[0], (BATCH, SEQ, EMB), jnp.float32), 'g1': jnp.ones((EMB,), jnp.float32), 'Wq': jax.random.normal(ks[1], (EMB, EMB), jnp.float32) * s, 'Wdkv': jax.random.normal(ks[2], (EMB, LATENT), jnp.float32) * s, 'Wuk': jax.random.normal(ks[3], (LATENT, EMB), jnp.float32) * s, 'Wuv': jax.random.normal(ks[4], (LATENT, EMB), jnp.float32) * s, 'Wo': jax.random.normal(ks[5], (EMB, EMB), jnp.float32) * s, 'g2': jnp.ones((EMB,), jnp.float32), 'gate_w': jax.random.normal(ks[6], (EMB, N_EXP), jnp.float32) * s, 'w1': jax.random.normal(ks[7], (N_EXP, EMB, EXP_DIM), jnp.float32) * s, 'w2': jax.random.normal(ks[8], (N_EXP, EXP_DIM, EMB), jnp.float32) * s}
    _L0_ffn_all = _L0_ffn_setup()
    _L0_ffn_in = {k: v for k, v in _L0_ffn_all.items() if k in ('g1', 'Wq', 'Wdkv', 'Wuk', 'Wuv', 'Wo', 'g2', 'gate_w', 'w1', 'w2')}
    del _L0_ffn_all

    def _L1_attn_setup():
        import jax, jax.numpy as jnp
        import numpy as np
        B, T, D, R = (4, 512, 256, 32)
        key = jax.random.key(seed)
        kx, ku = jax.random.split(key)
        x = jax.random.normal(kx, (B, T, D), dtype=jnp.float32)
        U = jax.random.normal(ku, (D, R), dtype=jnp.float32) * 0.05
        return {'x': x, 'U': U}
    _L1_attn_all = _L1_attn_setup()
    _L1_attn_in = {k: v for k, v in _L1_attn_all.items() if k in ('U',)}
    del _L1_attn_all

    def _L1_ffn_setup():
        import math
        import jax, jax.numpy as jnp
        import numpy as np
        B, T, D, H, E, K, S = (4, 1024, 256, 512, 16, 2, 2)
        ROUTE_SCALE = 1.0

        def _swiglu(x, w1, w3, w2):
            return jax.nn.silu(x @ w1) * (x @ w3) @ w2
        key = jax.random.key(seed)
        ks = jax.random.split(key, 9)
        s = 0.02
        return {'x': jax.random.normal(ks[0], (B, T, D), jnp.float32), 'gate_w': jax.random.normal(ks[1], (D, E), jnp.float32) * s, 'gate_b': jnp.zeros((E,), jnp.float32), 'ew1': jax.random.normal(ks[2], (E, D, H), jnp.float32) * s, 'ew3': jax.random.normal(ks[3], (E, D, H), jnp.float32) * s, 'ew2': jax.random.normal(ks[4], (E, H, D), jnp.float32) * s, 'sw1': jax.random.normal(ks[5], (S, D, H), jnp.float32) * s, 'sw3': jax.random.normal(ks[6], (S, D, H), jnp.float32) * s, 'sw2': jax.random.normal(ks[7], (S, H, D), jnp.float32) * s}
    _L1_ffn_all = _L1_ffn_setup()
    _L1_ffn_in = {k: v for k, v in _L1_ffn_all.items() if k in ('gate_w', 'gate_b', 'ew1', 'ew3', 'ew2', 'sw1', 'sw3', 'sw2')}
    del _L1_ffn_all
    return {'x': x, 'x_txt': x_txt, 'L0_tok_Wa': _L0_tok_in['Wa'], 'L0_tok_ba': _L0_tok_in['ba'], 'L0_tok_Wd1': _L0_tok_in['Wd1'], 'L0_tok_bd1': _L0_tok_in['bd1'], 'L0_tok_Wd2': _L0_tok_in['Wd2'], 'L0_tok_bd2': _L0_tok_in['bd2'], 'L0_tok_Wd3': _L0_tok_in['Wd3'], 'L0_tok_bd3': _L0_tok_in['bd3'], 'L0_txt_weight': _L0_txt_in['weight'], 'L0_txt_lora_A': _L0_txt_in['lora_A'], 'L0_txt_lora_B': _L0_txt_in['lora_B'], 'L0_attn_Wq': _L0_attn_in['Wq'], 'L0_attn_bq': _L0_attn_in['bq'], 'L0_attn_Wk': _L0_attn_in['Wk'], 'L0_attn_bk': _L0_attn_in['bk'], 'L0_attn_Wv': _L0_attn_in['Wv'], 'L0_attn_bv': _L0_attn_in['bv'], 'L0_attn_Wo': _L0_attn_in['Wo'], 'L0_attn_bo': _L0_attn_in['bo'], 'L0_ffn_g1': _L0_ffn_in['g1'], 'L0_ffn_Wq': _L0_ffn_in['Wq'], 'L0_ffn_Wdkv': _L0_ffn_in['Wdkv'], 'L0_ffn_Wuk': _L0_ffn_in['Wuk'], 'L0_ffn_Wuv': _L0_ffn_in['Wuv'], 'L0_ffn_Wo': _L0_ffn_in['Wo'], 'L0_ffn_g2': _L0_ffn_in['g2'], 'L0_ffn_gate_w': _L0_ffn_in['gate_w'], 'L0_ffn_w1': _L0_ffn_in['w1'], 'L0_ffn_w2': _L0_ffn_in['w2'], 'L1_attn_U': _L1_attn_in['U'], 'L1_ffn_gate_w': _L1_ffn_in['gate_w'], 'L1_ffn_gate_b': _L1_ffn_in['gate_b'], 'L1_ffn_ew1': _L1_ffn_in['ew1'], 'L1_ffn_ew3': _L1_ffn_in['ew3'], 'L1_ffn_ew2': _L1_ffn_in['ew2'], 'L1_ffn_sw1': _L1_ffn_in['sw1'], 'L1_ffn_sw3': _L1_ffn_in['sw3'], 'L1_ffn_sw2': _L1_ffn_in['sw2']}

def reference(x, x_txt, L0_tok_Wa, L0_tok_ba, L0_tok_Wd1, L0_tok_bd1, L0_tok_Wd2, L0_tok_bd2, L0_tok_Wd3, L0_tok_bd3, L0_txt_weight, L0_txt_lora_A, L0_txt_lora_B, L0_attn_Wq, L0_attn_bq, L0_attn_Wk, L0_attn_bk, L0_attn_Wv, L0_attn_bv, L0_attn_Wo, L0_attn_bo, L0_ffn_g1, L0_ffn_Wq, L0_ffn_Wdkv, L0_ffn_Wuk, L0_ffn_Wuv, L0_ffn_Wo, L0_ffn_g2, L0_ffn_gate_w, L0_ffn_w1, L0_ffn_w2, L1_attn_U, L1_ffn_gate_w, L1_ffn_gate_b, L1_ffn_ew1, L1_ffn_ew3, L1_ffn_ew2, L1_ffn_sw1, L1_ffn_sw3, L1_ffn_sw2):
    import jax
    import jax.numpy as jnp

    def _L0_tok_ref(x, Wa, ba, Wd1, bd1, Wd2, bd2, Wd3, bd3):
        import jax, jax.numpy as jnp
        import numpy as np
        INV_SQRT2 = 0.7071067811865476
        LEVEL = 3

        def _split(x, axis):
            ax = axis % x.ndim
            sl0 = [slice(None)] * x.ndim
            sl0[ax] = slice(0, None, 2)
            sl1 = [slice(None)] * x.ndim
            sl1[ax] = slice(1, None, 2)
            x0, x1 = (x[tuple(sl0)], x[tuple(sl1)])
            return ((x0 + x1) * INV_SQRT2, (x0 - x1) * INV_SQRT2)

        def _merge(lo, hi, axis):
            ax = axis % lo.ndim
            e = (lo + hi) * INV_SQRT2
            o = (lo - hi) * INV_SQRT2
            s = jnp.stack([e, o], axis=ax + 1)
            shape = list(lo.shape)
            shape[ax] *= 2
            return s.reshape(shape)

        def _dwt2(x):
            lo, hi = _split(x, -1)
            a, h = _split(lo, -2)
            v, d = _split(hi, -2)
            return (a, h, v, d)

        def _idwt2(a, h, v, d):
            lo = _merge(a, h, -2)
            hi = _merge(v, d, -2)
            return _merge(lo, hi, -1)
        img = x[..., 0]
        B = img.shape[0]
        details = []
        cur = img
        for _ in range(LEVEL):
            cur, h, v, d = _dwt2(cur)
            details.append((h, v, d))
        aw = jax.nn.sigmoid(cur.reshape(B, -1) @ Wa + ba)
        rec = cur * aw[:, :, None]
        det_params = [(Wd1, bd1), (Wd2, bd2), (Wd3, bd3)]
        for (h, v, d), (Wd, bd) in zip(reversed(details), det_params):
            flat = jnp.stack([h, v, d], axis=1).reshape(B, -1)
            w = jax.nn.softmax(flat @ Wd + bd, axis=-1)
            rec = _idwt2(rec, h * w[:, 0, None, None], v * w[:, 1, None, None], d * w[:, 2, None, None])
        return rec

    def _L0_txt_ref(x, weight, lora_A, lora_B):
        import jax, jax.numpy as jnp
        import numpy as np
        NUM_EMB = 50257
        EMB_DIM = 256
        RANK = 8
        ALPHA = 16.0
        SCALING = ALPHA / RANK
        base = weight[x]
        lora_out = jnp.einsum('bsr,rd->bsd', lora_A[x], lora_B) * SCALING
        return base + lora_out

    def _L0_attn_ref(x, Wq, bq, Wk, bk, Wv, bv, Wo, bo):
        import jax, jax.numpy as jnp
        import numpy as np
        NUM_HEADS = 16
        HIDDEN = 256
        ATTN_DIM = 64
        HEAD_OUT = 64
        OUT_DIM = 256
        BATCH, SEQ = (2, 512)

        def _split_heads(y, h):
            b, s, _ = y.shape
            return y.reshape(b, s, h, -1).transpose(0, 2, 1, 3)
        h = NUM_HEADS
        q = _split_heads(x @ Wq + bq, h)
        k = _split_heads(x @ Wk + bk, h)
        v = _split_heads(x @ Wv + bv, h)
        scale = 1.0 / jnp.sqrt(jnp.float32(ATTN_DIM))
        pattern = jnp.einsum('bhid,bhjd->bhij', k, q) * scale
        prob = jax.nn.softmax(pattern, axis=-2)
        out = jnp.einsum('bhis,bhid->bhsd', prob, v)
        b, _, s, dv = out.shape
        concat = out.transpose(0, 2, 1, 3).reshape(b, s, h * dv)
        return concat @ Wo + bo

    def _L0_ffn_ref(x, g1, Wq, Wdkv, Wuk, Wuv, Wo, g2, gate_w, w1, w2):
        import jax, jax.numpy as jnp
        import numpy as np
        EMB = 256
        HEADS = 16
        SEQ = 512
        LATENT = 128
        N_EXP = 8
        TOP_K = 2
        EXP_DIM = 512
        BATCH = 2
        EPS = 1e-06

        def _rmsnorm(x, g):
            return x * jax.lax.rsqrt(jnp.mean(x * x, axis=-1, keepdims=True) + EPS) * g

        def _mla(h, Wq, Wdkv, Wuk, Wuv, Wo):
            B, S, D = h.shape
            hd = D // HEADS
            q = (h @ Wq).reshape(B, S, HEADS, hd)
            c = h @ Wdkv
            k = (c @ Wuk).reshape(B, S, HEADS, hd)
            v = (c @ Wuv).reshape(B, S, HEADS, hd)
            scores = jnp.einsum('bqhd,bkhd->bhqk', q, k) / jnp.sqrt(jnp.asarray(hd, h.dtype))
            causal = jnp.tril(jnp.ones((S, S), bool))
            scores = jnp.where(causal, scores, jnp.asarray(-1000000000.0, h.dtype))
            a = jax.nn.softmax(scores, axis=-1)
            out = jnp.einsum('bhqk,bkhd->bqhd', a, v).reshape(B, S, D)
            return out @ Wo

        def _moe(h, gate_w, w1, w2):
            B, S, D = h.shape
            t = h.reshape(B * S, D)
            logits = t @ gate_w
            top_v, top_i = jax.lax.top_k(logits, TOP_K)
            gates = jax.nn.softmax(top_v, axis=-1)
            T = t.shape[0]
            combine = jnp.zeros((T, N_EXP), t.dtype).at[jnp.arange(T)[:, None], top_i].add(gates)
            hid = jax.nn.silu(jnp.einsum('td,edh->teh', t, w1))
            ye = jnp.einsum('teh,ehd->ted', hid, w2)
            out = jnp.einsum('te,ted->td', combine, ye)
            return out.reshape(B, S, D)
        x = x + _mla(_rmsnorm(x, g1), Wq, Wdkv, Wuk, Wuv, Wo)
        x = x + _moe(_rmsnorm(x, g2), gate_w, w1, w2)
        return x

    def _L1_attn_ref(x, U):
        import jax, jax.numpy as jnp
        import numpy as np
        B, T, D, R = (4, 512, 256, 32)
        y = jnp.einsum('btd,dr->btr', x, U)
        n = jnp.sum(y * y, axis=-1)
        cross = jnp.einsum('btr,bjr->btj', y, y)
        dist_sq = n[:, :, None] + n[:, None, :] - 2.0 * cross
        attn = jax.nn.softmax(-dist_sq, axis=-1)
        return jnp.einsum('btj,bjd->btd', attn, x)

    def _L1_ffn_ref(x, gate_w, gate_b, ew1, ew3, ew2, sw1, sw3, sw2):
        import math
        import jax, jax.numpy as jnp
        import numpy as np
        B, T, D, H, E, K, S = (4, 1024, 256, 512, 16, 2, 2)
        ROUTE_SCALE = 1.0

        def _swiglu(x, w1, w3, w2):
            return jax.nn.silu(x @ w1) * (x @ w3) @ w2
        Bx, Tx, Dx = x.shape
        flat = x.reshape(-1, Dx)
        N = flat.shape[0]
        n_experts = gate_w.shape[1]
        logits = flat @ gate_w
        scores = jax.nn.softmax(logits.astype(jnp.float32), -1) + gate_b
        _, topi = jax.lax.top_k(scores, K)
        weights = jnp.take_along_axis(logits, topi, axis=-1) * ROUTE_SCALE
        weights = weights.astype(flat.dtype)
        capacity = math.ceil(N * K / n_experts * 1.25)

        def per_expert(gid, w1, w3, w2):
            match = topi == gid
            assigned = match.any(-1)
            w_tok = jnp.sum(jnp.where(match, weights, 0.0), -1)
            wm = jnp.where(assigned, w_tok, -jnp.inf)
            vals, idx = jax.lax.top_k(wm, capacity)
            valid = assigned[idx]
            xs = flat[idx]
            y = _swiglu(xs, w1, w3, w2) * jnp.where(valid, vals, 0.0)[:, None]
            return (idx, y)
        idxs, ys = jax.vmap(per_expert)(jnp.arange(n_experts), ew1, ew3, ew2)
        out = jnp.zeros_like(flat).at[idxs.reshape(-1)].add(ys.reshape(-1, Dx))
        shared = jax.vmap(lambda w1, w3, w2: _swiglu(flat, w1, w3, w2))(sw1, sw3, sw2)
        out = out + shared.mean(0)
        return out.reshape(Bx, Tx, Dx)
    h = _L0_tok_ref(x, L0_tok_Wa, L0_tok_ba, L0_tok_Wd1, L0_tok_bd1, L0_tok_Wd2, L0_tok_bd2, L0_tok_Wd3, L0_tok_bd3)
    h = jnp.concatenate([h, _L0_txt_ref(x_txt, L0_txt_weight, L0_txt_lora_A, L0_txt_lora_B)], axis=1)
    h = h + _L0_attn_ref(_layernorm(h, axis=-1), L0_attn_Wq, L0_attn_bq, L0_attn_Wk, L0_attn_bk, L0_attn_Wv, L0_attn_bv, L0_attn_Wo, L0_attn_bo)
    h = h + _L0_ffn_ref(_layernorm(h, axis=-1), L0_ffn_g1, L0_ffn_Wq, L0_ffn_Wdkv, L0_ffn_Wuk, L0_ffn_Wuv, L0_ffn_Wo, L0_ffn_g2, L0_ffn_gate_w, L0_ffn_w1, L0_ffn_w2)
    h = h + _L1_attn_ref(_layernorm(h, axis=-1), L1_attn_U)
    h = h + _L1_ffn_ref(_layernorm(h, axis=-1), L1_ffn_gate_w, L1_ffn_gate_b, L1_ffn_ew1, L1_ffn_ew3, L1_ffn_ew2, L1_ffn_sw1, L1_ffn_sw3, L1_ffn_sw2)
    return h

_drawn_inputs = setup_inputs


def setup_inputs(seed=0):
    import zlib

    import numpy as np

    out = dict(_drawn_inputs(seed))
    spreads = {'L0_tok_bd1': (0.0, 0.784),
     'L0_tok_bd2': (0.0, 0.8),
     'L0_tok_bd3': (0.0, 0.8),
     'L0_ffn_g1': (1.0, 0.6),
     'L0_ffn_g2': (1.0, 0.6),
     'L1_ffn_gate_b': (0.0, 0.8)}
    factors = {'L0_attn_Wq': 3.364,
     'L0_attn_bq': 8.0,
     'L0_attn_Wk': 3.376,
     'L0_attn_bk': 8.0,
     'L0_ffn_Wq': 8.0,
     'L0_ffn_Wdkv': 8.0,
     'L0_ffn_Wuk': 8.0,
     'L0_ffn_Wuv': 8.0,
     'L0_ffn_Wo': 8.0,
     'L1_attn_U': 8.0,
     'L1_ffn_gate_w': 8.0,
     'L1_ffn_ew1': 8.0,
     'L1_ffn_ew3': 8.0,
     'L1_ffn_ew2': 8.0,
     'L1_ffn_sw1': 8.0,
     'L1_ffn_sw3': 8.0,
     'L1_ffn_sw2': 8.0}
    for name, (base, spread) in spreads.items():
        noise = np.random.default_rng([zlib.crc32(name.encode()), seed]).standard_normal(out[name].shape)
        drawn = base * np.exp(spread * noise) if base else spread * noise
        out[name] = jnp.asarray(drawn.astype(out[name].dtype))
    for name, factor in factors.items():
        out[name] = (out[name] * factor).astype(out[name].dtype)
    return out
```

```python
from contextlib import ExitStack

import concourse.bass as bass
import numpy as np
from concourse import mybir

ALU = mybir.AluOpType
ACT = mybir.ActivationFunctionType
AX = mybir.AxisListType
F32 = mybir.dt.float32
BF16 = mybir.dt.bfloat16
I32 = mybir.dt.int32

B, IMG, TXT, D = 16, 256, 32, 256
S = IMG + TXT
TR = 96
NJ = S // TR
NT = B * NJ
NTOK = B * S
KD = D // 128
LN_EPS, RMS_EPS = 1e-5, 1e-6
BANK = 512
NEG = -1e30


class Tally:

    def __init__(self, sem, per, ahead=0):
        self.sem, self.per, self.ahead = sem, per, ahead

    def now(self, b, n):
        assert self.ahead + n > 0
        return b * self.per + (self.ahead + n)

    def before(self, b, n):
        assert self.ahead + n > self.per
        return b * self.per + (self.ahead + n - self.per)


class Chain:

    def __init__(self, eng, sem):
        self.eng, self.sem, self.n = eng, sem, 0

    def link(self, ins):
        ins.then_inc(self.sem, 1)
        self.n += 1
        self.eng.wait_ge(self.sem, self.n)


class LoopChain:

    def __init__(self, eng, sem, per, ahead=0):
        self.eng, self.tally, self.n = eng, Tally(sem, per, ahead), 0

    def start(self, b):
        self.b, self.n = b, 0

    def link(self, ins):
        ins.then_inc(self.tally.sem, 1)
        self.n += 1
        assert self.n <= self.tally.per
        self.eng.wait_ge(self.tally.sem, self.tally.now(self.b, self.n))

    def end(self):
        assert self.n == self.tally.per, self.n


def slot(b, j=None):
    return bass.ds(b * NJ, NJ) if j is None else bass.ds(b * NJ + j, 1)


def column(a, n):
    return a.rearrange("(c p) -> p c", p=n)


def rows_of(a, n=128):
    return a.rearrange("(k p) n -> p k n", p=n)


def stage_front(nc, A, keep, sem, sb, pb):
    ident = keep["ident"]
    h0 = keep["h0"]
    NI = B // 4
    xt = sb("xt", [128, NI, 8, IMG], F32)
    out_rows = sb("out_rows", [128, 2, 8, IMG], F32)
    low = sb("low", [128, 1024], F32)
    high = sb("high", [128, 1024], F32)
    approx = [sb(f"approx{lv}", [128, 512 >> 2 * lv], F32) for lv in range(2)]
    detail = [sb(f"detail{lv}", [128, NI, 3, 512 >> 2 * lv], F32) for lv in range(3)]
    coarse = sb("coarse", [128, NI, 32], F32)
    back = [sb(f"back{lv}", [128, 512 >> 2 * lv], F32) for lv in range(2)]
    vv = sb("vv", [128, 512], F32)
    scratch = sb("scratch", [128, 3 * 512], F32)
    w_band = [sb(f"w_band{lv}", [128, 3, (512 >> 2 * lv) * 3], F32) for lv in range(3)]
    w_app = sb("w_app", [128, 32], F32)
    dots = sb("dots", [128, NI, 10], F32)
    bias = sb("bias", [128, 10], F32)
    z = sb("z", [128, NI, 10], F32)
    zm = sb("zm", [128, NI, 3], F32)
    zs = sb("zs", [128, NI, 4], F32)
    wt = sb("wt", [128, NI, 10], F32)
    nwt = sb("nwt", [128, NI, 10], F32)
    same_image = sb("same_image", [128, 4, 32], F32)
    tok_id = sb("tok_id", [128, 4], I32)
    text = sb("text", [128, 4, D], F32)
    lora = sb("lora", [128, 4, 8], F32)
    lora_t = sb("lora_t", [8, 4, 128], F32)
    lora_b = sb("lora_b", [8, D], F32)
    text_out = sb("text_out", [128, 4, D], F32)
    p_sum = pb("p_sum", [128, BANK], F32)
    p_lora_t = pb("p_lora_t", [128, BANK], F32)
    p_lora = pb("p_lora", [128, 4, BANK], F32)

    img_in = [sem(f"img_in{t}") for t in range(NI)]
    weights_in, small_in, ids_in = sem("weights_in"), sem("small_in"), sem("ids_in")
    text_in, lora_in = sem("text_in"), sem("lora_in")
    ident_done, same_done = keep["ident_done"], sem("same_done")
    fdve, dots_done, sums_done = sem("front_dve"), sem("dots_done"), sem("sums_done")
    z_ready, exp_z = sem("z_ready"), sem("exp_z")
    lora_t_full, lora_t_done, lora_full = sem("lora_t_full"), sem("lora_t_done"), sem("lora_full")
    text_done, rows_done, text_stored = sem("text_done"), sem("rows_done"), sem("text_stored")
    rows_out = [sem(f"rows_out{u}") for u in range(2)]

    x_rows = A["x"].rearrange("b (i r) w o -> (b i) r (w o)", r=8)
    h0_img = h0.rearrange("(b s) d -> b s d", b=B)

    with nc.Block() as block:

        @block.sync
        def _(sp):
            for t in range(NI):
                sp.dma_start(xt[:, t], x_rows[t * 128:(t + 1) * 128]).then_inc(img_in[t], 16)
            for lv, name in enumerate(("L0_tok_Wd3", "L0_tok_Wd2", "L0_tok_Wd1")):
                src = A[name].rearrange("(c p q) k -> p c (q k)", c=3, p=32)
                for m in range(4):
                    sp.dma_start(w_band[lv][32 * m:32 * m + 32], src).then_inc(weights_in, 16)
            for m in range(4):
                sp.dma_start(w_app[32 * m:32 * m + 32], A["L0_tok_Wa"].rearrange("(p q) k -> p (q k)", p=32)).then_inc(weights_in, 16)
            for t in range(NI):
                sp.wait_ge(rows_done, t + 1)
                for m in range(4):
                    sp.dma_start(h0_img[4 * t + m, 0:IMG].rearrange("(p r) d -> p r d", r=8),
                                 out_rows[32 * m:32 * m + 32, t % 2]).then_inc(rows_out[t % 2], 16)
            for u in range(2):
                sp.wait_ge(rows_out[u], 16 * 4 * (NI // 2))

        @block.scalar
        def _(act):
            act.dma_start(tok_id[:, :], A["x_txt"].rearrange("b s -> (b s)").rearrange("(q p) -> p q", p=128),
                          allow_slow_non_contiguous=True).then_inc(ids_in, 16)
            act.dma_start(lora_b[:, :], A["L0_txt_lora_B"]).then_inc(small_in, 16)
            for name, a, n in (("L0_tok_bd3", 0, 3), ("L0_tok_bd2", 3, 3), ("L0_tok_bd1", 6, 3), ("L0_tok_ba", 9, 1)):
                act.dma_start(bias[:, a:a + n], A[name].partition_broadcast(128)).then_inc(small_in, 16)
            act.wait_ge(z_ready, 1)
            act.activation(z[:, :, :], z[:, :, :], ACT.Exp).then_inc(exp_z, 1)
            act.wait_ge(text_done, 4)
            for q in range(4):
                for m in range(4):
                    act.dma_start(h0_img[4 * q + m, IMG:S], text_out[32 * m:32 * m + 32, q]).then_inc(text_stored, 16)
            act.wait_ge(text_stored, 16 * 16)

        @block.gpsimd
        def _(pool):
            pool.memset(ident[:, :], 0.0).then_inc(ident_done, 1)
            pool.memset(same_image[:, :, :], 1.0).then_inc(same_done, 1)
            pool.wait_ge(ident_done, 1)
            pool.affine_select(out=ident[:, :], in_=ident[:, :], compare_op=ALU.not_equal, fill=1.0, base=0,
                               pattern=[[-1, 128]], channel_multiplier=1).then_inc(ident_done, 1)
            pool.wait_ge(same_done, 1)
            pool.affine_select(out=same_image[:, :, :], in_=same_image[:, :, :], compare_op=ALU.is_ge, fill=0.0, base=0,
                               pattern=[[-32, 4], [0, 32]], channel_multiplier=1).then_inc(same_done, 1)
            pool.wait_ge(same_done, 2)
            pool.affine_select(out=same_image[:, :, :], in_=same_image[:, :, :], compare_op=ALU.is_ge, fill=0.0, base=31,
                               pattern=[[32, 4], [0, 32]], channel_multiplier=-1).then_inc(same_done, 1)
            pool.wait_ge(ids_in, 16)
            for q in range(4):
                rows = bass.IndirectOffsetOnAxis(ap=tok_id[:, q:q + 1], axis=0)
                pool.indirect_dma_start(lora[:, q], None, A["L0_txt_lora_A"], rows).then_inc(lora_in, 16)
                pool.indirect_dma_start(text[:, q], None, A["L0_txt_weight"], rows).then_inc(text_in, 16)
            pool.wait_ge(lora_in, 64)
            pool.wait_ge(text_in, 64)

        @block.tensor
        def _(pe):
            pe.wait_ge(ident_done, 2)
            pe.wait_ge(lora_in, 64)
            for q in range(4):
                mm = pe.transpose(p_lora_t[0:8, q * 128:(q + 1) * 128], lora[:, q], ident[:, :])
            mm.then_inc(lora_t_full, 1)
            pe.wait_ge(lora_t_done, 1)
            pe.wait_ge(small_in, 16 * 5)
            for q in range(4):
                mm = pe.matmul(p_lora[:, q, 0:D], lora_t[:, q], lora_b[:, :], start=True, stop=True)
            mm.then_inc(lora_full, 1)
            pe.wait_ge(same_done, 3)
            pe.wait_ge(dots_done, NI * 10)
            pe.matmul(p_sum[:, 0:NI * 10], same_image[:, :, :], dots[:, :, :], start=True, stop=True).then_inc(sums_done, 1)

        @block.vector
        def _(dve):
            ch = Chain(dve, fdve)

            def analyse(src, rows, cols, lv, t):
                n = rows * cols // 2
                lo = low[:, 0:n].rearrange("p (r c) -> p r c", r=rows)
                hi = high[:, 0:n].rearrange("p (r c) -> p r c", r=rows)
                dve.tensor_tensor(lo, src[:, :, 0::2], src[:, :, 1::2], ALU.add)
                ch.link(dve.tensor_tensor(hi, src[:, :, 0::2], src[:, :, 1::2], ALU.subtract))
                to = [a.rearrange("p (r c) -> p r c", r=rows // 2)
                      for a in (approx[lv][:, :] if lv < 2 else coarse[:, t], detail[lv][:, t, 0], detail[lv][:, t, 1], detail[lv][:, t, 2])]
                dve.tensor_tensor(to[0], lo[:, 0::2], lo[:, 1::2], ALU.add)
                dve.tensor_tensor(to[1], lo[:, 0::2], lo[:, 1::2], ALU.subtract)
                dve.tensor_tensor(to[2], hi[:, 0::2], hi[:, 1::2], ALU.add)
                ch.link(dve.tensor_tensor(to[3], hi[:, 0::2], hi[:, 1::2], ALU.subtract))

            def analysis(t):
                analyse(xt[:, t], 8, IMG, 0, t)
                analyse(approx[0][:, :].rearrange("p (r c) -> p r c", r=4), 4, IMG // 2, 1, t)
                analyse(approx[1][:, :].rearrange("p (r c) -> p r c", r=2), 2, IMG // 4, 2, t)

            dve.wait_ge(weights_in, 16 * 16)
            for t in range(NI):
                dve.wait_ge(img_in[t], 16)
                analysis(t)
                for lv in range(3):
                    for k in range(3):
                        w = w_band[lv][:, :, :].rearrange("p c (q k) -> p (c q) k", k=3)[:, :, k]
                        n = 3 * (512 >> 2 * lv)
                        ch.link(dve.tensor_tensor_reduce(
                            scratch[:, 0:n], detail[lv][:, t].rearrange("p c q -> p (c q)"), w,
                            0.5 ** (lv + 1), 0.0, ALU.mult, ALU.add, dots[:, t, 3 * lv + k:3 * lv + k + 1]))
                        dve.sem_inc(dots_done, 1)
                ch.link(dve.tensor_tensor_reduce(scratch[:, 0:32], coarse[:, t], w_app[:, :], 0.125, 0.0,
                                                 ALU.mult, ALU.add, dots[:, t, 9:10]))
                dve.sem_inc(dots_done, 1)
            dve.wait_ge(lora_t_full, 1)
            dve.tensor_copy(lora_t[:, :, :], p_lora_t[0:8, :].rearrange("p (q n) -> p q n", q=4)).then_inc(lora_t_done, 1)
            dve.wait_ge(small_in, 16 * 5)
            dve.wait_ge(sums_done, 1)
            ch.link(dve.tensor_tensor(z[:, :, :], p_sum[:, 0:NI * 10].rearrange("p (t n) -> p t n", n=10),
                                      bias[:, :].unsqueeze(1).to_broadcast([128, NI, 10]), ALU.add))
            bands = z[:, :, 0:9].rearrange("p t (l k) -> p t l k", k=3)
            ch.link(dve.tensor_reduce(zm[:, :, :], bands, AX.X, ALU.max))
            for t in range(NI):
                last = dve.tensor_tensor(z[:, t, 0:9].rearrange("p (l k) -> p l k", k=3),
                                         z[:, t, 0:9].rearrange("p (l k) -> p l k", k=3),
                                         zm[:, t].unsqueeze(2).to_broadcast([128, 3, 3]), ALU.subtract)
            ch.link(last)
            ch.link(dve.tensor_scalar(z[:, :, 9], z[:, :, 9], -1.0, None, ALU.mult))
            dve.sem_inc(z_ready, 1)
            dve.wait_ge(exp_z, 1)
            dve.tensor_reduce(zs[:, :, 0:3], bands, AX.X, ALU.add)
            ch.link(dve.tensor_scalar(zs[:, :, 3], z[:, :, 9], 1.0, None, ALU.add))
            ch.link(dve.reciprocal(zs[:, :, :], zs[:, :, :]))
            for t in range(NI):
                for lv in range(3):
                    last = dve.tensor_scalar(wt[:, t, 3 * lv:3 * lv + 3], z[:, t, 3 * lv:3 * lv + 3],
                                             zs[:, t, lv:lv + 1], 0.25 ** (lv + 1), ALU.mult, ALU.mult)
            ch.link(last)
            ch.link(dve.tensor_scalar(wt[:, :, 9], zs[:, :, 3], 1 / 64, None, ALU.mult))
            ch.link(dve.tensor_scalar(nwt[:, :, :], wt[:, :, :], -1.0, None, ALU.mult))

            def synthesise(src, lv, t, dst, cols):
                n = 512 >> 2 * lv
                rows = n // cols
                v3 = lambda a: a.rearrange("p (r c) -> p r c", r=rows)
                lo = low[:, 0:2 * n].rearrange("p (r u c) -> p r u c", u=2, c=cols)
                hi = high[:, 0:2 * n].rearrange("p (r u c) -> p r u c", u=2, c=cols)
                w = lambda a, k: a[:, t, 3 * lv + k:3 * lv + k + 1]
                h_, v_, d_ = (v3(detail[lv][:, t, c]) for c in range(3))
                ch.link(dve.tensor_scalar(vv[:, 0:n], detail[lv][:, t, 1], w(wt, 1), None, ALU.mult))
                for u, s in ((0, wt), (1, nwt)):
                    dve.scalar_tensor_tensor(out=lo[:, :, u], in0=h_, scalar=w(s, 0), in1=v3(src), op0=ALU.mult, op1=ALU.add)
                    last = dve.scalar_tensor_tensor(out=hi[:, :, u], in0=d_, scalar=w(s, 2), in1=v3(vv[:, 0:n]), op0=ALU.mult, op1=ALU.add)
                ch.link(last)
                lo2 = low[:, 0:2 * n].rearrange("p (r c) -> p r c", c=cols)
                hi2 = high[:, 0:2 * n].rearrange("p (r c) -> p r c", c=cols)
                dve.tensor_tensor(dst[:, :, 0::2], lo2, hi2, ALU.add)
                ch.link(dve.tensor_tensor(dst[:, :, 1::2], lo2, hi2, ALU.subtract))

            for t in range(NI):
                ch.link(dve.tensor_scalar(coarse[:, t], coarse[:, t], wt[:, t, 9:10], None, ALU.mult))
                synthesise(coarse[:, t], 2, t, back[1][:, :].rearrange("p (r c) -> p r c", r=2), 32)
                synthesise(back[1][:, :], 1, t, back[0][:, :].rearrange("p (r c) -> p r c", r=4), 64)
                if t >= 2:
                    dve.wait_ge(rows_out[t % 2], 16 * 4 * (t // 2))
                synthesise(back[0][:, :], 0, t, out_rows[:, t % 2], 128)
                dve.sem_inc(rows_done, 1)
                if t == 0:
                    dve.wait_ge(lora_full, 1)
                    dve.wait_ge(text_in, 64)
                    for q in range(4):
                        dve.scalar_tensor_tensor(out=text_out[:, q], in0=p_lora[:, q, 0:D], scalar=2.0, in1=text[:, q],
                                                 op0=ALU.mult, op1=ALU.add).then_inc(text_done, 1)


class Heads:

    def __init__(self, nc, sem, sb, pb, name, n_heads, pack, causal, first_use, ring, uses):
        self.nh, self.pack, self.causal, self.u0, self.ring, self.uses = n_heads, pack, causal, first_use, ring, uses
        self.gw = 128 // pack
        self.prob = sb(name + "_prob", [TR, 2, NJ, S], F32)
        self.prob_t = sb(name + "_prob_t", [TR, 2, NJ, S], F32)
        self.neg_max = sb(name + "_neg_max", [TR, 2, NJ], F32)
        self.row_sum = sb(name + "_row_sum", [TR, 2, NJ], F32)
        self.inv_sum = sb(name + "_inv_sum", [TR, 2, NJ], F32)
        self.p_t = [pb(f"{name}_p_t{kt}", [TR, BANK], F32) for kt in range(NJ)]
        self.p_o = pb(name + "_p_o", [128, BANK], F32)
        n, g = n_heads, n_heads // pack
        self.scored = Tally(sem(name + "_scored"), NJ * n)
        self.max_done = Tally(sem(name + "_max_done"), NJ * n)
        self.exp_done = Tally(sem(name + "_exp_done"), NJ * n)
        self.inv_done = Tally(sem(name + "_inv_done"), n)
        self.scaled = Tally(sem(name + "_scaled"), NJ * n)
        self.turned = Tally(sem(name + "_turned"), n, ahead=n)
        self.copied = Tally(sem(name + "_copied"), 2 * n, ahead=2 * n)
        self.copied2 = Tally(sem(name + "_copied2"), n, ahead=n)
        self.weighted = Tally(sem(name + "_weighted"), n, ahead=n)
        self.heads_out = Tally(sem(name + "_heads_out"), g, ahead=g)

    def keys(self, j):
        return TR * (j + 1) if self.causal else S

    def pe_ahead(self, pe):
        pe.sem_inc(self.turned.sem, self.turned.ahead)
        pe.sem_inc(self.weighted.sem, self.weighted.ahead)

    def act_ahead(self, act):
        act.sem_inc(self.copied.sem, self.copied.ahead)

    def dve_ahead(self, dve):
        dve.sem_inc(self.copied2.sem, self.copied2.ahead)
        dve.sem_inc(self.heads_out.sem, self.heads_out.ahead)

    def pe_scores(self, pe, b, hd, claim, q, k, mask=None):
        for j in range(NJ):
            u = self.u0 + NJ * hd + j
            claim(pe, b, u)
            n = self.keys(j)
            bank = self.ring[u % len(self.ring)]
            mm = pe.matmul(bank[0:TR, 0:n], q(hd, j), k(hd, n), start=True, stop=mask is None)
            if mask is not None:
                mm = pe.matmul(bank[0:TR, TR * j:n], mask[0], mask[1], start=False, stop=True)
            mm.then_inc(self.scored.sem, 1)

    def pe_turn(self, pe, b, hd, ident):
        for t, last in ((self.copied, 2), (self.copied2, 1)):
            pe.wait_ge(t.sem, t.now(b, last * hd) if hd else t.before(b, last * self.nh))
        for j in range(NJ):
            pe.wait_ge(self.scaled.sem, self.scaled.now(b, NJ * hd + j + 1))
            for kt in range(j + 1 if self.causal else NJ):
                mm = pe.transpose(self.p_t[kt][:, TR * j:TR * j + TR],
                                  self.prob[:, hd % 2, j, TR * kt:TR * kt + TR], ident[0:TR, 0:TR])
        mm.then_inc(self.turned.sem, 1)

    def pe_values(self, pe, b, hd, v):
        g = hd // self.pack
        if hd % self.pack == 0:
            pe.wait_ge(self.heads_out.sem, self.heads_out.now(b, g) if g else self.heads_out.before(b, self.nh // self.pack))
        at = self.gw * (hd % self.pack)
        for kt in range(NJ):
            if kt == 0:
                pe.wait_ge(self.copied.sem, self.copied.now(b, 2 * hd + 2))
            if kt == 2:
                pe.wait_ge(self.copied2.sem, self.copied2.now(b, hd + 1))
            n0 = TR * kt if self.causal else 0
            mm = pe.matmul(self.p_o[at:at + self.gw, n0:S], v(hd, kt), self.prob_t[:, hd % 2, kt, n0:S],
                           start=kt == 0, stop=kt == NJ - 1)
        mm.then_inc(self.weighted.sem, 1)

    def pe_heads(self, pe, b, claim, q, k, v, ident, mask=None):
        self.pe_scores(pe, b, 0, claim, q, k, mask)
        for hd in range(self.nh):
            if hd + 1 < self.nh:
                self.pe_scores(pe, b, hd + 1, claim, q, k, mask)
            self.pe_turn(pe, b, hd, ident)
            if hd:
                self.pe_values(pe, b, hd - 1, v)
        self.pe_values(pe, b, self.nh - 1, v)

    def act_exps(self, act, b, hd):
        act.wait_ge(self.turned.sem, self.turned.now(b, hd - 1) if hd >= 2 else self.turned.before(b, self.nh - 1 + hd))
        for j in range(NJ):
            act.wait_ge(self.max_done.sem, self.max_done.now(b, NJ * hd + j + 1))
            n = self.keys(j)
            u = self.u0 + NJ * hd + j
            act.activation(self.prob[:, hd % 2, j, 0:n], self.ring[u % len(self.ring)][0:TR, 0:n], ACT.Exp,
                           bias=self.neg_max[:, hd % 2, j:j + 1], accum_out=self.row_sum[:, hd % 2, j:j + 1])\
               .then_inc(self.exp_done.sem, 1)

    def act_copies(self, act, b, hd):
        act.wait_ge(self.turned.sem, self.turned.now(b, hd + 1))
        act.wait_ge(self.weighted.sem, self.weighted.now(b, hd - 1) if hd >= 2 else self.weighted.before(b, self.nh - 1 + hd))
        for kt in range(2):
            n0 = TR * kt if self.causal else 0
            act.activation(self.prob_t[:, hd % 2, kt, n0:S], self.p_t[kt][:, n0:S], ACT.Copy).then_inc(self.copied.sem, 1)

    def act_heads(self, act, b, extra=None):
        self.act_exps(act, b, 0)
        for hd in range(self.nh):
            if hd + 1 < self.nh:
                self.act_exps(act, b, hd + 1)
            self.act_copies(act, b, hd)
            if extra and hd in extra:
                extra[hd](act, b)

    def dve_max(self, dve, b, hd):
        for j in range(NJ):
            dve.wait_ge(self.scored.sem, self.scored.now(b, NJ * hd + j + 1))
            u = self.u0 + NJ * hd + j
            dve.tensor_reduce(self.neg_max[:, hd % 2, j:j + 1], self.ring[u % len(self.ring)][0:TR, 0:self.keys(j)],
                              AX.X, ALU.max, negate=True).then_inc(self.max_done.sem, 1)

    def dve_scale(self, dve, b, hd):
        dve.wait_ge(self.exp_done.sem, self.exp_done.now(b, NJ * hd + NJ))
        dve.reciprocal(self.inv_sum[:, hd % 2], self.row_sum[:, hd % 2]).then_inc(self.inv_done.sem, 1)
        dve.wait_ge(self.inv_done.sem, self.inv_done.now(b, hd + 1))
        for j in range(NJ):
            p = self.prob[:, hd % 2, j, 0:self.keys(j)]
            dve.tensor_scalar(p, p, self.inv_sum[:, hd % 2, j:j + 1], None, ALU.mult).then_inc(self.scaled.sem, 1)

    def dve_copy(self, dve, b, hd):
        dve.wait_ge(self.turned.sem, self.turned.now(b, hd + 1))
        dve.wait_ge(self.weighted.sem, self.weighted.now(b, hd - 1) if hd >= 2 else self.weighted.before(b, self.nh - 1 + hd))
        n0 = 2 * TR if self.causal else 0
        dve.tensor_copy(self.prob_t[:, hd % 2, 2, n0:S], self.p_t[2][:, n0:S]).then_inc(self.copied2.sem, 1)

    def dve_out(self, dve, b, hd, out_t):
        if hd % self.pack == self.pack - 1:
            dve.wait_ge(self.weighted.sem, self.weighted.now(b, hd + 1))
            dve.tensor_copy(out_t[:, hd // self.pack], self.p_o[:, 0:S]).then_inc(self.heads_out.sem, 1)

    def dve_heads(self, dve, b, out_t, extra=None):
        self.dve_max(dve, b, 0)
        for hd in range(self.nh):
            self.dve_scale(dve, b, hd)
            if hd + 1 < self.nh:
                self.dve_max(dve, b, hd + 1)
            self.dve_copy(dve, b, hd)
            if hd:
                self.dve_out(dve, b, hd - 1, out_t)
            if extra and hd in extra:
                extra[hd](dve, b)
        self.dve_out(dve, b, self.nh - 1, out_t)


class Ring:

    def __init__(self, banks, freed):
        self.banks, self.freed = banks, freed
        assert len(freed) % len(banks) == 0

    def bank(self, u):
        return self.banks[u % len(self.banks)]

    def claim(self, pe, b, u):
        v = u - len(self.banks)
        if v >= 0:
            t, n = self.freed[v]
            pe.wait_ge(t.sem, t.now(b, n))
        else:
            t, n = self.freed[v + len(self.freed)]
            pe.wait_ge(t.sem, t.before(b, n))


class Norm:

    def __init__(self, sem, sb, name, ahead):
        self.stats = sb(name + "_stats", [TR, NJ, 6], F32)
        self.mv = sb(name + "_mv", [TR, NJ, 2], F32)
        self.stats_done = Tally(sem(name + "_stats_done"), NJ, ahead * NJ)
        self.stats_seen = sem(name + "_stats_seen")
        self.mv_done = Tally(sem(name + "_mv_done"), NJ, ahead * NJ)
        self.power = Power(sem, sb, name, ahead)

    def dve_stats(self, dve, src, at):
        for j in range(NJ):
            dve.bn_stats(self.stats[:, j], src(j)).then_inc(self.stats_done.sem, 1)
        dve.wait_ge(self.stats_done.sem, at(self.stats_done, NJ))
        dve.sem_inc(self.stats_seen, 1)
        for j in range(NJ):
            dve.bn_aggr(self.mv[:, j], self.stats[:, j]).then_inc(self.mv_done.sem, 1)

    def pool_inverse(self, pool, eps, minus_half, at):
        self.power.pool_inverse(pool, self.mv[:, :, 1], self.mv_done, eps, minus_half, at)

    def dve_apply(self, dve, src, dst, at, done):
        dve.wait_ge(self.power.done.sem, at(self.power.done, 1))
        for j in range(NJ):
            dve.tensor_scalar(dst(j), src(j), self.mv[:, j, 0:1], self.power.inv[:, j:j + 1], ALU.subtract, ALU.mult)\
               .then_inc(done.sem, 1)


class Power:

    def __init__(self, sem, sb, name, ahead):
        self.inv = sb(name + "_inv", [TR, NJ], F32)
        self.eps_done = Tally(sem(name + "_eps_done"), 1, ahead)
        self.done = Tally(sem(name + "_inv_done"), 1, ahead)

    def pool_inverse(self, pool, x, x_done, eps, minus_half, at):
        pool.wait_ge(x_done.sem, at(x_done, NJ))
        pool.tensor_tensor(self.inv[:, :], x, eps[:, :], ALU.add).then_inc(self.eps_done.sem, 1)
        pool.wait_ge(self.eps_done.sem, at(self.eps_done, 1))
        pool.tensor_tensor(self.inv[:, :], self.inv[:, :], minus_half[:, :], ALU.pow).then_inc(self.done.sem, 1)


def at_now(b):
    return lambda tally, n: tally.now(b, n)


def at_first(tally, n):
    return n


def at_turn(b):
    return lambda tally, n: tally.now(b, n)


def stage_attention(nc, A, keep, sem, sb, pb):
    h, ident = keep["h"], keep["ident"]
    NH, HD = 16, 64
    E = NH * HD
    KE = E // 128
    wq, wk, wv = (sb(n, [128, KD, E], F32) for n in ("wq", "wk", "wv"))
    wo = sb("wo", [128, KE, D], F32)
    bq = sb("bq", [128, KE], F32)
    bk = sb("bk", [128, KE], F32)
    bv = sb("bv", [TR, E], F32)
    bo = sb("bo", [1, D], F32)
    ones = sb("ones_row", [1, TR], F32)
    minus_half = sb("minus_half", [TR, NJ], F32)
    eps = sb("eps", [TR, NJ], F32)
    xn = sb("xn", [TR, NJ, D], F32)
    x_t = sb("x_t", [128, KD, S], F32)
    q_t = sb("q_t", [128, KE, S], F32)
    k_t = sb("k_t", [128, KE, S], F32)
    v = sb("v", [TR, NJ, E], F32)
    o_t = sb("o_t", [128, KE, S], F32)
    banks = [pb(f"ring{i}", [128, BANK], F32) for i in range(4)]

    N_QK, N_V = 2 * KE, NJ * E // BANK
    U_V, U_S = N_QK, N_QK + N_V
    U_O = U_S + NJ * NH
    U_X = U_O + NJ
    heads = Heads(nc, sem, sb, pb, "attn", NH, 2, False, U_S, banks, None)
    q_done, k_done, v_done = Tally(sem("q_done"), KE), Tally(sem("k_done"), KE), Tally(sem("v_done"), N_V)
    x_t_done = Tally(sem("x_t_done"), KD, KD)
    h_done = Tally(sem("h_done"), NJ, NJ)
    freed = [(q_done, u // 2 + 1) if u % 2 == 0 else (k_done, u // 2 + 1) for u in range(N_QK)]
    freed += [(v_done, i + 1) for i in range(N_V)]
    freed += [(heads.exp_done, i + 1) for i in range(NJ * NH)]
    freed += [(h_done, i + 1) for i in range(NJ)]
    freed += [(x_t_done, i + 1) for i in range(KD)]
    freed += [freed[-4]]
    ring = Ring(banks, freed)
    projected = Tally(sem("projected"), N_QK + N_V)
    out_done = Tally(sem("out_done"), NJ)
    turned_x = Tally(sem("turned_x"), KD, KD)
    xn_done = Tally(sem("xn_done"), NJ, NJ)
    norm = Norm(sem, sb, "ln1", ahead=1)
    h_in = [sem(f"h_in{i}") for i in range(4)]
    zero = sb("zero_rows", [128, 5, D], F32)
    zero_done, xs_zeroed = sem("zero_done"), sem("xs_zeroed")
    w_in, consts, bq_done = sem("attn_w_in"), sem("attn_consts"), sem("bq_done")

    with nc.Block() as block:

        @block.sync
        def _(sp):
            h0 = keep["h0"].rearrange("(n p) d -> p n d", p=TR)
            n = NT // 4
            sp.dma_start(h[:, 0:n], h0[:, 0:n]).then_inc(h_in[0], 16)
            for name, t in (("Wq", wq), ("Wk", wk), ("Wv", wv), ("Wo", wo)):
                sp.dma_start(t[:, :, :], rows_of(A["L0_attn_" + name])).then_inc(w_in, 16)
            sp.dma_start(bq[:, :], column(A["L0_attn_bq"], 128), allow_slow_non_contiguous=True).then_inc(w_in, 16)
            sp.dma_start(bk[:, :], column(A["L0_attn_bk"], 128), allow_slow_non_contiguous=True).then_inc(w_in, 16)
            sp.dma_start(bv[:, :], A["L0_attn_bv"].partition_broadcast(TR)).then_inc(w_in, 16)
            sp.dma_start(bo[:, :], A["L0_attn_bo"].partition_broadcast(1)).then_inc(w_in, 16)
            for i in range(1, 4):
                sp.dma_start(h[:, i * n:(i + 1) * n], h0[:, i * n:(i + 1) * n]).then_inc(h_in[i], 16)
            sp.wait_ge(zero_done, 1)
            step = zero.shape[1] * 128
            xs = keep["xs"].rearrange("(n j p) d -> n p j d", p=128, j=zero.shape[1])
            for i in range(keep["xs"].shape[0] // step):
                sp.dma_start(xs[i], zero[:, :, :]).then_inc(xs_zeroed, 16)
            sp.wait_ge(xs_zeroed, 16 * (keep["xs"].shape[0] // step))

        @block.gpsimd
        def _(pool):
            pool.memset(minus_half[:, :], -0.5).then_inc(consts, 1)
            pool.memset(zero[:, :, :], 0.0).then_inc(zero_done, 1)
            pool.memset(ones[:, :], 1.0).then_inc(consts, 1)
            pool.memset(h[:, NT:NT + NJ], 0.0).then_inc(consts, 1)
            pool.memset(eps[:, :], LN_EPS).then_inc(consts, 1)
            pool.wait_ge(consts, 4)
            norm.pool_inverse(pool, eps, minus_half, at_first)
            with pool.Fori(0, B) as b:
                norm.pool_inverse(pool, eps, minus_half, at_turn(b))

        @block.scalar
        def _(act):
            act.wait_ge(w_in, 16 * 8)
            act.activation(bq[:, :], bq[:, :], ACT.Copy, scale=HD ** -0.5).then_inc(bq_done, 1)
            act.wait_ge(bq_done, 1)
            heads.act_ahead(act)

            def x_copies(at):
                for k in range(KD):
                    act.wait_ge(turned_x.sem, at(turned_x, k + 1))
                    act.activation(x_t[:, k], ring.bank(U_X + k)[:, 0:S], ACT.Copy).then_inc(x_t_done.sem, 1)

            x_copies(at_first)
            with act.Fori(0, B) as b:
                for m in range(KE):
                    act.wait_ge(projected.sem, projected.now(b, 2 * m + 1))
                    act.activation(q_t[:, m], ring.bank(2 * m)[:, 0:S], ACT.Identity, bias=bq[:, m:m + 1],
                                   scale=HD ** -0.5).then_inc(q_done.sem, 1)
                heads.act_heads(act, b)
                x_copies(at_turn(b))

        @block.tensor
        def _(pe):
            heads.pe_ahead(pe)

            def turn_x(at, claim):
                pe.wait_ge(xn_done.sem, at(xn_done, NJ))
                for k in range(KD):
                    if claim:
                        claim(U_X + k)
                    for j in range(NJ):
                        mm = pe.transpose(ring.bank(U_X + k)[:, TR * j:TR * j + TR], xn[:, j, 128 * k:128 * k + 128],
                                          ident[0:TR, 0:TR])
                    mm.then_inc(turned_x.sem, 1)

            turn_x(at_first, None)
            pe.wait_ge(consts, 4)
            pe.wait_ge(w_in, 16 * 8)
            with pe.Fori(0, B) as b:
                pe.wait_ge(x_t_done.sem, x_t_done.before(b, KD))
                for m in range(KE):
                    for u, w in ((2 * m, wq), (2 * m + 1, wk)):
                        ring.claim(pe, b, u)
                        for k in range(KD):
                            mm = pe.matmul(ring.bank(u)[:, 0:S], w[:, k, 128 * m:128 * m + 128], x_t[:, k],
                                           start=k == 0, stop=k == KD - 1)
                        mm.then_inc(projected.sem, 1)
                for i in range(N_V):
                    j, half = divmod(i, E // BANK)
                    ring.claim(pe, b, U_V + i)
                    for k in range(KD):
                        mm = pe.matmul(ring.bank(U_V + i)[0:TR, :], x_t[:, k, TR * j:TR * j + TR],
                                       wv[:, k, BANK * half:BANK * half + BANK], start=k == 0, stop=k == KD - 1)
                    mm.then_inc(projected.sem, 1)
                pe.wait_ge(q_done.sem, q_done.now(b, KE))
                pe.wait_ge(k_done.sem, k_done.now(b, KE))
                pe.wait_ge(v_done.sem, v_done.now(b, N_V))
                part = lambda hd: slice(HD * (hd % 2), HD * (hd % 2) + HD)
                heads.pe_heads(pe, b, ring.claim,
                               lambda hd, j: q_t[part(hd), hd // 2, TR * j:TR * j + TR],
                               lambda hd, n: k_t[part(hd), hd // 2, 0:n],
                               lambda hd, kt: v[:, kt, HD * hd:HD * hd + HD], ident)
                pe.wait_ge(heads.heads_out.sem, heads.heads_out.now(b, KE))
                for j in range(NJ):
                    ring.claim(pe, b, U_O + j)
                    to = ring.bank(U_O + j)[0:TR, 0:D]
                    pe.matmul(to, ones[:, :], bo[:, :], start=True, stop=False)
                    for k in range(KE):
                        mm = pe.matmul(to, o_t[:, k, TR * j:TR * j + TR], wo[:, k], start=False, stop=k == KE - 1)
                    mm.then_inc(out_done.sem, 1)
                turn_x(at_turn(b), lambda u: ring.claim(pe, b, u))

        @block.vector
        def _(dve):
            dve.wait_ge(h_in[0], 16)
            heads.dve_ahead(dve)
            dve.sem_inc(h_done.sem, h_done.ahead)

            def prepare(tile, at):
                norm.dve_stats(dve, tile, at)
                norm.dve_apply(dve, tile, lambda j: xn[:, j:j + 1], at, xn_done)

            prepare(lambda j: h[:, j:j + 1], at_first)
            for i in range(1, 4):
                dve.wait_ge(h_in[i], 16)
            dve.wait_ge(consts, 4)
            dve.wait_ge(w_in, 16 * 8)
            with dve.Fori(0, B) as b:
                for m in range(KE):
                    dve.wait_ge(projected.sem, projected.now(b, 2 * m + 2))
                    dve.tensor_scalar(k_t[:, m], ring.bank(2 * m + 1)[:, 0:S], bk[:, m:m + 1], None, ALU.add)\
                       .then_inc(k_done.sem, 1)
                for i in range(N_V):
                    j, half = divmod(i, E // BANK)
                    dve.wait_ge(projected.sem, projected.now(b, N_QK + i + 1))
                    cols = slice(BANK * half, BANK * half + BANK)
                    dve.tensor_tensor(v[:, j, cols], ring.bank(U_V + i)[0:TR, :], bv[:, cols], ALU.add)\
                       .then_inc(v_done.sem, 1)
                heads.dve_heads(dve, b, o_t, extra={
                    8: lambda e, b: prepare(lambda j: h[:, slot(b + 1, j)], at_turn(b))})
                for j in range(NJ):
                    dve.wait_ge(out_done.sem, out_done.now(b, j + 1))
                    to = h[:, slot(b, j)]
                    dve.tensor_tensor(to, ring.bank(U_O + j)[0:TR, 0:D].unsqueeze(1), to, ALU.add).then_inc(h_done.sem, 1)


def stage_latent(nc, A, keep, sem, sb, pb):
    h, rows, ident, logits = keep["h"], keep["rows"], keep["ident"], keep["logits0"]
    NH, HD, HP = 16, 16, 32
    KE = NH * HP // 128
    NE = 8
    wq0 = sb("lwq0", [128, KD, D], F32)
    wuk0 = sb("lwuk0", [128, D], F32)
    wuv0 = sb("lwuv0", [128, D], F32)
    wq = sb("lwq", [128, KD, NH, HP], F32)
    wuk = sb("lwuk", [128, NH, HP], F32)
    wuv = sb("lwuv", [128, NH, HP], F32)
    wo = sb("lwo", [128, KE, D], F32)
    wdkv = sb("lwdkv", [128, KD, 128], F32)
    gate = sb("gate0", [128, KD, NE], F32)
    g1 = sb("g1", [128, KD], F32)
    g2 = sb("g2", [TR, D], F32)
    mask = sb("mask", [TR, TR], BF16)
    ident_b = sb("ident_b", [TR, TR], BF16)
    minus_half = sb("minus_half3", [TR, NJ], F32)
    ln_eps = sb("ln_eps3", [TR, NJ], F32)
    rms_eps = sb("rms_eps3", [TR, NJ], F32)
    zero = sb("zero", [TR, NJ, D], F32)
    squares = sb("squares", [TR, NJ, D], F32)
    mean_sq = sb("mean_sq", [TR, NJ], F32)
    mean_sq2 = sb("mean_sq2", [TR, NJ], F32)
    xr = sb("xr", [TR, NJ, D], F32)
    t_rows = sb("t_rows", [TR, NJ, D], F32)
    r_t = sb("r_t", [128, KD, S], F32)
    t_t = sb("t_t", [128, KD, S], F32)
    c_t = sb("c_t", [128, S], F32)
    q_t = sb("lq_t", [128, KE, S], F32)
    k_t = sb("lk_t", [128, KE, S], F32)
    v = sb("lv", [TR, NJ, NH * HP], F32)
    o_t = sb("lo_t", [128, KE, S], F32)
    banks = [pb(f"lring{i}", [128, BANK], F32) for i in range(4)]

    U_C, U_Q = 0, 1
    U_K = U_Q + KE
    U_V = U_K + KE
    U_S = U_V + NJ
    U_O = U_S + NJ * NH
    U_T = U_O + NJ
    U_G = U_T + KD
    U_R = U_G + 1
    heads = Heads(nc, sem, sb, pb, "lat", NH, 4, True, U_S, banks, None)
    c_done, q_done, k_done, v_done = (Tally(sem("l" + n), per) for n, per in
                                      (("c_done", 1), ("q_done", KE), ("k_done", KE), ("v_done", NJ)))
    x1_done = Tally(sem("x1_done"), NJ, NJ)
    t_t_done = Tally(sem("t_t_done"), KD, KD)
    logits_done = Tally(sem("logits_done"), 1, 1)
    r_t_done = Tally(sem("r_t_done"), KD, KD)
    freed = [(c_done, 1)] + [(q_done, i + 1) for i in range(KE)] + [(k_done, i + 1) for i in range(KE)]
    freed += [(v_done, i + 1) for i in range(NJ)] + [(heads.exp_done, i + 1) for i in range(NJ * NH)]
    freed += [(x1_done, i + 1) for i in range(NJ)] + [(t_t_done, i + 1) for i in range(KD)]
    freed += [(logits_done, 1)] + [(r_t_done, i + 1) for i in range(KD)]
    ring = Ring(banks, freed)
    projected = Tally(sem("lprojected"), U_S)
    out_full = Tally(sem("out_full"), NJ)
    turned_t = Tally(sem("turned_t"), KD)
    turned_r = Tally(sem("turned_r"), KD, KD)
    gated = Tally(sem("gated"), 1)
    xn_done = Tally(sem("lxn_done"), NJ, NJ)
    sq_done = Tally(sem("sq_done"), NJ, NJ)
    sq2_done = Tally(sem("sq2_done"), NJ)
    xr_done = Tally(sem("xr_done"), NJ, NJ)
    t_done = Tally(sem("t_done"), NJ)
    h_done = Tally(sem("lh_done"), 1)
    rows_done = Tally(sem("lrows_done"), 1)
    norm = Norm(sem, sb, "ln2", ahead=1)
    rms1 = Power(sem, sb, "rms1", ahead=1)
    rms2 = Power(sem, sb, "rms2", ahead=0)
    w_in, consts, padded = sem("lat_w_in"), sem("lat_consts"), sem("padded")
    weights_padded, pool_seen = sem("weights_padded"), sem("pool_seen")

    with nc.Block() as block:

        @block.sync
        def _(sp):
            sp.dma_start(wq0[:, :, :], rows_of(A["L0_ffn_Wq"])).then_inc(w_in, 16)
            sp.dma_start(wdkv[:, :, :], rows_of(A["L0_ffn_Wdkv"])).then_inc(w_in, 16)
            sp.dma_start(wuk0[:, :], A["L0_ffn_Wuk"]).then_inc(w_in, 16)
            sp.dma_start(wuv0[:, :], A["L0_ffn_Wuv"]).then_inc(w_in, 16)
            sp.dma_start(gate[:, :, :], rows_of(A["L0_ffn_gate_w"])).then_inc(w_in, 16)
            sp.dma_start(g1[:, :], column(A["L0_ffn_g1"], 128), allow_slow_non_contiguous=True).then_inc(w_in, 16)
            sp.dma_start(g2[:, :], A["L0_ffn_g2"].partition_broadcast(TR)).then_inc(w_in, 16)
            sp.wait_ge(padded, 1)
            wo_rows = A["L0_ffn_Wo"].rearrange("(g i p) d -> i p g d", i=128 // HP, p=HD)
            for i in range(128 // HP):
                sp.dma_start(wo[HP * i:HP * i + HD], wo_rows[i]).then_inc(w_in, 16)

        @block.gpsimd
        def _(pool):
            pool.memset(wo[:, :, :], 0.0).then_inc(padded, 1)
            for t, x in ((minus_half, -0.5), (ln_eps, LN_EPS), (rms_eps, RMS_EPS), (mask, 0.0), (ident_b, 0.0)):
                pool.memset(t[:, :], x).then_inc(consts, 1)
            pool.wait_ge(weights_padded, 1)
            pool.wait_ge(consts, 5)
            pool.affine_select(out=mask[:, :], in_=mask[:, :], compare_op=ALU.is_ge, fill=NEG, base=0,
                               pattern=[[-1, TR]], channel_multiplier=1).then_inc(consts, 1)
            pool.affine_select(out=ident_b[:, :], in_=ident_b[:, :], compare_op=ALU.not_equal, fill=1.0, base=0,
                               pattern=[[-1, TR]], channel_multiplier=1).then_inc(consts, 1)

            def prepare(at):
                norm.pool_inverse(pool, ln_eps, minus_half, at)
                rms1.pool_inverse(pool, mean_sq[:, :], sq_done, rms_eps, minus_half, at)

            prepare(at_first)
            with pool.Fori(0, B) as b:
                prepare(at_turn(b))
                rms2.pool_inverse(pool, mean_sq2[:, :], sq2_done, rms_eps, minus_half, at_now(b))
                pool.wait_ge(x1_done.sem, x1_done.now(b, NJ))
                pool.sem_inc(pool_seen, 1)
                pool.tensor_tensor(h[:, slot(b)], h[:, slot(b)], rows[:, slot(b)], ALU.add).then_inc(h_done.sem, 1)
                pool.wait_ge(h_done.sem, h_done.now(b, 1))
                pool.wait_ge(t_done.sem, t_done.now(b, NJ))
                pool.sem_inc(pool_seen, 1)
                pool.tensor_tensor(rows[:, slot(b)], t_rows[:, :, :], zero[:, :, :], ALU.add).then_inc(rows_done.sem, 1)

        @block.scalar
        def _(act):
            heads.act_ahead(act)
            act.sem_inc(t_t_done.sem, t_t_done.ahead)

            def mean_squares(src, to, at, src_done, done):
                for j in range(NJ):
                    act.wait_ge(src_done.sem, at(src_done, j + 1))
                    act.activation(squares[:, j:j + 1], src(j), ACT.Square, scale=D ** -0.5,
                                   accum_out=to[:, j:j + 1]).then_inc(done.sem, 1)

            def copies(u0, dst, full, done, at, scale=None):
                for k in range(KD):
                    act.wait_ge(full.sem, at(full, k + 1))
                    if scale is None:
                        act.activation(dst[:, k], ring.bank(u0 + k)[:, 0:S], ACT.Copy).then_inc(done.sem, 1)
                    else:
                        act.activation(dst[:, k], ring.bank(u0 + k)[:, 0:S], ACT.Identity, scale=scale[:, k:k + 1])\
                           .then_inc(done.sem, 1)

            mean_squares(lambda j: rows[:, j:j + 1], mean_sq, at_first, xn_done, sq_done)
            act.wait_ge(w_in, 16 * 11)
            copies(U_R, r_t, turned_r, r_t_done, at_first, g1)
            with act.Fori(0, B) as b:
                for m in range(KE):
                    act.wait_ge(projected.sem, projected.now(b, U_Q + m + 1))
                    act.activation(q_t[:, m], ring.bank(U_Q + m)[:, 0:S], ACT.Copy, scale=HD ** -0.5).then_inc(q_done.sem, 1)
                heads.act_heads(act, b, extra={
                    8: lambda e, b: mean_squares(lambda j: rows[:, slot(b + 1, j)], mean_sq, at_turn(b), xn_done, sq_done)})
                mean_squares(lambda j: rows[:, slot(b, j)], mean_sq2, at_turn(b), x1_done, sq2_done)
                copies(U_T, t_t, turned_t, t_t_done, at_now(b))
                copies(U_R, r_t, turned_r, r_t_done, at_turn(b), g1)

        @block.tensor
        def _(pe):
            heads.pe_ahead(pe)

            def turn(src, src_done, full, u0, at, b=None):
                pe.wait_ge(src_done.sem, at(src_done, NJ))
                for k in range(KD):
                    if b is not None:
                        ring.claim(pe, b, u0 + k)
                    for j in range(NJ):
                        mm = pe.transpose(ring.bank(u0 + k)[:, TR * j:TR * j + TR], src[:, j, 128 * k:128 * k + 128],
                                          ident[0:TR, 0:TR])
                    mm.then_inc(full.sem, 1)

            turn(xr, xr_done, turned_r, U_R, at_first)
            pe.wait_ge(consts, 7)
            pe.wait_ge(weights_padded, 8)
            pe.wait_ge(w_in, 16 * 11)
            with pe.Fori(0, B) as b:
                pe.wait_ge(r_t_done.sem, r_t_done.before(b, KD))
                ring.claim(pe, b, U_C)
                for k in range(KD):
                    mm = pe.matmul(ring.bank(U_C)[:, 0:S], wdkv[:, k], r_t[:, k], start=k == 0, stop=k == KD - 1)
                mm.then_inc(projected.sem, 1)
                for m in range(KE):
                    ring.claim(pe, b, U_Q + m)
                    for k in range(KD):
                        mm = pe.matmul(ring.bank(U_Q + m)[:, 0:S], wq[:, k, 4 * m:4 * m + 4], r_t[:, k],
                                       start=k == 0, stop=k == KD - 1)
                    mm.then_inc(projected.sem, 1)
                pe.wait_ge(c_done.sem, c_done.now(b, 1))
                for m in range(KE):
                    ring.claim(pe, b, U_K + m)
                    pe.matmul(ring.bank(U_K + m)[:, 0:S], wuk[:, 4 * m:4 * m + 4], c_t[:, :], start=True, stop=True)\
                      .then_inc(projected.sem, 1)
                for j in range(NJ):
                    ring.claim(pe, b, U_V + j)
                    pe.matmul(ring.bank(U_V + j)[0:TR, :], c_t[:, TR * j:TR * j + TR], wuv[:, :, :], start=True, stop=True)\
                      .then_inc(projected.sem, 1)
                pe.wait_ge(q_done.sem, q_done.now(b, KE))
                pe.wait_ge(k_done.sem, k_done.now(b, KE))
                pe.wait_ge(v_done.sem, v_done.now(b, NJ))
                part = lambda hd: slice(HP * (hd % 4), HP * (hd % 4) + HP)
                heads.pe_heads(pe, b, ring.claim,
                               lambda hd, j: q_t[part(hd), hd // 4, TR * j:TR * j + TR],
                               lambda hd, n: k_t[part(hd), hd // 4, 0:n],
                               lambda hd, kt: v[:, kt, HP * hd:HP * hd + HP], ident, (ident_b[:, :], mask[:, :]))
                pe.wait_ge(heads.heads_out.sem, heads.heads_out.now(b, KE))
                for j in range(NJ):
                    ring.claim(pe, b, U_O + j)
                    for k in range(KE):
                        mm = pe.matmul(ring.bank(U_O + j)[0:TR, 0:D], o_t[:, k, TR * j:TR * j + TR], wo[:, k],
                                       start=k == 0, stop=k == KE - 1)
                    mm.then_inc(out_full.sem, 1)
                turn(t_rows, t_done, turned_t, U_T, at_now(b), b)
                pe.wait_ge(t_t_done.sem, t_t_done.now(b, KD))
                ring.claim(pe, b, U_G)
                for j in range(NJ):
                    for k in range(KD):
                        mm = pe.matmul(ring.bank(U_G)[0:TR, NE * j:NE * j + NE], t_t[:, k, TR * j:TR * j + TR], gate[:, k],
                                       start=k == 0, stop=k == KD - 1)
                mm.then_inc(gated.sem, 1)
                turn(xr, xr_done, turned_r, U_R, at_turn(b), b)

        @block.vector
        def _(dve):
            heads.dve_ahead(dve)
            dve.sem_inc(x1_done.sem, x1_done.ahead)
            dve.sem_inc(logits_done.sem, logits_done.ahead)

            def prepare(tile, row, at):
                norm.dve_stats(dve, tile, at)
                norm.dve_apply(dve, tile, row, at, xn_done)

            def prepare2(row, at):
                dve.wait_ge(rms1.done.sem, at(rms1.done, 1))
                for j in range(NJ):
                    dve.tensor_scalar(xr[:, j:j + 1], row(j), rms1.inv[:, j:j + 1], None, ALU.mult).then_inc(xr_done.sem, 1)

            dve.memset(zero[:, :, :], 0.0).then_inc(weights_padded, 1)
            dve.memset(wq[:, :, :, :], 0.0).then_inc(weights_padded, 1)
            dve.memset(wuk[:, :, :], 0.0).then_inc(weights_padded, 1)
            dve.memset(wuv[:, :, :], 0.0).then_inc(weights_padded, 1)
            prepare(lambda j: h[:, j:j + 1], lambda j: rows[:, j:j + 1], at_first)
            prepare2(lambda j: rows[:, j:j + 1], at_first)
            dve.wait_ge(w_in, 16 * 11)
            dve.wait_ge(weights_padded, 4)
            for dst, src in ((wq[:, 0], wq0[:, 0]), (wq[:, 1], wq0[:, 1]), (wuk[:, :, :], wuk0[:, :]), (wuv[:, :, :], wuv0[:, :])):
                dve.tensor_copy(dst[:, :, 0:HD], src.rearrange("p (n e) -> p n e", e=HD)).then_inc(weights_padded, 1)
            with dve.Fori(0, B) as b:
                dve.wait_ge(projected.sem, projected.now(b, U_C + 1))
                dve.tensor_copy(c_t[:, :], ring.bank(U_C)[:, 0:S]).then_inc(c_done.sem, 1)
                for m in range(KE):
                    dve.wait_ge(projected.sem, projected.now(b, U_K + m + 1))
                    dve.tensor_copy(k_t[:, m], ring.bank(U_K + m)[:, 0:S]).then_inc(k_done.sem, 1)
                for j in range(NJ):
                    dve.wait_ge(projected.sem, projected.now(b, U_V + j + 1))
                    dve.tensor_copy(v[:, j], ring.bank(U_V + j)[0:TR, :]).then_inc(v_done.sem, 1)
                heads.dve_heads(dve, b, o_t, extra={
                    6: lambda e, b: prepare(lambda j: h[:, slot(b + 1, j)], lambda j: rows[:, slot(b + 1, j)], at_turn(b)),
                    10: lambda e, b: prepare2(lambda j: rows[:, slot(b + 1, j)], at_turn(b))})
                for j in range(NJ):
                    dve.wait_ge(out_full.sem, out_full.now(b, j + 1))
                    to = rows[:, slot(b, j)]
                    dve.tensor_tensor(to, ring.bank(U_O + j)[0:TR, 0:D].unsqueeze(1), to, ALU.add).then_inc(x1_done.sem, 1)
                dve.wait_ge(rms2.done.sem, rms2.done.now(b, 1))
                for j in range(NJ):
                    dve.scalar_tensor_tensor(out=t_rows[:, j:j + 1], in0=rows[:, slot(b, j)], scalar=rms2.inv[:, j:j + 1],
                                             in1=g2[:, :].unsqueeze(1), op0=ALU.mult, op1=ALU.mult).then_inc(t_done.sem, 1)
                dve.wait_ge(gated.sem, gated.now(b, 1))
                dve.tensor_copy(logits[:, slot(b)], ring.bank(U_G)[0:TR, 0:NJ * NE].rearrange("p (j e) -> p j e", e=NE))\
                   .then_inc(logits_done.sem, 1)


class Routing:

    def __init__(self, sem, sb, pb, name, n_experts, slots):
        self.ne = n_experts
        shape = [TR, NT, n_experts]
        self.work = sb(name + "_work", shape, F32)
        self.pick = sb(name + "_pick", shape, F32)
        self.first = sb(name + "_first", shape, F32)
        self.second = sb(name + "_second", shape, F32)
        self.top = sb(name + "_top", [TR, 2, NT], F32)
        self.best = sb(name + "_best", [TR, NT], F32)
        self.mask = sb(name + "_mask", shape, F32)
        self.place = sb(name + "_place", shape, F32)
        self.total = sb(name + "_total", [128, NT, n_experts], F32)
        self.until = sb(name + "_until", [128, NT, n_experts], F32)
        self.rank = sb(name + "_rank", [TR, n_experts], F32)
        self.tri = sb(name + "_tri", [TR, TR], F32)
        self.ones = sb(name + "_ones", [128, 128], F32)
        self.slot_f = sb(name + "_slot_f", [TR, 2, NT], F32)
        self.slot = slots
        half = NT // 2 if NT * n_experts > BANK else NT
        self.halves = [slice(a, a + half) for a in range(0, NT, half)]
        self.p_before = [pb(f"{name}_p_before{i}", [128, BANK], F32) for i in range(len(self.halves))]
        self.p_total = [pb(f"{name}_p_total{i}", [128, BANK], F32) for i in range(len(self.halves))]
        self.consts = sem(name + "_consts")
        self.mask_ready, self.counted = sem(name + "_mask_ready"), sem(name + "_counted")
        self.n_counts = 0

    def pool_consts(self, pool, seen):
        pool.iota(self.rank[:, :], pattern=[[-1, self.ne]], base=self.ne, channel_multiplier=0,
                  allow_small_or_imprecise_dtypes=True).then_inc(self.consts, 1)
        pool.memset(self.ones[:, :], 1.0).then_inc(self.consts, 1)
        pool.memset(self.tri[:, :], 1.0).then_inc(seen, 1)
        pool.wait_ge(seen, 1)
        pool.affine_select(out=self.tri[:, :], in_=self.tri[:, :], compare_op=ALU.is_gt, fill=0.0, base=0,
                           pattern=[[1, TR]], channel_multiplier=-1).then_inc(self.consts, 1)

    def dve_top2(self, dve, ch, scores):
        wide = lambda a: a.unsqueeze(2).to_broadcast([TR, NT, self.ne])
        rank = self.rank[:, :].unsqueeze(1).to_broadcast([TR, NT, self.ne])
        for i, (src, to) in enumerate(((scores, self.first), (self.work[:, :, :], self.second))):
            if i:
                ch.link(dve.scalar_tensor_tensor(out=self.work[:, :, :], in0=self.first[:, :, :], scalar=NEG, in1=scores,
                                                 op0=ALU.mult, op1=ALU.add))
            ch.link(dve.tensor_reduce(self.top[:, i], src, AX.X, ALU.max))
            ch.link(dve.tensor_tensor(self.pick[:, :, :], src, wide(self.top[:, i]), ALU.is_ge))
            ch.link(dve.tensor_tensor(self.pick[:, :, :], self.pick[:, :, :], rank, ALU.mult))
            ch.link(dve.tensor_reduce(self.best[:, :], self.pick[:, :, :], AX.X, ALU.max))
            ch.link(dve.tensor_tensor(to[:, :, :], self.pick[:, :, :], wide(self.best[:, :]), ALU.is_equal))

    def pe_counts(self, pe, n):
        pe.wait_ge(self.consts, 3)
        pe.wait_ge(self.mask_ready, n)
        for i, part in enumerate(self.halves):
            w = (part.stop - part.start) * self.ne
            pe.matmul(self.p_before[i][0:TR, 0:w], self.tri[:, :], self.mask[:, part], start=True, stop=True)
            mm = pe.matmul(self.p_total[i][:, 0:w], self.ones[0:TR, :], self.mask[:, part], start=True, stop=True)
        mm.then_inc(self.counted, 1)

    def dve_places(self, dve, ch):
        self.n_counts += 1
        dve.sem_inc(self.mask_ready, 1)
        dve.wait_ge(self.counted, self.n_counts)
        for i, part in enumerate(self.halves):
            w = (part.stop - part.start) * self.ne
            last = dve.tensor_copy(self.total[:, part].rearrange("p t e -> p (t e)"), self.p_total[i][:, 0:w])
        ch.link(last)
        for e in range(self.ne):
            last = dve.tensor_tensor_scan(self.until[:, :, e], self.ones[:, 0:NT], self.total[:, :, e], 0.0, ALU.mult, ALU.add)
        ch.link(last)
        ch.link(dve.tensor_tensor(self.total[:, :, :], self.until[:, :, :], self.total[:, :, :], ALU.subtract))
        for i, part in enumerate(self.halves):
            w = (part.stop - part.start) * self.ne
            last = dve.tensor_tensor(self.place[:, part].rearrange("p t e -> p (t e)"), self.p_before[i][0:TR, 0:w],
                                     self.total[0:TR, part].rearrange("p t e -> p (t e)"), ALU.add)
        ch.link(last)

    def dve_take(self, dve, ch, values, chosen, to):
        ch.link(dve.tensor_tensor(self.pick[:, :, :], values, chosen[:, :, :], ALU.mult))
        ch.link(dve.tensor_reduce(to, self.pick[:, :, :], AX.X, ALU.add))


class Experts:

    def __init__(self, nc, sem, sb, pb, name, tile_rows, n_chunks, nc_turn, gated, weight_of):
        self.r, self.n, self.turns, self.ct, self.gated = tile_rows, 3 * tile_rows, n_chunks // nc_turn, nc_turn, gated
        self.weight_of = weight_of
        r, n, f = self.r, self.n, nc_turn
        self.x = sb(name + "_x", [r, 2, 3, D], F32)
        self.x_t = sb(name + "_x_t", [128, 2, KD, n], F32)
        self.w1 = sb(name + "_w1", [128, 2, KD, 512], F32)
        self.w3 = sb(name + "_w3", [128, 2, KD, 512], F32) if gated else None
        self.w2 = sb(name + "_w2", [128, 2, 4, D], F32)
        self.act = sb(name + "_act", [128, 2, n], F32) if gated else None
        self.hid = sb(name + "_hid", [128, 2, 4, n], F32)
        self.y = sb(name + "_y", [r, 2, 3, D], F32)
        self.p_x = [pb(f"{name}_p_x{k}", [128, BANK], F32) for k in range(2)]
        self.p_g = [pb(f"{name}_p_g{k}", [128, BANK], F32) for k in range(2)]
        self.p_u = [pb(f"{name}_p_u{k}", [128, BANK], F32) for k in range(2)] if gated else None
        self.p_y = [pb(f"{name}_p_y{k}", [128, BANK], F32) for k in range(2)]
        self.x_in = [Tally(sem(f"{name}_x_in{u}"), 16 * f // 2, 16 * (1 - u)) for u in range(2)]
        self.y_out = [Tally(sem(f"{name}_y_out{u}"), 16 * f // 2, 1) for u in range(2)]
        self.turned = Tally(sem(name + "_turned"), f, 2)
        self.x_t_done = Tally(sem(name + "_x_t_done"), 2 * f, 2)
        self.up_full = Tally(sem(name + "_up_full"), 4 * f)
        self.act_done = Tally(sem(name + "_act_done"), 4 * f, 4)
        self.hid_done = Tally(sem(name + "_hid_done"), 4 * f, 4) if gated else self.act_done
        self.y_full = Tally(sem(name + "_y_full"), 3 * f, 7)
        self.y_done = Tally(sem(name + "_y_done"), 3 * f, 3)

    def x_load(self, sp, b, i, src):
        if b is not None:
            sp.wait_ge(self.turned.sem, self.turned.now(b, i - 2))
        u = i % 2
        sp.dma_start(self.x[:, u], src).then_inc(self.x_in[u].sem, 16)

    def x_here(self, b, i):
        t = self.x_in[i % 2]
        if b is None:
            return 16
        return b * t.per + 16 * (i // 2 + 1)

    def pe_ahead(self, pe):
        pe.sem_inc(self.y_full.sem, self.y_full.ahead)
        pe.sem_inc(self.turned.sem, self.turned.ahead - 1)

    def pe_turn(self, pe, b, i, ident):
        u = i % 2
        pe.wait_ge(self.x_in[u].sem, self.x_here(b, i))
        if b is not None:
            pe.wait_ge(self.x_t_done.sem, self.x_t_done.now(b, 2 * (i - 1)))
        for k in range(KD):
            for j in range(3):
                mm = pe.transpose(self.p_x[k][:, self.r * j:self.r * (j + 1)], self.x[:, u, j, k::2], ident[0:self.r, 0:self.r])
        mm.then_inc(self.turned.sem, 1)

    def pe_up(self, pe, b, i):
        u, w = i % 2, self.weight_of(i)
        pe.wait_ge(self.x_t_done.sem, self.x_t_done.now(b, 2 * i))
        for c in range(4):
            done = self.hid_done if self.gated else self.act_done
            pe.wait_ge(done.sem, done.now(b, 4 * i + c - 1))
            pairs = ((self.w1, self.p_g), (self.w3, self.p_u)) if self.gated else ((self.w1, self.p_g),)
            for wt, to in pairs:
                for k in range(KD):
                    mm = pe.matmul(to[c % 2][:, 0:self.n], wt[:, w, k, c::4], self.x_t[:, u, k], start=k == 0, stop=k == KD - 1)
            mm.then_inc(self.up_full.sem, 1)

    def pe_down(self, pe, b, i):
        u, w = i % 2, self.weight_of(i)
        pe.wait_ge(self.hid_done.sem, self.hid_done.now(b, 4 * i + 4))
        for j in range(3):
            n = 3 * i + j
            pe.wait_ge(self.y_done.sem, self.y_done.now(b, n - 1))
            for c in range(4):
                mm = pe.matmul(self.p_y[(3 * u + j) % 2][0:self.r, 0:D], self.hid[:, u, c, self.r * j:self.r * (j + 1)],
                               self.w2[:, w, c], start=c == 0, stop=c == 3)
            mm.then_inc(self.y_full.sem, 1)

    def act_up(self, act, b, i):
        u = i % 2
        for c in range(4):
            act.wait_ge(self.up_full.sem, self.up_full.now(b, 4 * i + c + 1))
            if self.gated:
                act.wait_ge(self.hid_done.sem, self.hid_done.now(b, 4 * i + c - 1))
            else:
                act.wait_ge(self.y_full.sem, self.y_full.now(b, 3 * (i - 1)))
            to = self.act[:, c % 2] if self.gated else self.hid[:, u, c]
            act.activation(to, self.p_g[c % 2][:, 0:self.n], ACT.Silu).then_inc(self.act_done.sem, 1)

    def dve_up(self, dve, b, i):
        u = i % 2
        for c in range(4):
            dve.wait_ge(self.act_done.sem, self.act_done.now(b, 4 * i + c + 1))
            dve.wait_ge(self.y_full.sem, self.y_full.now(b, 3 * (i - 1)))
            dve.tensor_tensor(self.hid[:, u, c], self.p_u[c % 2][:, 0:self.n], self.act[:, c % 2], ALU.mult)\
               .then_inc(self.hid_done.sem, 1)

    def x_copies(self, eng, copy, b, i):
        u = i % 2
        eng.wait_ge(self.turned.sem, 2 if b is None else self.turned.now(b, i))
        for k in range(KD):
            copy(self.x_t[:, u, k], self.p_x[k][:, 0:self.n]).then_inc(self.x_t_done.sem, 1)

    def dve_out(self, dve, b, i):
        u = i % 2
        for j in range(3):
            dve.wait_ge(self.y_full.sem, self.y_full.now(b, 3 * i + j + 1))
            if j == 0:
                t = self.y_out[u]
                dve.wait_ge(t.sem, t.now(b, 16 * (i // 2)))
            dve.tensor_copy(self.y[:, u, j], self.p_y[(3 * u + j) % 2][0:self.r, 0:D]).then_inc(self.y_done.sem, 1)

    def dve_add(self, dve, b, i, h, factor):
        for j in range(3):
            n = 3 * i + j
            dve.wait_ge(self.y_full.sem, self.y_full.now(b, n + 1))
            dve.wait_ge(self.y_done.sem, self.y_done.now(b, n - 2))
            to = h(j)
            dve.scalar_tensor_tensor(out=to, in0=self.p_y[n % 2][0:self.r, 0:D].unsqueeze(1), scalar=factor, in1=to,
                                     op0=ALU.mult, op1=ALU.add).then_inc(self.y_done.sem, 1)

    def sp_ahead(self, sp):
        for t in self.y_out:
            sp.sem_inc(t.sem, t.ahead)

    def y_store(self, eng, b, i, dst):
        eng.wait_ge(self.y_done.sem, self.y_done.now(b, 3 * i + 3))
        eng.dma_start(dst, self.y[:, i % 2]).then_inc(self.y_out[i % 2].sem, 16)


SLOTS = 11520


def chunk_rows(dram, b, per_turn, i, r):
    return dram[bass.ds(b * (per_turn * 3 * r) + i * 3 * r, 3 * r)].rearrange("(j p) d -> p j d", p=r)


def pool_scatter(pool, slots, rows, dram, limit, done, done_slots):
    if done_slots:
        pool.wait_ge(done_slots[0], done_slots[1])
    for t in range(NT):
        for i in range(2):
            pool.indirect_dma_start(dram, bass.IndirectOffsetOnAxis(ap=slots[:, i, t:t + 1], axis=0), rows[:, t], None,
                                    bounds_check=limit, oob_is_err=False).then_inc(done, 16)
    pool.wait_ge(done, 16 * 2 * NT)


class Combine:

    DEPTH = 4

    def __init__(self, sem, sb, name):
        self.g = sb(name + "_g", [TR, self.DEPTH, 2, D], F32)
        self.here = [sem(f"{name}_here{u}") for u in range(self.DEPTH)]
        self.used = sem(name + "_used")

    def pool_gather(self, pool, t, slots, ys):
        if t >= self.DEPTH:
            pool.wait_ge(self.used, 2 * (t - self.DEPTH + 1))
        for i in range(2):
            pool.indirect_dma_start(self.g[:, t % self.DEPTH, i], None, ys,
                                    bass.IndirectOffsetOnAxis(ap=slots[:, i, t:t + 1], axis=0))\
                .then_inc(self.here[t % self.DEPTH], 16)

    def dve_add(self, dve, t, h, weight):
        dve.wait_ge(self.here[t % self.DEPTH], 32 * (t // self.DEPTH + 1))
        for i in range(2):
            if i:
                dve.wait_ge(self.used, 2 * t + 1)
            dve.scalar_tensor_tensor(out=h[:, t], in0=self.g[:, t % self.DEPTH, i], scalar=weight[:, i, t:t + 1], in1=h[:, t],
                                     op0=ALU.mult, op1=ALU.add).then_inc(self.used, 1)


def stage_experts0(nc, A, keep, sem, sb, pb):
    h, rows, ident, logits = keep["h"], keep["rows"], keep["ident"], keep["logits0"]
    NE, R = 8, TR
    N = 3 * R
    NC = SLOTS // N
    MOST = NTOK // N
    assert NC == 2 * NTOK // N + NE
    slots = sb("slots0", [TR, 2, NT], I32)
    rt = Routing(sem, sb, pb, "rt0", NE, slots)
    weight = sb("weight0", [TR, 2, NT], F32)
    filled = sb("filled", [128, NE, MOST], F32)
    bound = sb("bound", [128, MOST], F32)
    n_chunks = sb("n_chunks", [128, NE], F32)
    chunks_until = sb("chunks_until", [128, NE], F32)
    start = sb("start", [128, NE], F32)
    chunk_id = sb("chunk_id", [128, NC], F32)
    passed = sb("passed", [128, NC, NE], F32)
    of_chunk = sb("of_chunk", [128, NC], F32)
    part_id = sb("part_id", [128, 1], F32)
    w_row = sb("w_row", [128, NC], I32)
    w_row_now = sb("w_row_now", [128, 2], I32)
    xs, ys = keep["xs"], keep["ys"]
    rdve, rseen, iotas = sem("rt0_dve"), sem("rt0_seen"), sem("rt0_iotas")
    gap, gap_exp = sem("gap"), sem("gap_exp")
    slots_done, scattered = sem("slots0_done"), sem("scattered0")

    with nc.Block() as block:

        @block.gpsimd
        def _(pool):
            rt.pool_consts(pool, rseen)
            pool.iota(bound[:, :], pattern=[[N, MOST]], base=0, channel_multiplier=0,
                      allow_small_or_imprecise_dtypes=True).then_inc(iotas, 1)
            pool.iota(chunk_id[:, :], pattern=[[1, NC]], base=0, channel_multiplier=0,
                      allow_small_or_imprecise_dtypes=True).then_inc(iotas, 1)
            pool.iota(part_id[:, :], pattern=[[0, 1]], base=0, channel_multiplier=1,
                      allow_small_or_imprecise_dtypes=True).then_inc(iotas, 1)
            pool_scatter(pool, rt.slot, rows, xs, SLOTS - 1, scattered, (slots_done, 1))

        @block.scalar
        def _(act):
            act.wait_ge(gap, 1)
            act.activation(weight[:, 1], weight[:, 1], ACT.Exp).then_inc(gap_exp, 1)

        @block.tensor
        def _(pe):
            rt.pe_counts(pe, 1)

        @block.vector
        def _(dve):
            ch = Chain(dve, rdve)
            dve.wait_ge(rt.consts, 3)
            dve.wait_ge(iotas, 3)
            rt.dve_top2(dve, ch, logits[:, 0:NT])
            ch.link(dve.tensor_tensor(weight[:, 1], rt.top[:, 1], rt.top[:, 0], ALU.subtract))
            dve.sem_inc(gap, 1)
            ch.link(dve.tensor_tensor(rt.mask[:, :, :], rt.first[:, :, :], rt.second[:, :, :], ALU.add))
            rt.dve_places(dve, ch)
            ch.link(dve.tensor_tensor(filled[:, :, :], rt.until[:, NT - 1].unsqueeze(2).to_broadcast([128, NE, MOST]),
                                      bound[:, :].unsqueeze(1).to_broadcast([128, NE, MOST]), ALU.is_gt))
            ch.link(dve.tensor_reduce(n_chunks[:, :], filled[:, :, :], AX.X, ALU.add))
            ch.link(dve.tensor_tensor_scan(chunks_until[:, :], rt.ones[:, 0:NE], n_chunks[:, :], 0.0, ALU.mult, ALU.add))
            ch.link(dve.tensor_tensor(start[:, :], chunks_until[:, :], n_chunks[:, :], ALU.subtract))
            ch.link(dve.tensor_scalar(start[:, :], start[:, :], float(N), None, ALU.mult))
            ch.link(dve.tensor_tensor(rt.place[:, :, :], rt.place[:, :, :],
                                      start[0:TR].unsqueeze(1).to_broadcast([TR, NT, NE]), ALU.add))
            for i, chosen in enumerate((rt.first, rt.second)):
                rt.dve_take(dve, ch, rt.place[:, :, :], chosen, rt.slot_f[:, i])
            dve.tensor_copy(rt.slot[:, :, :], rt.slot_f[:, :, :]).then_inc(slots_done, 1)
            ch.link(dve.tensor_tensor(passed[:, :, :], chunk_id[:, :].unsqueeze(2).to_broadcast([128, NC, NE]),
                                      chunks_until[:, :].unsqueeze(1).to_broadcast([128, NC, NE]), ALU.is_ge))
            ch.link(dve.tensor_reduce(of_chunk[:, :], passed[:, :, :], AX.X, ALU.add))
            ch.link(dve.tensor_scalar(of_chunk[:, :], of_chunk[:, :], float(NE - 1), 128.0, ALU.min, ALU.mult))
            ch.link(dve.tensor_scalar(w_row[:, :], of_chunk[:, :], part_id[:, 0:1], None, ALU.add))
            dve.wait_ge(gap_exp, 1)
            ch.link(dve.tensor_scalar(weight[:, 0], weight[:, 1], 1.0, None, ALU.add))
            ch.link(dve.reciprocal(weight[:, 0], weight[:, 0]))
            ch.link(dve.tensor_tensor(weight[:, 1], weight[:, 1], weight[:, 0], ALU.mult))

    with ExitStack() as inner:
        sb2 = lambda name, shape, dt: inner.enter_context(nc.sbuf_tensor(name, shape, dt))
        pb2 = lambda name, shape, dt: inner.enter_context(nc.psum_tensor(name, shape, dt))
        ex = Experts(nc, sem, sb2, pb2, "ex0", R, NC, 2, False, lambda i: i)
        w_in = [Tally(sem(f"w0_in{u}"), 32) for u in range(2)]
        row_copied = Tally(sem("row_copied"), 2)
        w1_rows = A["L0_ffn_w1"].rearrange("e (p k) n -> (e p) (k n)", k=KD)
        w2_rows = A["L0_ffn_w2"].rearrange("e (p c) n -> (e p) (c n)", c=4)

        with nc.Block() as block:

            @block.sync
            def _(sp):
                ex.sp_ahead(sp)
                ex.x_load(sp, None, 0, xs[0:N].rearrange("(j p) d -> p j d", p=R))
                with sp.Fori(0, ex.turns) as b:
                    for i in range(2):
                        ex.x_load(sp, b, i + 1, chunk_rows(xs, b, 2, i + 1, R))
                    for i in range(2):
                        ex.y_store(sp, b, i, chunk_rows(ys, b, 2, i, R))
                for u in range(2):
                    sp.wait_ge(ex.y_out[u].sem, ex.y_out[u].now(ex.turns, 0))

            @block.gpsimd
            def _(pool):
                with pool.Fori(0, ex.turns) as b:
                    for u in range(2):
                        pool.wait_ge(ex.y_full.sem, ex.y_full.now(b, 3 * (u - 1)))
                        pool.sem_inc(rseen, 1)
                        pool.tensor_copy(w_row_now[:, u:u + 1], w_row[:, bass.ds(b * 2 + u, 1)]).then_inc(row_copied.sem, 1)
                        pool.wait_ge(row_copied.sem, row_copied.now(b, u + 1))
                        pool.sem_inc(rseen, 1)
                        for w, src in ((ex.w1, w1_rows), (ex.w2, w2_rows)):
                            pool.indirect_dma_start(w[:, u].rearrange("p a n -> p (a n)"), None, src,
                                                    bass.IndirectOffsetOnAxis(ap=w_row_now[:, u:u + 1], axis=0))\
                                .then_inc(w_in[u].sem, 16)

            @block.scalar
            def _(act):
                act.sem_inc(ex.act_done.sem, ex.act_done.ahead)
                with act.Fori(0, ex.turns) as b:
                    for i in range(2):
                        ex.act_up(act, b, i)

            @block.tensor
            def _(pe):
                ex.pe_ahead(pe)
                ex.pe_turn(pe, None, 0, ident)
                with pe.Fori(0, ex.turns) as b:
                    for i in range(2):
                        pe.wait_ge(w_in[i].sem, w_in[i].now(b, 32))
                        ex.pe_up(pe, b, i)
                        ex.pe_turn(pe, b, i + 1, ident)
                        ex.pe_down(pe, b, i)

            @block.vector
            def _(dve):
                dve.sem_inc(ex.y_done.sem, ex.y_done.ahead)
                ex.x_copies(dve, dve.tensor_copy, None, 0)
                with dve.Fori(0, ex.turns) as b:
                    for i in range(2):
                        ex.x_copies(dve, dve.tensor_copy, b, i + 1)
                        ex.dve_out(dve, b, i)

    with ExitStack() as inner:
        cb = Combine(sem, lambda name, shape, dt: inner.enter_context(nc.sbuf_tensor(name, shape, dt)), "cb0")
        with nc.Block() as block:

            @block.gpsimd
            def _(pool):
                for t in range(NT):
                    cb.pool_gather(pool, t, rt.slot, ys)

            @block.vector
            def _(dve):
                for t in range(NT):
                    cb.dve_add(dve, t, h, weight)


def stage_distance(nc, A, keep, sem, sb, pb):
    h, rows, ident, logits = keep["h"], keep["rows"], keep["ident"], keep["logits1"]
    R, NE = 32, 16
    u3 = sb("u3", [128, KD, 3, R], F32)
    gate = sb("gate1", [128, KD, NE], F32)
    minus_half = sb("minus_half5", [TR, NJ], F32)
    eps = sb("ln_eps5", [TR, NJ], F32)
    zero = sb("zero5", [TR, NJ, D], F32)
    xn = sb("dxn", [TR, NJ, D], F32)
    xc = sb("dxc", [TR, NJ, D], F32)
    x_t = sb("dx_t", [128, KD, S], F32)
    c_t = sb("dc_t", [128, KD, S], F32)
    q_t = sb("dq_t", [3 * R, S], F32)
    k_t = sb("dk_t", [3 * R, S], F32)
    prob = sb("dprob", [TR, NJ, S], F32)
    prob_t = sb("dprob_t", [TR, NJ, S], F32)
    neg_max = sb("dneg_max", [TR, NJ], F32)
    row_sum = sb("drow_sum", [TR, NJ], F32)
    inv_sum = sb("dinv_sum", [TR, NJ], F32)
    p_s = [pb(f"dp_s{j}", [TR, BANK], F32) for j in range(NJ)]
    p_t = [pb(f"dp_t{j}", [TR, BANK], F32) for j in range(NJ)]
    p_x = [pb(f"dp_x{k}", [128, BANK], F32) for k in range(KD)]

    norm = Norm(sem, sb, "ln5", ahead=1)
    norm_c = Norm(sem, sb, "ln6", ahead=0)
    xn_done, xc_done = Tally(sem("dxn_done"), NJ, NJ), Tally(sem("dxc_done"), NJ)
    turned_x, turned_c = Tally(sem("dturned_x"), 1, 1), Tally(sem("dturned_c"), 1, 1)
    kept_x, kept_c = Tally(sem("dkept_x"), 1, 1), Tally(sem("dkept_c"), 1, 1)
    x_t_done, c_t_done = Tally(sem("dx_t_done"), KD, KD), Tally(sem("dc_t_done"), KD, KD)
    y_full, y_done = Tally(sem("dy_full"), 1, 1), Tally(sem("dy_done"), 4, 4)
    scored, max_done, exp_done = (Tally(sem("d" + n), NJ, NJ) for n in ("scored", "max_done", "exp_done"))
    inv_done, h_done = Tally(sem("dinv_done"), 1), Tally(sem("dh_done"), NJ)
    turned_p, p_t_done = Tally(sem("dturned_p"), 1), Tally(sem("dp_t_done"), NJ)
    weighted = Tally(sem("dweighted"), NJ, NJ)
    gated, logits_done = Tally(sem("dgated"), 1), Tally(sem("dlogits_done"), 1, 1)
    w_in, consts, pool_seen = sem("dist_w_in"), sem("dist_consts"), sem("dpool_seen")

    with nc.Block() as block:

        @block.sync
        def _(sp):
            for i in range(3):
                sp.dma_start(u3[:, :, i], rows_of(A["L1_attn_U"])).then_inc(w_in, 16)
            sp.dma_start(gate[:, :, :], rows_of(A["L1_ffn_gate_w"])).then_inc(w_in, 16)

        @block.gpsimd
        def _(pool):
            pool.memset(minus_half[:, :], -0.5).then_inc(consts, 1)
            pool.memset(eps[:, :], LN_EPS).then_inc(consts, 1)
            pool.memset(zero[:, :, :], 0.0).then_inc(consts, 1)
            pool.wait_ge(consts, 5)
            pool.sem_inc(kept_c.sem, kept_c.ahead)

            def keep_rows(src, src_done, to, done, at):
                pool.wait_ge(src_done.sem, at(src_done, NJ))
                pool.sem_inc(pool_seen, 1)
                pool.tensor_tensor(to, src[:, :, :], zero[:, :, :], ALU.add).then_inc(done.sem, 1)

            norm.pool_inverse(pool, eps, minus_half, at_first)
            keep_rows(xn, xn_done, rows[:, 0:NJ], kept_x, at_first)
            with pool.Fori(0, B) as b:
                norm.pool_inverse(pool, eps, minus_half, at_turn(b))
                keep_rows(xn, xn_done, rows[:, slot(b + 1)], kept_x, at_turn(b))
                norm_c.pool_inverse(pool, eps, minus_half, at_now(b))
                keep_rows(xc, xc_done, rows[:, slot(b)], kept_c, at_now(b))

        @block.scalar
        def _(act):
            act.sem_inc(c_t_done.sem, c_t_done.ahead)
            act.sem_inc(logits_done.sem, logits_done.ahead)

            def project(at):
                act.wait_ge(turned_x.sem, at(turned_x, 1))
                for k in range(KD):
                    act.activation(x_t[:, k], p_x[k][:, 0:S], ACT.Copy).then_inc(x_t_done.sem, 1)
                act.wait_ge(y_full.sem, at(y_full, 1))
                act.activation(q_t[0:R, :], p_x[0][0:R, 0:S], ACT.Copy, scale=2.0).then_inc(y_done.sem, 1)
                act.activation(k_t[0:R, :], p_x[0][0:R, 0:S], ACT.Copy).then_inc(y_done.sem, 1)
                act.activation(q_t[R:2 * R, :], p_x[0][R:2 * R, 0:S], ACT.Square).then_inc(y_done.sem, 1)
                act.activation(k_t[2 * R:3 * R, :], p_x[0][2 * R:3 * R, 0:S], ACT.Square).then_inc(y_done.sem, 1)

            def exps(at):
                for j in range(NJ):
                    act.wait_ge(max_done.sem, at(max_done, j + 1))
                    act.activation(prob[:, j], p_s[j][:, 0:S], ACT.Exp, bias=neg_max[:, j:j + 1],
                                   accum_out=row_sum[:, j:j + 1]).then_inc(exp_done.sem, 1)

            project(at_first)
            exps(at_first)
            with act.Fori(0, B) as b:
                act.wait_ge(turned_p.sem, turned_p.now(b, 1))
                for j in range(NJ):
                    act.activation(prob_t[:, j], p_t[j][:, 0:S], ACT.Copy).then_inc(p_t_done.sem, 1)
                project(at_turn(b))
                act.wait_ge(inv_done.sem, inv_done.now(b, 1))
                exps(at_turn(b))
                act.wait_ge(turned_c.sem, turned_c.now(b, 1))
                for k in range(KD):
                    act.activation(c_t[:, k], p_x[k][:, 0:S], ACT.Copy).then_inc(c_t_done.sem, 1)
                act.wait_ge(gated.sem, gated.now(b, 1))
                act.activation(logits[:, slot(b)], p_t[0][:, 0:NJ * NE].rearrange("p (j e) -> p j e", e=NE), ACT.Copy)\
                   .then_inc(logits_done.sem, 1)

        @block.tensor
        def _(pe):
            pe.sem_inc(turned_c.sem, turned_c.ahead)
            pe.sem_inc(weighted.sem, weighted.ahead)

            def turn(src, src_done, done, at):
                pe.wait_ge(src_done.sem, at(src_done, NJ))
                for k in range(KD):
                    for j in range(NJ):
                        mm = pe.transpose(p_x[k][:, TR * j:TR * j + TR], src[:, j, 128 * k:128 * k + 128], ident[0:TR, 0:TR])
                mm.then_inc(done.sem, 1)

            def project(at):
                pe.wait_ge(x_t_done.sem, at(x_t_done, KD))
                for k in range(KD):
                    mm = pe.matmul(p_x[0][0:3 * R, 0:S], u3[:, k], x_t[:, k], start=k == 0, stop=k == KD - 1)
                mm.then_inc(y_full.sem, 1)

            def scores(at, b=None):
                pe.wait_ge(y_done.sem, at(y_done, 4))
                for j in range(NJ):
                    if b is not None:
                        pe.wait_ge(h_done.sem, h_done.now(b, j + 1))
                    pe.matmul(p_s[j][:, 0:S], q_t[:, TR * j:TR * j + TR], k_t[:, :], start=True, stop=True)\
                      .then_inc(scored.sem, 1)

            pe.wait_ge(consts, 5)
            pe.wait_ge(w_in, 16 * 4)
            turn(xn, xn_done, turned_x, at_first)
            project(at_first)
            scores(at_first)
            with pe.Fori(0, B) as b:
                pe.wait_ge(exp_done.sem, exp_done.before(b, NJ))
                pe.wait_ge(logits_done.sem, logits_done.before(b, 1))
                for j in range(NJ):
                    for kt in range(NJ):
                        mm = pe.transpose(p_t[kt][:, TR * j:TR * j + TR], prob[:, j, TR * kt:TR * kt + TR], ident[0:TR, 0:TR])
                mm.then_inc(turned_p.sem, 1)
                pe.wait_ge(c_t_done.sem, c_t_done.before(b, KD))
                turn(xn, xn_done, turned_x, at_turn(b))
                pe.wait_ge(kept_x.sem, kept_x.before(b, 1))
                pe.wait_ge(p_t_done.sem, p_t_done.now(b, NJ))
                for j in range(NJ):
                    for kt in range(NJ):
                        mm = pe.matmul(p_s[j][:, 0:D].unsqueeze(1), prob_t[:, kt, TR * j:TR * j + TR], rows[:, slot(b, kt)],
                                       start=kt == 0, stop=kt == NJ - 1)
                    mm.then_inc(weighted.sem, 1)
                project(at_turn(b))
                scores(at_turn(b), b)
                turn(xc, xc_done, turned_c, at_now(b))
                pe.wait_ge(c_t_done.sem, c_t_done.now(b, KD))
                for j in range(NJ):
                    for k in range(KD):
                        mm = pe.matmul(p_t[0][:, NE * j:NE * j + NE], c_t[:, k, TR * j:TR * j + TR], gate[:, k],
                                       start=k == 0, stop=k == KD - 1)
                mm.then_inc(gated.sem, 1)

        @block.vector
        def _(dve):
            def maxima(at):
                for j in range(NJ):
                    dve.wait_ge(scored.sem, at(scored, j + 1))
                    dve.tensor_reduce(neg_max[:, j:j + 1], p_s[j][:, 0:S], AX.X, ALU.max, negate=True)\
                       .then_inc(max_done.sem, 1)

            dve.memset(q_t[2 * R:3 * R, :], -1.0).then_inc(consts, 1)
            dve.memset(k_t[R:2 * R, :], -1.0).then_inc(consts, 1)
            norm.dve_stats(dve, lambda j: h[:, j:j + 1], at_first)
            norm.dve_apply(dve, lambda j: h[:, j:j + 1], lambda j: xn[:, j:j + 1], at_first, xn_done)
            maxima(at_first)
            with dve.Fori(0, B) as b:
                norm.dve_stats(dve, lambda j: h[:, slot(b + 1, j)], at_turn(b))
                dve.wait_ge(turned_x.sem, turned_x.before(b, 1))
                dve.wait_ge(kept_x.sem, kept_x.before(b, 1))
                norm.dve_apply(dve, lambda j: h[:, slot(b + 1, j)], lambda j: xn[:, j:j + 1], at_turn(b), xn_done)
                dve.wait_ge(exp_done.sem, exp_done.before(b, NJ))
                dve.reciprocal(inv_sum[:, :], row_sum[:, :]).then_inc(inv_done.sem, 1)
                dve.wait_ge(inv_done.sem, inv_done.now(b, 1))
                for j in range(NJ):
                    dve.wait_ge(weighted.sem, weighted.now(b, j + 1))
                    to = h[:, slot(b, j)]
                    dve.scalar_tensor_tensor(out=to, in0=p_s[j][:, 0:D].unsqueeze(1), scalar=inv_sum[:, j:j + 1], in1=to,
                                             op0=ALU.mult, op1=ALU.add).then_inc(h_done.sem, 1)
                maxima(at_turn(b))
                dve.wait_ge(h_done.sem, h_done.now(b, NJ))
                dve.sem_inc(norm_c.stats_seen, 1)
                norm_c.dve_stats(dve, lambda j: h[:, slot(b, j)], at_now(b))
                dve.wait_ge(turned_c.sem, turned_c.before(b, 1))
                dve.wait_ge(kept_c.sem, kept_c.before(b, 1))
                norm_c.dve_apply(dve, lambda j: h[:, slot(b, j)], lambda j: xc[:, j:j + 1], at_now(b), xc_done)


CAP = 720
LOWEST = -3.4028234663852886e38


def stage_experts1(nc, A, keep, sem, sb, pb):
    h, rows, ident, logits = keep["h"], keep["rows"], keep["ident"], keep["logits1"]
    xs, ys = keep["xs"], keep["ys"]
    NE, R = 16, 120
    N = 3 * R
    assert NE * CAP == SLOTS and CAP % N == 0
    shape = [TR, NT, NE]
    slots = sb("slots1", [TR, 2, NT], I32)
    weight = sb("weight1", [TR, 2, NT], F32)
    gather_slot = sb("gather_slot", [TR, 2, NT], I32)
    route_sem = [sem(n) for n in ("rt1_dve", "rt1_seen", "rt1_in", "shifted", "exp1_done", "slots1_done", "scattered1")]
    rdve, rseen, b_in, shifted, exp_done, slots_done, scattered = route_sem
    steps = 31

    with ExitStack() as inner:
        sb2 = lambda name, shape, dt: inner.enter_context(nc.sbuf_tensor(name, shape, dt))
        pb2 = lambda name, shape, dt: inner.enter_context(nc.psum_tensor(name, shape, dt))
        rt = Routing(sem, sb2, pb2, "rt1", NE, slots)
        gate_b = sb2("gate_b", [TR, NE], F32)
        score = sb2("score", shape, F32)
        token_max = sb2("token_max", [TR, NT], F32)
        own = sb2("own", shape, F32)
        above = sb2("above", shape, F32)
        equal = sb2("equal", shape, F32)
        count = sb2("count", [TR, NE], F32)
        limit = sb2("limit", [TR, NE], I32)
        trial = sb2("trial", [TR, NE], I32)
        raised = sb2("raised", [TR, NE], I32)
        bit_f = sb2("bit_f", [TR, NE], F32)
        bit = sb2("bit", [TR, NE], I32)
        n_above = sb2("n_above", [TR, NE], F32)
        expert_slot = sb2("expert_slot", [TR, NE], F32)
        p_count = pb2("p_count", [TR, BANK], F32)
        summed = Tally(sem("summed"), 1, 1)
        totalled = Tally(sem("totalled"), 1, 1)
        search = LoopChain(None, sem("search"), 7)

        with nc.Block() as block:

            @block.sync
            def _(sp):
                sp.dma_start(gate_b[:, :], A["L1_ffn_gate_b"].partition_broadcast(TR)).then_inc(b_in, 16)

            @block.gpsimd
            def _(pool):
                rt.pool_consts(pool, rseen)
                pool.iota(expert_slot[:, :], pattern=[[CAP, NE]], base=-SLOTS, channel_multiplier=0,
                          allow_small_or_imprecise_dtypes=True).then_inc(rt.consts, 1)

            @block.scalar
            def _(act):
                act.wait_ge(shifted, 1)
                act.activation(score[:, :, :], score[:, :, :], ACT.Exp).then_inc(exp_done, 1)

            @block.tensor
            def _(pe):
                def total(value):
                    pe.wait_ge(summed.sem, value)
                    pe.matmul(p_count[:, 0:NE], rt.ones[0:TR, 0:TR], count[:, :], start=True, stop=True).then_inc(totalled.sem, 1)

                pe.wait_ge(rt.consts, 4)
                total(1)
                with pe.Fori(0, steps) as b:
                    total(summed.now(b, 1))
                rt.pe_counts(pe, 1)
                rt.pe_counts(pe, 2)

            @block.vector
            def _(dve):
                ch = Chain(dve, rdve)
                wide = lambda a: a.unsqueeze(2).to_broadcast(shape)
                each = lambda a: a.unsqueeze(1).to_broadcast(shape)
                lg = logits[:, 0:NT]
                ch.link(dve.tensor_reduce(token_max[:, :], lg, AX.X, ALU.max))
                ch.link(dve.tensor_tensor(score[:, :, :], lg, wide(token_max[:, :]), ALU.subtract))
                dve.sem_inc(shifted, 1)
                dve.wait_ge(exp_done, 1)
                ch.link(dve.tensor_reduce(token_max[:, :], score[:, :, :], AX.X, ALU.add))
                ch.link(dve.reciprocal(token_max[:, :], token_max[:, :]))
                ch.link(dve.tensor_tensor(score[:, :, :], score[:, :, :], wide(token_max[:, :]), ALU.mult))
                dve.wait_ge(b_in, 16)
                ch.link(dve.tensor_tensor(score[:, :, :], score[:, :, :], each(gate_b[:, :]), ALU.add))
                dve.wait_ge(rt.consts, 4)
                rt.dve_top2(dve, ch, score[:, :, :])
                ch.link(dve.tensor_tensor(rt.mask[:, :, :], rt.first[:, :, :], rt.second[:, :, :], ALU.add))
                ch.link(dve.tensor_scalar(own[:, :, :], rt.mask[:, :, :], 1.0, -LOWEST, ALU.subtract, ALU.mult))
                ch.link(dve.tensor_tensor(rt.work[:, :, :], lg, rt.mask[:, :, :], ALU.mult))
                ch.link(dve.tensor_tensor(own[:, :, :], own[:, :, :], rt.work[:, :, :], ALU.add))

                def tokens_reaching(threshold, link):
                    link(dve.tensor_tensor(above[:, :, :], own[:, :, :], each(threshold), ALU.is_ge))
                    dve.tensor_reduce(count[:, :], above[:, :, :].rearrange("p t e -> p e t"), AX.X, ALU.add)\
                       .then_inc(summed.sem, 1)

                ch.link(dve.memset(bit_f[:, :], 0.0))
                tokens_reaching(bit_f[:, :], ch.link)
                dve.wait_ge(totalled.sem, 1)
                ch.link(dve.tensor_scalar(n_above[:, :], p_count[:, 0:NE], float(CAP), 1.0, ALU.is_ge, ALU.subtract))
                dve.tensor_copy(limit[:, :], n_above[:, :])
                ch.link(dve.memset(bit_f[:, :], float(2 ** (steps - 1))))
                with dve.Fori(0, steps) as b:
                    search.eng = dve
                    search.start(b)
                    search.link(dve.tensor_copy(bit[:, :], bit_f[:, :]))
                    search.link(dve.tensor_tensor(trial[:, :], limit[:, :], bit[:, :], ALU.bitwise_xor))
                    tokens_reaching(trial[:, :].bitcast(F32), search.link)
                    dve.wait_ge(totalled.sem, totalled.now(b, 1))
                    search.link(dve.tensor_scalar(n_above[:, :], p_count[:, 0:NE], float(CAP), None, ALU.is_ge))
                    search.link(dve.tensor_tensor(raised[:, :], n_above[:, :], bit_f[:, :], ALU.mult))
                    search.link(dve.tensor_tensor(limit[:, :], limit[:, :], raised[:, :], ALU.bitwise_xor))
                    search.link(dve.tensor_scalar(bit_f[:, :], bit_f[:, :], 0.5, None, ALU.mult))
                    search.end()

                threshold = each(limit[:, :].bitcast(F32))
                ch.link(dve.tensor_tensor(equal[:, :, :], own[:, :, :], threshold, ALU.is_equal))
                ch.link(dve.tensor_tensor(equal[:, :, :], equal[:, :, :], rt.mask[:, :, :], ALU.mult))
                ch.link(dve.tensor_tensor(rt.mask[:, :, :], own[:, :, :], threshold, ALU.is_gt))
                rt.dve_places(dve, ch)
                ch.link(dve.tensor_copy(above[:, :, :], rt.mask[:, :, :]))
                ch.link(dve.tensor_tensor(score[:, :, :], rt.place[:, :, :], above[:, :, :], ALU.mult))
                ch.link(dve.tensor_copy(n_above[:, :], rt.until[0:TR, NT - 1]))
                ch.link(dve.tensor_copy(rt.mask[:, :, :], equal[:, :, :]))
                rt.dve_places(dve, ch)
                ch.link(dve.tensor_tensor(rt.place[:, :, :], rt.place[:, :, :], each(n_above[:, :]), ALU.add))
                ch.link(dve.scalar_tensor_tensor(out=equal[:, :, :], in0=rt.place[:, :, :], scalar=float(CAP), in1=equal[:, :, :],
                                                 op0=ALU.is_lt, op1=ALU.mult))
                ch.link(dve.tensor_tensor(rt.place[:, :, :], rt.place[:, :, :], equal[:, :, :], ALU.mult))
                ch.link(dve.tensor_tensor(rt.place[:, :, :], rt.place[:, :, :], score[:, :, :], ALU.add))
                ch.link(dve.tensor_tensor(above[:, :, :], above[:, :, :], equal[:, :, :], ALU.add))
                ch.link(dve.tensor_tensor(rt.place[:, :, :], rt.place[:, :, :], each(expert_slot[:, :]), ALU.add))
                ch.link(dve.tensor_tensor(rt.place[:, :, :], rt.place[:, :, :], above[:, :, :], ALU.mult))
                ch.link(dve.tensor_scalar(rt.place[:, :, :], rt.place[:, :, :], float(SLOTS), None, ALU.add))
                ch.link(dve.tensor_tensor(above[:, :, :], above[:, :, :], lg, ALU.mult))
                for i, chosen in enumerate((rt.first, rt.second)):
                    rt.dve_take(dve, ch, rt.place[:, :, :], chosen, rt.slot_f[:, i])
                    rt.dve_take(dve, ch, above[:, :, :], chosen, weight[:, i])
                ch.link(dve.tensor_copy(rt.slot[:, :, :], rt.slot_f[:, :, :]))
                ch.link(dve.tensor_scalar(gather_slot[:, :, :], rt.slot_f[:, :, :], float(SLOTS - 1), None, ALU.min))

    with ExitStack() as inner:
        sb2 = lambda name, shape, dt: inner.enter_context(nc.sbuf_tensor(name, shape, dt))
        pb2 = lambda name, shape, dt: inner.enter_context(nc.psum_tensor(name, shape, dt))
        ex = Experts(nc, sem, sb2, pb2, "sh", TR, 2 * B, 2, True, lambda i: i)
        w_in = sem("shared_w_in")

        with nc.Block() as block:

            @block.sync
            def _(sp):
                for s in range(2):
                    for w, name in ((ex.w1, "sw1"), (ex.w3, "sw3")):
                        sp.dma_start(w[:, s], A["L1_ffn_" + name][s].rearrange("(p k) n -> p k n", k=KD)).then_inc(w_in, 16)
                    sp.dma_start(ex.w2[:, s], A["L1_ffn_sw2"][s].rearrange("(p c) n -> p c n", c=4)).then_inc(w_in, 16)
                ex.x_load(sp, None, 0, rows[:, 0:NJ])
                with sp.Fori(0, ex.turns) as b:
                    for i in range(2):
                        ex.x_load(sp, b, i + 1, rows[:, slot(b + i)])

            @block.gpsimd
            def _(pool):
                pool_scatter(pool, rt.slot, rows, xs, SLOTS - 1, scattered, None)

            @block.scalar
            def _(act):
                act.sem_inc(ex.act_done.sem, ex.act_done.ahead)
                with act.Fori(0, ex.turns) as b:
                    for i in range(2):
                        ex.act_up(act, b, i)

            @block.tensor
            def _(pe):
                ex.pe_ahead(pe)
                ex.pe_turn(pe, None, 0, ident)
                pe.wait_ge(w_in, 16 * 6)
                with pe.Fori(0, ex.turns) as b:
                    for i in range(2):
                        ex.pe_up(pe, b, i)
                        ex.pe_turn(pe, b, i + 1, ident)
                        ex.pe_down(pe, b, i)

            @block.vector
            def _(dve):
                dve.sem_inc(ex.y_done.sem, ex.y_done.ahead)
                dve.sem_inc(ex.hid_done.sem, ex.hid_done.ahead)
                ex.x_copies(dve, dve.tensor_copy, None, 0)
                with dve.Fori(0, ex.turns) as b:
                    for i in range(2):
                        ex.dve_up(dve, b, i)
                        ex.x_copies(dve, dve.tensor_copy, b, i + 1)
                        ex.dve_add(dve, b, i, lambda j: h[:, slot(b, j)], 0.5)

    with ExitStack() as inner:
        sb2 = lambda name, shape, dt: inner.enter_context(nc.sbuf_tensor(name, shape, dt))
        pb2 = lambda name, shape, dt: inner.enter_context(nc.psum_tensor(name, shape, dt))
        ex = Experts(nc, sem, sb2, pb2, "ex1", R, SLOTS // N, 4, True, lambda i: i // 2)
        w_in = [Tally(sem(f"w1_in{u}"), 48) for u in range(2)]

        with nc.Block() as block:

            @block.sync
            def _(sp):
                ex.sp_ahead(sp)
                ex.x_load(sp, None, 0, xs[0:N].rearrange("(j p) d -> p j d", p=R))
                with sp.Fori(0, ex.turns) as b:
                    ex.x_load(sp, b, 1, chunk_rows(xs, b, 4, 1, R))
                    for i in range(4):
                        if i < 3:
                            ex.x_load(sp, b, i + 2, chunk_rows(xs, b, 4, i + 2, R))
                        ex.y_store(sp, b, i, chunk_rows(ys, b, 4, i, R))
                for u in range(2):
                    sp.wait_ge(ex.y_out[u].sem, ex.y_out[u].now(ex.turns, 0))

            @block.gpsimd
            def _(pool):
                with pool.Fori(0, ex.turns) as b:
                    for u in range(2):
                        pool.wait_ge(ex.y_full.sem, ex.y_full.now(b, 6 * (u - 1)))
                        pool.sem_inc(rseen, 1)
                        e = bass.ds(b * 2 + u, 1)
                        for w, name in ((ex.w1, "ew1"), (ex.w3, "ew3")):
                            pool.dma_start(w[:, u], A["L1_ffn_" + name][e].rearrange("e (p k) n -> p (e k) n", k=KD)).then_inc(w_in[u].sem, 16)
                        pool.dma_start(ex.w2[:, u], A["L1_ffn_ew2"][e].rearrange("e (p c) n -> p (e c) n", c=4)).then_inc(w_in[u].sem, 16)

            @block.scalar
            def _(act):
                act.sem_inc(ex.act_done.sem, ex.act_done.ahead)
                with act.Fori(0, ex.turns) as b:
                    for i in range(4):
                        ex.act_up(act, b, i)

            @block.tensor
            def _(pe):
                ex.pe_ahead(pe)
                ex.pe_turn(pe, None, 0, ident)
                with pe.Fori(0, ex.turns) as b:
                    for i in range(4):
                        if i % 2 == 0:
                            pe.wait_ge(w_in[i // 2].sem, w_in[i // 2].now(b, 48))
                        ex.pe_up(pe, b, i)
                        ex.pe_turn(pe, b, i + 1, ident)
                        ex.pe_down(pe, b, i)

            @block.vector
            def _(dve):
                dve.sem_inc(ex.y_done.sem, ex.y_done.ahead)
                dve.sem_inc(ex.hid_done.sem, ex.hid_done.ahead)
                ex.x_copies(dve, dve.tensor_copy, None, 0)
                with dve.Fori(0, ex.turns) as b:
                    for i in range(4):
                        ex.dve_up(dve, b, i)
                        ex.x_copies(dve, dve.tensor_copy, b, i + 1)
                        ex.dve_out(dve, b, i)

    with ExitStack() as inner:
        cb = Combine(sem, lambda name, shape, dt: inner.enter_context(nc.sbuf_tensor(name, shape, dt)), "cb1")
        out_stored = sem("out_stored")
        out = keep["out"].rearrange("b (j p) d -> p (b j) d", p=TR)

        with nc.Block() as block:

            @block.sync
            def _(sp):
                for b in range(B):
                    sp.wait_ge(cb.used, 2 * NJ * (b + 1))
                    sp.dma_start(out[:, NJ * b:NJ * b + NJ], h[:, NJ * b:NJ * b + NJ]).then_inc(out_stored, 16)
                sp.wait_ge(out_stored, 16 * B)

            @block.gpsimd
            def _(pool):
                for t in range(NT):
                    cb.pool_gather(pool, t, gather_slot, ys)

            @block.vector
            def _(dve):
                for t in range(NT):
                    cb.dve_add(dve, t, h, weight)


STAGES = (stage_front, stage_attention, stage_latent, stage_experts0, stage_distance, stage_experts1)


def build(nc, A, out):
    with ExitStack() as whole:
        def sem(name):
            return whole.enter_context(nc.semaphore(name))

        def big(name):
            return whole.enter_context(nc.sbuf_tensor(name, [TR, NT + NJ, D], F32))

        keep = {
            "ident": whole.enter_context(nc.sbuf_tensor("ident", [128, 128], F32)),
            "logits0": whole.enter_context(nc.sbuf_tensor("logits0", [TR, NT + NJ, 8], F32)),
            "logits1": whole.enter_context(nc.sbuf_tensor("logits1", [TR, NT + NJ, 16], F32)),
            "ident_done": sem("ident_done"),
            "h0": nc.dram_tensor("h0", [NTOK, D], F32).ap(),
            "xs": nc.dram_tensor("xs", [SLOTS + 640, D], F32).ap(),
            "ys": nc.dram_tensor("ys", [SLOTS, D], F32).ap(),
            "out": out,
        }
        for stage in STAGES:
            if stage is stage_attention:
                keep["h"] = big("h")
            if stage is stage_latent:
                keep["rows"] = big("rows")
            with ExitStack() as here:
                stage_sems = []

                def stage_sem(name):
                    stage_sems.append(nc.alloc_semaphore(name=name))
                    return stage_sems[-1]

                sb = lambda name, shape, dt: here.enter_context(nc.sbuf_tensor(name, shape, dt))
                pb = lambda name, shape, dt: here.enter_context(nc.psum_tensor(name, shape, dt))
                stage(nc, A, keep, stage_sem, sb, pb)
            nc.clear_and_free_semaphores(stage_sems)
            nc.all_engine_barrier()


_INS = ['x', 'x_txt', 'L0_tok_Wa', 'L0_tok_ba', 'L0_tok_Wd1', 'L0_tok_bd1', 'L0_tok_Wd2', 'L0_tok_bd2', 'L0_tok_Wd3',
        'L0_tok_bd3', 'L0_txt_weight', 'L0_txt_lora_A', 'L0_txt_lora_B', 'L0_attn_Wq', 'L0_attn_bq', 'L0_attn_Wk',
        'L0_attn_bk', 'L0_attn_Wv', 'L0_attn_bv', 'L0_attn_Wo', 'L0_attn_bo', 'L0_ffn_g1', 'L0_ffn_Wq', 'L0_ffn_Wdkv',
        'L0_ffn_Wuk', 'L0_ffn_Wuv', 'L0_ffn_Wo', 'L0_ffn_g2', 'L0_ffn_gate_w', 'L0_ffn_w1', 'L0_ffn_w2', 'L1_attn_U',
        'L1_ffn_gate_w', 'L1_ffn_gate_b', 'L1_ffn_ew1', 'L1_ffn_ew3', 'L1_ffn_ew2', 'L1_ffn_sw1', 'L1_ffn_sw3',
        'L1_ffn_sw2']


def kernel(**inputs):
    from concourse import bacc
    from concourse.bass_utils import run_bass_kernel_spmd

    nc = bacc.Bacc("TRN2", target_bir_lowering=False, num_devices=1)
    arrays, A = {}, {}
    for name in _INS:
        a = np.ascontiguousarray(inputs[name])
        arrays[f"in_{name}"] = a
        A[name] = nc.dram_tensor(f"in_{name}", a.shape, mybir.dt.from_np(a.dtype), kind="ExternalInput").ap()
    out = nc.dram_tensor("out_h", (B, S, D), F32, kind="ExternalOutput").ap()
    build(nc, A, out)
    return run_bass_kernel_spmd(nc, [arrays], core_ids=[0]).results[0]["out_h"]
```

```python
from contextlib import ExitStack

import concourse.bass as bass
import numpy as np
from concourse import mybir

ALU = mybir.AluOpType
ACT = mybir.ActivationFunctionType
AX = mybir.AxisListType
F32 = mybir.dt.float32
F32R = mybir.dt.float32r
BF16 = mybir.dt.bfloat16
I32 = mybir.dt.int32

B, IMG, TXT, D = 16, 256, 32, 256
S = IMG + TXT
TR = 96
NJ = S // TR
NT = B * NJ
NTOK = B * S
KD = D // 128
LN_EPS, RMS_EPS = 1e-5, 1e-6
BANK = 512
NEG = -1e30


class Tally:

    def __init__(self, sem, per, ahead=0):
        self.sem, self.per, self.ahead = sem, per, ahead

    def now(self, b, n):
        assert isinstance(b, int) or self.ahead + n > 0
        return b * self.per + (self.ahead + n)

    def before(self, b, n):
        assert self.ahead + n > self.per
        return b * self.per + (self.ahead + n - self.per)


def wait(eng, tally, b, n):
    if isinstance(b, int) and b * tally.per + tally.ahead + n <= 0:
        return
    eng.wait_ge(tally.sem, tally.now(b, n))


class Chain:

    def __init__(self, eng, sem):
        self.eng, self.sem, self.n = eng, sem, 0

    def link(self, ins):
        ins.then_inc(self.sem, 1)
        self.n += 1
        self.eng.wait_ge(self.sem, self.n)


class LoopChain:

    def __init__(self, eng, sem, per, ahead=0):
        self.eng, self.tally, self.n = eng, Tally(sem, per, ahead), 0

    def start(self, b):
        self.b, self.n = b, 0

    def link(self, ins):
        ins.then_inc(self.tally.sem, 1)
        self.n += 1
        assert self.n <= self.tally.per
        self.eng.wait_ge(self.tally.sem, self.tally.now(self.b, self.n))

    def end(self):
        assert self.n == self.tally.per, self.n


def slot(b, j=None):
    return bass.ds(b * NJ, NJ) if j is None else bass.ds(b * NJ + j, 1)


def column(a, n):
    return a.rearrange("(c p) -> p c", p=n)


def rows_of(a, n=128):
    return a.rearrange("(k p) n -> p k n", p=n)


def split_high(act, to, src):
    return act.activation(to, src, ACT.Copy)


def split_low(dve, to, src, high):
    return dve.tensor_tensor(to, src, high.bitcast(F32), ALU.subtract)


def matmul3(pe, out, lhs, rhs, start, stop):
    pe.matmul(out, lhs[0], rhs[0], start=start, stop=False)
    pe.matmul(out, lhs[0], rhs[1], start=False, stop=False)
    return pe.matmul(out, lhs[1], rhs[0], start=False, stop=stop)


def product(pe, out, lhs, rhs, start, stop):
    return matmul3(pe, out, lhs, rhs, start, stop) if isinstance(lhs, tuple) else pe.matmul(out, lhs, rhs, start=start, stop=stop)


def stage_front(nc, A, keep, sem, sb, pb):
    ident = keep["ident"]
    h0 = keep["h0"]
    NI = B // 4
    xt = sb("xt", [128, NI, 8, IMG], F32)
    out_rows = sb("out_rows", [128, 2, 8, IMG], F32)
    low = sb("low", [128, 1024], F32)
    high = sb("high", [128, 1024], F32)
    approx = [sb(f"approx{lv}", [128, 512 >> 2 * lv], F32) for lv in range(2)]
    detail = [sb(f"detail{lv}", [128, NI, 3, 512 >> 2 * lv], F32) for lv in range(3)]
    coarse = sb("coarse", [128, NI, 32], F32)
    back = [sb(f"back{lv}", [128, 512 >> 2 * lv], F32) for lv in range(2)]
    vv = sb("vv", [128, 512], F32)
    scratch = sb("scratch", [128, 3 * 512], F32)
    w_band = [sb(f"w_band{lv}", [128, 3, (512 >> 2 * lv) * 3], F32) for lv in range(3)]
    w_app = sb("w_app", [128, 32], F32)
    dots = sb("dots", [128, NI, 10], F32)
    bias = sb("bias", [128, 10], F32)
    z = sb("z", [128, NI, 10], F32)
    zm = sb("zm", [128, NI, 3], F32)
    zs = sb("zs", [128, NI, 4], F32)
    wt = sb("wt", [128, NI, 10], F32)
    nwt = sb("nwt", [128, NI, 10], F32)
    same_image = sb("same_image", [128, 4, 32], F32)
    tok_id = sb("tok_id", [128, 4], I32)
    text = sb("text", [128, 4, D], F32)
    lora = sb("lora", [128, 4, 8], F32)
    lora_t = sb("lora_t", [8, 4, 128], F32)
    lora_b = sb("lora_b", [8, D], F32)
    text_out = sb("text_out", [128, 4, D], F32)
    p_sum = pb("p_sum", [128, BANK], F32)
    p_lora_t = pb("p_lora_t", [128, BANK], F32)
    p_lora = pb("p_lora", [128, 4, BANK], F32)

    img_in = [sem(f"img_in{t}") for t in range(NI)]
    weights_in, small_in, ids_in = sem("weights_in"), sem("small_in"), sem("ids_in")
    text_in, lora_in = sem("text_in"), sem("lora_in")
    ident_done, same_done = keep["ident_done"], sem("same_done")
    fdve, dots_done, sums_done = sem("front_dve"), sem("dots_done"), sem("sums_done")
    z_ready, exp_z = sem("z_ready"), sem("exp_z")
    lora_t_full, lora_t_done, lora_full = sem("lora_t_full"), sem("lora_t_done"), sem("lora_full")
    text_done, rows_done, text_stored = sem("text_done"), sem("rows_done"), sem("text_stored")
    rows_out = [sem(f"rows_out{u}") for u in range(2)]

    x_rows = A["x"].rearrange("b (i r) w o -> (b i) r (w o)", r=8)
    h0_img = h0.rearrange("(b s) d -> b s d", b=B)

    with nc.Block() as block:

        @block.sync
        def _(sp):
            for t in range(NI):
                sp.dma_start(xt[:, t], x_rows[t * 128:(t + 1) * 128]).then_inc(img_in[t], 16)
            for lv, name in enumerate(("L0_tok_Wd3", "L0_tok_Wd2", "L0_tok_Wd1")):
                src = A[name].rearrange("(c p q) k -> p c (q k)", c=3, p=32)
                for m in range(4):
                    sp.dma_start(w_band[lv][32 * m:32 * m + 32], src).then_inc(weights_in, 16)
            for m in range(4):
                sp.dma_start(w_app[32 * m:32 * m + 32], A["L0_tok_Wa"].rearrange("(p q) k -> p (q k)", p=32)).then_inc(weights_in, 16)
            for t in range(NI):
                sp.wait_ge(rows_done, t + 1)
                for m in range(4):
                    sp.dma_start(h0_img[4 * t + m, 0:IMG].rearrange("(p r) d -> p r d", r=8),
                                 out_rows[32 * m:32 * m + 32, t % 2]).then_inc(rows_out[t % 2], 16)
            for u in range(2):
                sp.wait_ge(rows_out[u], 16 * 4 * (NI // 2))

        @block.scalar
        def _(act):
            act.dma_start(tok_id[:, :], A["x_txt"].rearrange("b s -> (b s)").rearrange("(q p) -> p q", p=128),
                          allow_slow_non_contiguous=True).then_inc(ids_in, 16)
            act.dma_start(lora_b[:, :], A["L0_txt_lora_B"]).then_inc(small_in, 16)
            for name, a, n in (("L0_tok_bd3", 0, 3), ("L0_tok_bd2", 3, 3), ("L0_tok_bd1", 6, 3), ("L0_tok_ba", 9, 1)):
                act.dma_start(bias[:, a:a + n], A[name].partition_broadcast(128)).then_inc(small_in, 16)
            act.wait_ge(z_ready, 1)
            act.activation(z[:, :, :], z[:, :, :], ACT.Exp).then_inc(exp_z, 1)
            act.wait_ge(text_done, 4)
            for q in range(4):
                for m in range(4):
                    act.dma_start(h0_img[4 * q + m, IMG:S], text_out[32 * m:32 * m + 32, q]).then_inc(text_stored, 16)
            act.wait_ge(text_stored, 16 * 16)

        @block.gpsimd
        def _(pool):
            pool.memset(ident[:, :], 0.0).then_inc(ident_done, 1)
            pool.memset(same_image[:, :, :], 1.0).then_inc(same_done, 1)
            pool.wait_ge(ident_done, 1)
            pool.affine_select(out=ident[:, :], in_=ident[:, :], compare_op=ALU.not_equal, fill=1.0, base=0,
                               pattern=[[-1, 128]], channel_multiplier=1).then_inc(ident_done, 1)
            pool.wait_ge(same_done, 1)
            pool.affine_select(out=same_image[:, :, :], in_=same_image[:, :, :], compare_op=ALU.is_ge, fill=0.0, base=0,
                               pattern=[[-32, 4], [0, 32]], channel_multiplier=1).then_inc(same_done, 1)
            pool.wait_ge(same_done, 2)
            pool.affine_select(out=same_image[:, :, :], in_=same_image[:, :, :], compare_op=ALU.is_ge, fill=0.0, base=31,
                               pattern=[[32, 4], [0, 32]], channel_multiplier=-1).then_inc(same_done, 1)
            pool.wait_ge(ids_in, 16)
            for q in range(4):
                rows = bass.IndirectOffsetOnAxis(ap=tok_id[:, q:q + 1], axis=0)
                pool.indirect_dma_start(lora[:, q], None, A["L0_txt_lora_A"], rows).then_inc(lora_in, 16)
                pool.indirect_dma_start(text[:, q], None, A["L0_txt_weight"], rows).then_inc(text_in, 16)
            pool.wait_ge(lora_in, 64)
            pool.wait_ge(text_in, 64)

        @block.tensor
        def _(pe):
            pe.wait_ge(ident_done, 2)
            pe.wait_ge(lora_in, 64)
            for q in range(4):
                mm = pe.transpose(p_lora_t[0:8, q * 128:(q + 1) * 128], lora[:, q], ident[:, :])
            mm.then_inc(lora_t_full, 1)
            pe.wait_ge(lora_t_done, 1)
            pe.wait_ge(small_in, 16 * 5)
            for q in range(4):
                mm = pe.matmul(p_lora[:, q, 0:D], lora_t[:, q], lora_b[:, :], start=True, stop=True)
            mm.then_inc(lora_full, 1)
            pe.wait_ge(same_done, 3)
            pe.wait_ge(dots_done, NI * 10)
            pe.matmul(p_sum[:, 0:NI * 10], same_image[:, :, :], dots[:, :, :], start=True, stop=True).then_inc(sums_done, 1)

        @block.vector
        def _(dve):
            ch = Chain(dve, fdve)

            def analyse(src, rows, cols, lv, t):
                n = rows * cols // 2
                lo = low[:, 0:n].rearrange("p (r c) -> p r c", r=rows)
                hi = high[:, 0:n].rearrange("p (r c) -> p r c", r=rows)
                dve.tensor_tensor(lo, src[:, :, 0::2], src[:, :, 1::2], ALU.add)
                ch.link(dve.tensor_tensor(hi, src[:, :, 0::2], src[:, :, 1::2], ALU.subtract))
                to = [a.rearrange("p (r c) -> p r c", r=rows // 2)
                      for a in (approx[lv][:, :] if lv < 2 else coarse[:, t], detail[lv][:, t, 0], detail[lv][:, t, 1], detail[lv][:, t, 2])]
                dve.tensor_tensor(to[0], lo[:, 0::2], lo[:, 1::2], ALU.add)
                dve.tensor_tensor(to[1], lo[:, 0::2], lo[:, 1::2], ALU.subtract)
                dve.tensor_tensor(to[2], hi[:, 0::2], hi[:, 1::2], ALU.add)
                ch.link(dve.tensor_tensor(to[3], hi[:, 0::2], hi[:, 1::2], ALU.subtract))

            def analysis(t):
                analyse(xt[:, t], 8, IMG, 0, t)
                analyse(approx[0][:, :].rearrange("p (r c) -> p r c", r=4), 4, IMG // 2, 1, t)
                analyse(approx[1][:, :].rearrange("p (r c) -> p r c", r=2), 2, IMG // 4, 2, t)

            dve.wait_ge(weights_in, 16 * 16)
            for t in range(NI):
                dve.wait_ge(img_in[t], 16)
                analysis(t)
                for lv in range(3):
                    for k in range(3):
                        w = w_band[lv][:, :, :].rearrange("p c (q k) -> p (c q) k", k=3)[:, :, k]
                        n = 3 * (512 >> 2 * lv)
                        ch.link(dve.tensor_tensor_reduce(
                            scratch[:, 0:n], detail[lv][:, t].rearrange("p c q -> p (c q)"), w,
                            0.5 ** (lv + 1), 0.0, ALU.mult, ALU.add, dots[:, t, 3 * lv + k:3 * lv + k + 1]))
                        dve.sem_inc(dots_done, 1)
                ch.link(dve.tensor_tensor_reduce(scratch[:, 0:32], coarse[:, t], w_app[:, :], 0.125, 0.0,
                                                 ALU.mult, ALU.add, dots[:, t, 9:10]))
                dve.sem_inc(dots_done, 1)
            dve.wait_ge(lora_t_full, 1)
            dve.tensor_copy(lora_t[:, :, :], p_lora_t[0:8, :].rearrange("p (q n) -> p q n", q=4)).then_inc(lora_t_done, 1)
            dve.wait_ge(small_in, 16 * 5)
            dve.wait_ge(sums_done, 1)
            ch.link(dve.tensor_tensor(z[:, :, :], p_sum[:, 0:NI * 10].rearrange("p (t n) -> p t n", n=10),
                                      bias[:, :].unsqueeze(1).to_broadcast([128, NI, 10]), ALU.add))
            bands = z[:, :, 0:9].rearrange("p t (l k) -> p t l k", k=3)
            ch.link(dve.tensor_reduce(zm[:, :, :], bands, AX.X, ALU.max))
            for t in range(NI):
                last = dve.tensor_tensor(z[:, t, 0:9].rearrange("p (l k) -> p l k", k=3),
                                         z[:, t, 0:9].rearrange("p (l k) -> p l k", k=3),
                                         zm[:, t].unsqueeze(2).to_broadcast([128, 3, 3]), ALU.subtract)
            ch.link(last)
            ch.link(dve.tensor_scalar(z[:, :, 9], z[:, :, 9], -1.0, None, ALU.mult))
            dve.sem_inc(z_ready, 1)
            dve.wait_ge(exp_z, 1)
            dve.tensor_reduce(zs[:, :, 0:3], bands, AX.X, ALU.add)
            ch.link(dve.tensor_scalar(zs[:, :, 3], z[:, :, 9], 1.0, None, ALU.add))
            ch.link(dve.reciprocal(zs[:, :, :], zs[:, :, :]))
            for t in range(NI):
                for lv in range(3):
                    last = dve.tensor_scalar(wt[:, t, 3 * lv:3 * lv + 3], z[:, t, 3 * lv:3 * lv + 3],
                                             zs[:, t, lv:lv + 1], 0.25 ** (lv + 1), ALU.mult, ALU.mult)
            ch.link(last)
            ch.link(dve.tensor_scalar(wt[:, :, 9], zs[:, :, 3], 1 / 64, None, ALU.mult))
            ch.link(dve.tensor_scalar(nwt[:, :, :], wt[:, :, :], -1.0, None, ALU.mult))

            def synthesise(src, lv, t, dst, cols):
                n = 512 >> 2 * lv
                rows = n // cols
                v3 = lambda a: a.rearrange("p (r c) -> p r c", r=rows)
                lo = low[:, 0:2 * n].rearrange("p (r u c) -> p r u c", u=2, c=cols)
                hi = high[:, 0:2 * n].rearrange("p (r u c) -> p r u c", u=2, c=cols)
                w = lambda a, k: a[:, t, 3 * lv + k:3 * lv + k + 1]
                h_, v_, d_ = (v3(detail[lv][:, t, c]) for c in range(3))
                ch.link(dve.tensor_scalar(vv[:, 0:n], detail[lv][:, t, 1], w(wt, 1), None, ALU.mult))
                for u, s in ((0, wt), (1, nwt)):
                    dve.scalar_tensor_tensor(out=lo[:, :, u], in0=h_, scalar=w(s, 0), in1=v3(src), op0=ALU.mult, op1=ALU.add)
                    last = dve.scalar_tensor_tensor(out=hi[:, :, u], in0=d_, scalar=w(s, 2), in1=v3(vv[:, 0:n]), op0=ALU.mult, op1=ALU.add)
                ch.link(last)
                lo2 = low[:, 0:2 * n].rearrange("p (r c) -> p r c", c=cols)
                hi2 = high[:, 0:2 * n].rearrange("p (r c) -> p r c", c=cols)
                dve.tensor_tensor(dst[:, :, 0::2], lo2, hi2, ALU.add)
                ch.link(dve.tensor_tensor(dst[:, :, 1::2], lo2, hi2, ALU.subtract))

            for t in range(NI):
                ch.link(dve.tensor_scalar(coarse[:, t], coarse[:, t], wt[:, t, 9:10], None, ALU.mult))
                synthesise(coarse[:, t], 2, t, back[1][:, :].rearrange("p (r c) -> p r c", r=2), 32)
                synthesise(back[1][:, :], 1, t, back[0][:, :].rearrange("p (r c) -> p r c", r=4), 64)
                if t >= 2:
                    dve.wait_ge(rows_out[t % 2], 16 * 4 * (t // 2))
                synthesise(back[0][:, :], 0, t, out_rows[:, t % 2], 128)
                dve.sem_inc(rows_done, 1)
                if t == 0:
                    dve.wait_ge(lora_full, 1)
                    dve.wait_ge(text_in, 64)
                    for q in range(4):
                        dve.scalar_tensor_tensor(out=text_out[:, q], in0=p_lora[:, q, 0:D], scalar=2.0, in1=text[:, q],
                                                 op0=ALU.mult, op1=ALU.add).then_inc(text_done, 1)


class Heads:

    def __init__(self, nc, sem, sb, pb, name, n_heads, lead, pack, causal, split, use, ring):
        self.nh, self.lead, self.pack, self.causal, self.split, self.use, self.ring = n_heads, lead, pack, causal, split, use, ring
        self.gw = 128 // pack
        self.prob = sb(name + "_prob", [TR, 2, NJ, S], F32)
        self.prob_t = sb(name + "_prob_t", [TR, 2, 2 if split else 1, NJ, S], F32R if split else F32)
        self.neg_max = sb(name + "_neg_max", [TR, 2, NJ], F32)
        self.row_sum = sb(name + "_row_sum", [TR, 2, NJ], F32)
        self.inv_sum = sb(name + "_inv_sum", [TR, 2, NJ], F32)
        self.p_t_all = pb(f"{name}_p_t", [TR, NJ, BANK], F32)
        self.p_t = [self.p_t_all[:, kt] for kt in range(NJ)]
        self.p_o = pb(name + "_p_o", [128, BANK], F32)
        n = n_heads
        self.scored = Tally(sem(name + "_scored"), NJ * n)
        self.max_done = Tally(sem(name + "_max_done"), NJ * n)
        self.exp_done = Tally(sem(name + "_exp_done"), NJ * n)
        self.inv_done = Tally(sem(name + "_inv_done"), n)
        self.scaled = Tally(sem(name + "_scaled"), NJ * n)
        self.turned = Tally(sem(name + "_turned"), n)
        self.na = 1 if split else 2
        self.copied = Tally(sem(name + "_copied"), self.na * n)
        self.copied2 = Tally(sem(name + "_copied2"), n)
        self.weighted = Tally(sem(name + "_weighted"), n)
        self.heads_out = Tally(sem(name + "_heads_out"), n // pack)

    def keys(self, j):
        return TR * (j + 1) if self.causal else S

    def steps(self, b, step):
        for hd in range(self.nh if isinstance(b, int) else self.lead, self.nh + self.lead):
            step(hd)


    def pe_scores(self, pe, b, hd, claim, q, k, mask=None):
        for j in range(NJ):
            u = self.use(hd) + j
            claim(pe, b, u)
            n = self.keys(j)
            bank = self.ring[u % len(self.ring)]
            mm = product(pe, bank[0:TR, 0:n], q(hd, j), k(hd, n), True, mask is None)
            if mask is not None:
                mm = pe.matmul(bank[0:TR, TR * j:n], mask[0], mask[1], start=False, stop=True)
            mm.then_inc(self.scored.sem, 1)

    def pe_turn(self, pe, b, hd, ident):
        wait(pe, self.copied, b, self.na * hd)
        wait(pe, self.copied2, b, hd)
        for j in range(NJ):
            wait(pe, self.scaled, b, NJ * hd + j + 1)
            for kt in range(j + 1 if self.causal else NJ):
                mm = pe.transpose(self.p_t[kt][:, TR * j:TR * j + TR],
                                  self.prob[:, hd % 2, j, TR * kt:TR * kt + TR], ident[0:TR, 0:TR])
        mm.then_inc(self.turned.sem, 1)

    def pe_values(self, pe, b, hd, v):
        if hd % self.pack == 0:
            wait(pe, self.heads_out, b, hd // self.pack)
        at = self.gw * (hd % self.pack)
        for kt in range(NJ):
            n0 = TR * kt if self.causal else 0
            p = tuple(self.prob_t[:, hd % 2, part, kt, n0:S] for part in range(2 if self.split else 1))
            if kt == 0 and not self.split:
                wait(pe, self.copied, b, 2 * hd + 2)
            if kt == (0 if self.split else 2):
                wait(pe, self.copied2, b, hd + 1)
            if self.split:
                mm = matmul3(pe, self.p_o[:, n0:S], v(hd, kt), p, kt == 0 and hd % self.pack == 0,
                             kt == NJ - 1 and hd % self.pack == self.pack - 1)
            else:
                mm = pe.matmul(self.p_o[at:at + self.gw, n0:S], v(hd, kt), p[0], start=kt == 0, stop=kt == NJ - 1)
        mm.then_inc(self.weighted.sem, 1)

    def pe_steps(self, pe, b, claim, q, k, v, ident, mask=None, extra=None, late=None):
        def step(hd):
            self.pe_scores(pe, b, hd + 1, claim, q, k, mask)
            if hd in (extra or {}):
                extra[hd](pe, b)
            self.pe_turn(pe, b, hd, ident)
            if not (isinstance(b, int) and hd == self.nh):
                self.pe_values(pe, b, hd - 1, v)
            if hd in (late or {}):
                late[hd](pe, b)

        self.steps(b, step)


    def act_exps(self, act, b, hd):
        wait(act, self.turned, b, hd - 1)
        for j in range(NJ):
            wait(act, self.max_done, b, NJ * hd + j + 1)
            n = self.keys(j)
            u = self.use(hd) + j
            act.activation(self.prob[:, hd % 2, j, 0:n], self.ring[u % len(self.ring)][0:TR, 0:n], ACT.Exp,
                           bias=self.neg_max[:, hd % 2, j:j + 1], accum_out=self.row_sum[:, hd % 2, j:j + 1])\
               .then_inc(self.exp_done.sem, 1)

    def act_scale(self, act, b, hd):
        wait(act, self.inv_done, b, hd + 1)
        for j in range(NJ):
            wait(act, self.exp_done, b, NJ * hd + j + 1)
            p = self.prob[:, hd % 2, j, 0:self.keys(j)]
            act.activation(p, p, ACT.Copy, scale=self.inv_sum[:, hd % 2, j:j + 1]).then_inc(self.scaled.sem, 1)

    def copies(self, eng, b, hd):
        wait(eng, self.turned, b, hd + 1)
        wait(eng, self.weighted, b, hd - 1)

    def act_copies(self, act, b, hd):
        self.copies(act, b, hd)
        if self.split:
            split_high(act, self.prob_t[:, hd % 2, 0], self.p_t_all[:, :, 0:S]).then_inc(self.copied.sem, 1)
            return
        for kt in range(self.na):
            n0 = TR * kt if self.causal else 0
            act.activation(self.prob_t[:, hd % 2, 0, kt, n0:S], self.p_t[kt][:, n0:S], ACT.Copy).then_inc(self.copied.sem, 1)

    def act_steps(self, act, b, extra=None, late=None):
        def step(hd):
            if self.split:
                self.act_scale(act, b, hd)
            self.act_exps(act, b, hd + 1)
            if hd in (extra or {}):
                extra[hd](act, b)
            self.act_copies(act, b, hd)
            if hd in (late or {}):
                late[hd](act, b)

        self.steps(b, step)


    def dve_max(self, dve, b, hd):
        for j in range(NJ):
            wait(dve, self.scored, b, NJ * hd + j + 1)
            u = self.use(hd) + j
            dve.tensor_reduce(self.neg_max[:, hd % 2, j:j + 1], self.ring[u % len(self.ring)][0:TR, 0:self.keys(j)],
                              AX.X, ALU.max, negate=True).then_inc(self.max_done.sem, 1)

    def dve_inverse(self, dve, b, hd):
        wait(dve, self.exp_done, b, NJ * hd + NJ)
        if self.split:
            wait(dve, self.scaled, b, NJ * (hd - 1))
        dve.reciprocal(self.inv_sum[:, hd % 2], self.row_sum[:, hd % 2]).then_inc(self.inv_done.sem, 1)

    def dve_scale(self, dve, b, hd):
        wait(dve, self.inv_done, b, hd + 1)
        for j in range(NJ):
            p = self.prob[:, hd % 2, j, 0:self.keys(j)]
            dve.tensor_scalar(p, p, self.inv_sum[:, hd % 2, j:j + 1], None, ALU.mult).then_inc(self.scaled.sem, 1)

    def dve_copy(self, dve, b, hd):
        self.copies(dve, b, hd)
        if self.split:
            wait(dve, self.copied, b, hd + 1)
            split_low(dve, self.prob_t[:, hd % 2, 1], self.p_t_all[:, :, 0:S], self.prob_t[:, hd % 2, 0]).then_inc(self.copied2.sem, 1)
            return
        n0 = 2 * TR if self.causal else 0
        dve.tensor_copy(self.prob_t[:, hd % 2, 0, 2, n0:S], self.p_t[2][:, n0:S]).then_inc(self.copied2.sem, 1)

    def dve_out(self, dve, b, hd, out):
        if hd % self.pack == self.pack - 1:
            to, bias = out(hd // self.pack)
            wait(dve, self.weighted, b, hd + 1)
            if bias is None:
                dve.tensor_copy(to, self.p_o[:, 0:S]).then_inc(self.heads_out.sem, 1)
            else:
                dve.tensor_scalar(to, self.p_o[:, 0:S], bias, None, ALU.add).then_inc(self.heads_out.sem, 1)

    def dve_first(self, dve):
        self.dve_max(dve, -1, self.nh)
        self.dve_inverse(dve, -1, self.nh)
        if not self.split:
            self.dve_scale(dve, -1, self.nh)

    def dve_steps(self, dve, b, out, extra=None, late=None):
        def step(hd):
            self.dve_max(dve, b, hd + 1)
            self.dve_inverse(dve, b, hd + 1)
            if not self.split:
                self.dve_scale(dve, b, hd + 1)
            if hd in (extra or {}):
                extra[hd](dve, b)
            self.dve_copy(dve, b, hd)
            if not (isinstance(b, int) and hd == self.nh):
                self.dve_out(dve, b, hd - 1, out)
            if hd in (late or {}):
                late[hd](dve, b)

        self.steps(b, step)


class Ring:

    def __init__(self, banks, freed):
        self.banks, self.freed = banks, freed
        assert len(freed) % len(banks) == 0

    def bank(self, u):
        return self.banks[u % len(self.banks)]

    def claim(self, pe, b, u):
        v = u - len(self.banks)
        t, n = self.freed[v % len(self.freed)]
        wait(pe, t, b, n if v >= 0 else n - t.per)


def join(*steps):
    def all_of_them(eng, b):
        for step in steps:
            step(eng, b)
    return all_of_them


class Norm:

    def __init__(self, sem, sb, name, ahead):
        self.stats = sb(name + "_stats", [TR, NJ, 6], F32)
        self.mv = sb(name + "_mv", [TR, NJ, 2], F32)
        self.stats_done = Tally(sem(name + "_stats_done"), NJ, ahead * NJ)
        self.stats_seen = sem(name + "_stats_seen")
        self.mv_done = Tally(sem(name + "_mv_done"), NJ, ahead * NJ)
        self.power = Power(sem, sb, name, ahead)

    def dve_stats(self, dve, src, at):
        for j in range(NJ):
            dve.bn_stats(self.stats[:, j], src(j)).then_inc(self.stats_done.sem, 1)
        dve.wait_ge(self.stats_done.sem, at(self.stats_done, NJ))
        dve.sem_inc(self.stats_seen, 1)
        for j in range(NJ):
            dve.bn_aggr(self.mv[:, j], self.stats[:, j]).then_inc(self.mv_done.sem, 1)

    def pool_inverse(self, pool, eps, minus_half, at):
        self.power.pool_inverse(pool, self.mv[:, :, 1], self.mv_done, eps, minus_half, at)

    def dve_apply(self, dve, src, dst, at, done):
        dve.wait_ge(self.power.done.sem, at(self.power.done, 1))
        for j in range(NJ):
            dve.tensor_scalar(dst(j), src(j), self.mv[:, j, 0:1], self.power.inv[:, j:j + 1], ALU.subtract, ALU.mult)\
               .then_inc(done.sem, 1)


class Power:

    def __init__(self, sem, sb, name, ahead):
        self.inv = sb(name + "_inv", [TR, NJ], F32)
        self.eps_done = Tally(sem(name + "_eps_done"), 1, ahead)
        self.done = Tally(sem(name + "_inv_done"), 1, ahead)

    def pool_inverse(self, pool, x, x_done, eps, minus_half, at):
        pool.wait_ge(x_done.sem, at(x_done, NJ))
        pool.tensor_tensor(self.inv[:, :], x, eps[:, :], ALU.add).then_inc(self.eps_done.sem, 1)
        pool.wait_ge(self.eps_done.sem, at(self.eps_done, 1))
        pool.tensor_tensor(self.inv[:, :], self.inv[:, :], minus_half[:, :], ALU.pow).then_inc(self.done.sem, 1)


def at_now(b):
    return lambda tally, n: tally.now(b, n)


def at_first(tally, n):
    return n


def at_second(tally, n):
    return tally.per + n


def at_turn(b):
    return lambda tally, n: tally.now(b, n)


def stage_attention(nc, A, keep, sem, sb, pb):
    h, ident = keep["h"], keep["ident"]
    NH, HD = 16, 64
    E = NH * HD
    KE = E // 128
    wq, wk, wv = (sb(n, [128, 2, KD, E], F32R) for n in ("wq", "wk", "wv"))
    wo = sb("wo", [128, KE, D], F32)
    bq = sb("bq", [128, KE], F32)
    bk = sb("bk", [128, KE], F32)
    bv = sb("bv", [128, KE], F32)
    bo = sb("bo", [1, D], F32)
    ones = sb("ones_row", [1, TR], F32)
    minus_half = sb("minus_half", [TR, NJ], F32)
    eps = sb("eps", [TR, NJ], F32)
    xn = sb("xn", [TR, NJ, D], F32)
    x_t = sb("x_t", [128, 2, KD, S], F32R)
    q_t = sb("q_t", [128, 2, 2, 2, S], F32R)
    k_t = sb("k_t", [128, 2, 2, S], F32R)
    v = sb("v", [TR, 2, 2, NJ, 3, HD], F32R)
    o_t = sb("o_t", [128, 2, S], F32)
    raw = sb("raw", [128, 2, E], F32)
    banks = [pb(f"ring{i}", [128, BANK], F32) for i in range(4)]

    LEAD = 2
    steps = range(LEAD, NH + LEAD)
    qk_at = {hd: hd // 2 + 1 for hd in steps if hd % 2 == 0}
    v_at = {hd: hd // 2 + 1 for hd in steps if hd % 2}
    X_AT = NH - 3
    out_at = {hd: hd // 2 - 1 for hd in steps if hd % 2}
    order = []
    for hd in steps:
        order += [("s", hd + 1, j) for j in range(NJ)]
        order += [("q", qk_at[hd]), ("k", qk_at[hd])] if hd in qk_at else []
        order += [("v", v_at[hd])] if hd in v_at else []
        order += [("x", k) for k in range(KD)] if hd == X_AT else []
        order += [("o", out_at[hd], i) for i in range(2)] if hd in out_at else []

    def at_use(*what):
        return order.index(what)

    heads = Heads(nc, sem, sb, pb, "attn", NH, LEAD, 2, False, True, lambda hd: at_use("s", hd, 0), banks)
    q_high, q_low = Tally(sem("q_high"), KE), Tally(sem("q_low"), KE)
    k_high, k_low = Tally(sem("k_high"), KE), Tally(sem("k_low"), KE)
    v_high, v_low = Tally(sem("v_high"), KE), Tally(sem("v_low"), KE)
    x_high, x_low = Tally(sem("x_high"), KD, KD), Tally(sem("x_low"), KD, KD)
    h_done = Tally(sem("h_done"), 2 * KE, 2 * KE)
    empties = {"q": lambda m: (q_low, m + 1), "k": lambda m: (k_low, m + 1), "v": lambda m: (v_low, m + 1),
               "s": lambda hd, j: (heads.exp_done, NJ * hd + j + 1), "o": lambda m, i: (h_done, 2 * m + i + 1),
               "x": lambda k: (x_low, k + 1)}
    freed = [empties[u[0]](*u[1:]) for u in order]
    while len(freed) % len(banks):
        freed.append(freed[-len(banks)])
    ring = Ring(banks, freed)
    qk_full, v_full = Tally(sem("qk_full"), 2 * KE), Tally(sem("v_full"), KE)

    out_done = Tally(sem("out_done"), 2 * KE)
    halves = (slice(0, 2), slice(2, NJ))
    turned_x = Tally(sem("turned_x"), KD, KD)
    xn_done = Tally(sem("xn_done"), NJ, NJ)
    norm = Norm(sem, sb, "ln1", ahead=1)
    h_in = [sem(f"h_in{i}") for i in range(4)]
    zero = sb("zero_rows", [128, 1, D], F32)
    zero_done, xs_zeroed = sem("zero_done"), sem("xs_zeroed")
    w_in, raw_high, raw_low = (sem("attn_" + n) for n in ("w_in", "raw_high", "raw_low"))
    raw_in = [sem(f"attn_raw_in{u}") for u in range(2)]
    q_zeroed, consts, bq_done = sem("q_zeroed"), sem("attn_consts"), sem("bq_done")
    raws = [(name, w, k, scale) for name, w, scale in (("Wq", wq, HD ** -0.5), ("Wk", wk, 1.0), ("Wv", wv, 1.0)) for k in range(KD)]

    def full_v(m, j):
        return ring.bank(at_use("v", m))[0:TR, 2 * HD * j:2 * HD * j + 2 * HD].rearrange("p (i d) -> p i d", i=2)

    with nc.Block() as block:

        @block.sync
        def _(sp):
            h0 = keep["h0"].rearrange("(n p) d -> p n d", p=TR)
            n = NT // 4
            sp.dma_start(h[:, 0:n], h0[:, 0:n]).then_inc(h_in[0], 16)
            blocks = [rows_of(A["L0_attn_" + name])[:, k] for name, w, k, scale in raws]
            for i in range(2):
                sp.dma_start(raw[:, i], blocks[i]).then_inc(raw_in[i], 16)
            for t, name in ((bq, "bq"), (bk, "bk"), (bv, "bv")):
                sp.dma_start(t[:, :], column(A["L0_attn_" + name], 128), allow_slow_non_contiguous=True).then_inc(w_in, 16)
            sp.dma_start(wo[:, :, :], rows_of(A["L0_attn_Wo"])).then_inc(w_in, 16)
            sp.dma_start(bo[:, :], A["L0_attn_bo"].partition_broadcast(1)).then_inc(w_in, 16)
            for i in range(2, len(raws)):
                sp.wait_ge(raw_low, i - 1)
                sp.dma_start(raw[:, i % 2], blocks[i]).then_inc(raw_in[i % 2], 16)
            for i in range(1, 4):
                sp.dma_start(h[:, i * n:(i + 1) * n], h0[:, i * n:(i + 1) * n]).then_inc(h_in[i], 16)
            sp.wait_ge(zero_done, 1)
            xs = keep["xs"].rearrange("(n p) d -> n p d", p=128)
            for i in range(0, xs.shape[0], 5):
                sp.dma_start(xs[i:i + 5].rearrange("n p d -> p n d"), zero[:, :, :].to_broadcast([128, 5, D])).then_inc(xs_zeroed, 16)
            sp.wait_ge(xs_zeroed, 16 * (xs.shape[0] // 5))

        @block.gpsimd
        def _(pool):
            pool.memset(minus_half[:, :], -0.5).then_inc(consts, 1)
            pool.memset(zero[:, :, :], 0.0).then_inc(zero_done, 1)
            pool.memset(ones[:, :], 1.0).then_inc(consts, 1)
            pool.memset(h[:, NT:NT + NJ], 0.0).then_inc(consts, 1)
            pool.memset(eps[:, :], LN_EPS).then_inc(consts, 1)
            pool.wait_ge(consts, 4)
            norm.pool_inverse(pool, eps, minus_half, at_first)
            with pool.Fori(0, B) as b:
                norm.pool_inverse(pool, eps, minus_half, at_turn(b))

        @block.scalar
        def _(act):
            for i, (name, w, k, scale) in enumerate(raws):
                act.wait_ge(raw_in[i % 2], 16 * (i // 2 + 1))
                act.activation(w[:, 0, k], raw[:, i % 2], ACT.Copy, scale=scale).then_inc(raw_high, 1)
            act.wait_ge(w_in, 16 * 5)
            act.activation(bq[:, :], bq[:, :], ACT.Copy, scale=HD ** -0.5).then_inc(bq_done, 1)
            act.wait_ge(bq_done, 1)
            act.wait_ge(q_zeroed, 1)

            def x_parts(at):
                for k in range(KD):
                    act.wait_ge(turned_x.sem, at(turned_x, k + 1))
                    split_high(act, x_t[:, 0, k], ring.bank(at_use("x", k))[:, 0:S]).then_inc(x_high.sem, 1)

            def qk_parts(m):
                def parts(act, b):
                    wait(act, qk_full, b, 2 * m + 1)
                    for i in range(2):
                        r = slice(HD * i, HD * i + HD)
                        ins = act.activation(q_t[r, m % 2, i, 0], ring.bank(at_use("q", m))[r, 0:S], ACT.Identity, bias=bq[r, m % KE:m % KE + 1])
                    ins.then_inc(q_high.sem, 1)
                    wait(act, qk_full, b, 2 * m + 2)
                    act.activation(k_t[:, m % 2, 0], ring.bank(at_use("k", m))[:, 0:S], ACT.Identity, bias=bk[:, m % KE:m % KE + 1])\
                       .then_inc(k_high.sem, 1)
                return parts

            def v_parts(m):
                def parts(act, b):
                    wait(act, v_full, b, m + 1)
                    wait(act, heads.weighted, b, 2 * m - 2)
                    for j in range(NJ):
                        ins = split_high(act, v[:, m % 2, 0, j, 0::2], full_v(m, j))
                    ins.then_inc(v_high.sem, 1)
                return parts

            x_parts(at_first)
            qk_parts(KE)(act, -1)
            v_parts(KE)(act, -1)
            heads.act_exps(act, -1, NH)
            extra = {hd: qk_parts(m) for hd, m in qk_at.items()} | {hd: v_parts(m) for hd, m in v_at.items()}
            heads.act_steps(act, -1, extra)
            extra[X_AT] = join(extra[X_AT], lambda act, b: x_parts(at_turn(b)))
            with act.Fori(0, B) as b:
                heads.act_steps(act, b, extra)

        @block.tensor
        def _(pe):
            parts = lambda t, *at: tuple(t[(slice(None), p, *at)] for p in range(2))

            def turn_x(at, claim):
                pe.wait_ge(xn_done.sem, at(xn_done, NJ))
                for k in range(KD):
                    if claim:
                        claim(at_use("x", k))
                    for j in range(NJ):
                        mm = pe.transpose(ring.bank(at_use("x", k))[:, TR * j:TR * j + TR], xn[:, j, 128 * k:128 * k + 128],
                                          ident[0:TR, 0:TR])
                    mm.then_inc(turned_x.sem, 1)

            def project_qk(m):
                def both(pe, b):
                    if m == KE:
                        wait(pe, x_low, b, KD)
                    for n, w in (("q", wq), ("k", wk)):
                        u = at_use(n, m)
                        ring.claim(pe, b, u)
                        for k in range(KD):
                            mm = matmul3(pe, ring.bank(u)[:, 0:S], parts(w, k, slice(128 * (m % KE), 128 * (m % KE) + 128)), parts(x_t, k),
                                         k == 0, k == KD - 1)
                        mm.then_inc(qk_full.sem, 1)
                return both

            def project_v(m):
                def values(pe, b):
                    u = at_use("v", m)
                    ring.claim(pe, b, u)
                    cols = slice(128 * (m % KE), 128 * (m % KE) + 128)
                    for j in range(NJ):
                        for k in range(KD):
                            mm = matmul3(pe, ring.bank(u)[0:TR, 128 * j:128 * j + 128], parts(x_t, k, slice(TR * j, TR * j + TR)),
                                         parts(wv, k, cols), k == 0, k == KD - 1)
                    mm.then_inc(v_full.sem, 1)
                return values

            turn_x(at_first, None)
            pe.wait_ge(consts, 4)
            pe.wait_ge(w_in, 16 * 5)
            pe.wait_ge(raw_low, len(raws))
            pe.wait_ge(q_zeroed, 5)
            def q(b):
                def parts(hd, j):
                    if j == 0 and hd % 2 == 0:
                        wait(pe, q_low, b, hd // 2 + 1)
                        wait(pe, k_low, b, hd // 2 + 1)
                    return tuple(q_t[:, hd // 2 % 2, hd % 2, p, TR * j:TR * j + TR] for p in range(2))
                return parts

            def values(b):
                def parts(hd, kt):
                    if hd % 2 == 0 and kt == 0:
                        wait(pe, v_low, b, hd // 2 + 1)
                    return tuple(v[:, hd // 2 % 2, p, kt, hd % 2:hd % 2 + 2] for p in range(2))
                return parts

            def output(m):
                def part_of_result(pe, b):
                    wait(pe, heads.heads_out, b, m + 1)
                    for i, tiles in enumerate(halves):
                        u = at_use("o", m, i)
                        ring.claim(pe, b, u)
                        for n, j in enumerate(range(NJ)[tiles]):
                            to = ring.bank(u)[0:TR, D * n:D * n + D]
                            mm = pe.matmul(to, o_t[:, m % 2, TR * j:TR * j + TR], wo[:, m % KE], start=True, stop=m != KE - 1)
                            if m == KE - 1:
                                mm = pe.matmul(to, ones[:, :], bo[:, :], start=False, stop=True)
                        mm.then_inc(out_done.sem, 1)
                return part_of_result

            keys = lambda hd, n: tuple(k_t[:, hd // 2 % 2, p, 0:n] for p in range(2))
            project_qk(KE)(pe, -1)
            wait(pe, q_low, -1, KE + 1)
            wait(pe, k_low, -1, KE + 1)
            project_v(KE)(pe, -1)
            wait(pe, v_low, -1, KE + 1)
            heads.pe_scores(pe, -1, NH, ring.claim, q(-1), keys)
            extra = {hd: project_qk(m) for hd, m in qk_at.items()} | {hd: project_v(m) for hd, m in v_at.items()}
            heads.pe_steps(pe, -1, ring.claim, q(-1), keys, values(-1), ident, None, extra)
            wait(pe, heads.exp_done, -1, NJ * (NH + LEAD + 1))
            for t in (q_low, k_low, v_low):
                wait(pe, t, -1, KE + LEAD // 2 + 1)
            extra[X_AT] = join(extra[X_AT], lambda pe, b: turn_x(at_turn(b), lambda u: ring.claim(pe, b, u)))
            with pe.Fori(0, B) as b:
                heads.pe_steps(pe, b, ring.claim, q(b), keys, values(b), ident, None, extra,
                               {hd: output(m) for hd, m in out_at.items()})
            pe.matmul(heads.p_o[:, 0:S], wq[:, 0, 0, 0:128], x_t[:, 0, 0], start=False, stop=True)

        @block.vector
        def _(dve):
            dve.wait_ge(h_in[0], 16)
            dve.sem_inc(h_done.sem, h_done.ahead)

            def prepare(tile, at):
                norm.dve_stats(dve, tile, at)
                norm.dve_apply(dve, tile, lambda j: xn[:, j:j + 1], at, xn_done)

            def x_parts(at):
                for k in range(KD):
                    dve.wait_ge(x_high.sem, at(x_high, k + 1))
                    split_low(dve, x_t[:, 1, k], ring.bank(at_use("x", k))[:, 0:S], x_t[:, 0, k]).then_inc(x_low.sem, 1)

            def biased_low(to, full, bias, high):
                return dve.scalar_tensor_tensor(out=to, in0=full, scalar=bias, in1=high.bitcast(F32), op0=ALU.add, op1=ALU.subtract)

            def qk_parts(m):
                def parts(dve, b):
                    wait(dve, q_high, b, m + 1)
                    for i in range(2):
                        r = slice(HD * i, HD * i + HD)
                        ins = biased_low(q_t[r, m % 2, i, 1], ring.bank(at_use("q", m))[r, 0:S], bq[r, m % KE:m % KE + 1], q_t[r, m % 2, i, 0])
                    ins.then_inc(q_low.sem, 1)
                    wait(dve, k_high, b, m + 1)
                    biased_low(k_t[:, m % 2, 1], ring.bank(at_use("k", m))[:, 0:S], bk[:, m % KE:m % KE + 1], k_t[:, m % 2, 0])\
                        .then_inc(k_low.sem, 1)
                return parts

            prepare(lambda j: h[:, j:j + 1], at_first)
            for i, (name, w, k, scale) in enumerate(raws):
                dve.wait_ge(raw_high, i + 1)
                dve.scalar_tensor_tensor(out=w[:, 1, k], in0=raw[:, i % 2], scalar=scale, in1=w[:, 0, k].bitcast(F32),
                                         op0=ALU.mult, op1=ALU.subtract).then_inc(raw_low, 1)
            dve.wait_ge(zero_done, 1)
            n = 2 * 2 * 2 * S // D
            dve.tensor_copy(q_t[:, :, :, :, :].rearrange("p a b c n -> p (a b c n)").rearrange("p (n d) -> p n d", n=n),
                            zero[:, :, :].to_broadcast([128, n, D])).then_inc(q_zeroed, 1)
            for parity in range(2):
                for part in range(2):
                    dve.tensor_copy(v[:, parity, part, :, 1], zero[0:TR, :, 0:HD].to_broadcast([TR, NJ, HD])).then_inc(q_zeroed, 1)
            x_parts(at_first)
            for i in range(1, 4):
                dve.wait_ge(h_in[i], 16)
            dve.wait_ge(consts, 4)
            dve.wait_ge(w_in, 16 * 5)
            def v_parts(m):
                def parts(dve, b):
                    wait(dve, v_high, b, m + 1)
                    for j in range(NJ):
                        ins = split_low(dve, v[:, m % 2, 1, j, 0::2], full_v(m, j), v[:, m % 2, 0, j, 0::2])
                    ins.then_inc(v_low.sem, 1)
                return parts

            def add(m):
                def parts(dve, b):
                    wait(dve, h_done, b, 2 * m)
                    for i, tiles in enumerate(halves):
                        n = tiles.stop - tiles.start
                        wait(dve, out_done, b, 2 * m + i + 1)
                        to = h[:, bass.ds(b * NJ + tiles.start, n)]
                        part = ring.bank(at_use("o", m, i))[0:TR, 0:D * n].rearrange("p (j d) -> p j d", j=n)
                        dve.tensor_tensor(to, part, to, ALU.add).then_inc(h_done.sem, 1)
                return parts

            next_tile = lambda b: lambda j: h[:, slot(b + 1, j)]
            out = lambda g: (o_t[:, g % 2], bv[:, g % KE:g % KE + 1])
            qk_parts(KE)(dve, -1)
            v_parts(KE)(dve, -1)
            heads.dve_first(dve)
            extra = {hd: qk_parts(m) for hd, m in qk_at.items()} | {hd: v_parts(m) for hd, m in v_at.items()}
            heads.dve_steps(dve, -1, out, extra)
            extra[X_AT] = join(extra[X_AT], lambda dve, b: x_parts(at_turn(b)))
            late = {hd: add(m) for hd, m in out_at.items()}
            late[6] = lambda dve, b: norm.dve_stats(dve, next_tile(b), at_turn(b))
            late[8] = lambda dve, b: norm.dve_apply(dve, next_tile(b), lambda j: xn[:, j:j + 1], at_turn(b), xn_done)
            with dve.Fori(0, B) as b:
                heads.dve_steps(dve, b, out, extra, late)


def stage_latent(nc, A, keep, sem, sb, pb):
    h, rows, ident, logits = keep["h"], keep["rows"], keep["ident"], keep["logits0"]
    NH, HD, HP = 16, 16, 32
    KE = NH * HP // 128
    NE = 8
    wq0 = sb("lwq0", [128, KD, D], F32)
    wuk0 = sb("lwuk0", [128, D], F32)
    wuv0 = sb("lwuv0", [128, D], F32)
    wq = sb("lwq", [128, KD, NH, HP], F32)
    wuk = sb("lwuk", [128, NH, HP], F32)
    wuv = sb("lwuv", [128, NH, HP], F32)
    wo = sb("lwo", [128, KE, D], F32)
    wdkv = sb("lwdkv", [128, KD, 128], F32)
    gate = sb("gate0", [128, KD, NE], F32)
    g1 = sb("g1", [128, KD], F32)
    g2 = sb("g2", [TR, D], F32)
    mask = sb("mask", [TR, TR], BF16)
    ident_b = sb("ident_b", [TR, TR], BF16)
    minus_half = sb("minus_half3", [TR, NJ], F32)
    ln_eps = sb("ln_eps3", [TR, NJ], F32)
    rms_eps = sb("rms_eps3", [TR, NJ], F32)
    zero = sb("zero", [TR, NJ, D], F32)
    squares = sb("squares", [TR, NJ, D], F32)
    mean_sq = sb("mean_sq", [TR, NJ], F32)
    mean_sq2 = sb("mean_sq2", [TR, NJ], F32)
    xr = sb("xr", [TR, NJ, D], F32)
    t_rows = sb("t_rows", [TR, NJ, D], F32)
    r_t = sb("r_t", [128, KD, S], F32)
    t_t = sb("t_t", [128, KD, S], F32)
    c_t = sb("c_t", [128, S], F32)
    q_t = sb("lq_t", [128, NH, S], F32)
    k_t = sb("lk_t", [128, KE, S], F32)
    v = sb("lv", [TR, NJ, NH * HP], F32)
    o_t = sb("lo_t", [128, KE, S], F32)
    banks = [pb(f"lring{i}", [128, BANK], F32) for i in range(4)]

    LEAD = 6
    R_AT, C_AT = 11, 12
    q_at = {13: KE, 15: KE + 1, 16: KE + 2, 17: KE + 3}
    k_at = {14: KE, 15: KE + 1, 16: KE + 2, 17: KE + 3}
    v_at = {14: KE, 15: KE + 1, 16: KE + 2, 18: KE + 3}
    O_AT, T_AT, G_AT = NH + 1, NH + 3, NH + 4
    order = []
    for hd in range(LEAD, NH + LEAD):
        order += [("s", hd + 1, j) for j in range(NJ)]
        for n, at in (("q", q_at), ("k", k_at), ("v", v_at)):
            order += [(n, at[hd])] if hd in at else []
        order += [("r", k) for k in range(KD)] if hd == R_AT else []
        order += [("c", 0)] if hd == C_AT else []
        order += [("o", j) for j in range(NJ)] if hd == O_AT else []
        order += [("t", k) for k in range(KD)] if hd == T_AT else []
        order += [("g", 0)] if hd == G_AT else []

    def at_use(*what):
        return order.index(what)

    heads = Heads(nc, sem, sb, pb, "lat", NH, LEAD, 4, True, False, lambda hd: at_use("s", hd, 0), banks)
    c_done, q_done, k_done, v_done = (Tally(sem("l" + n), per) for n, per in
                                      (("c_done", 1), ("q_done", KE), ("k_done", KE), ("v_done", KE)))
    x1_done = Tally(sem("x1_done"), NJ, NJ)
    t_t_done = Tally(sem("t_t_done"), KD, KD)
    logits_done = Tally(sem("logits_done"), 1, 1)
    r_t_done = Tally(sem("r_t_done"), KD, KD)
    empties = {"q": lambda m: (q_done, m + 1), "k": lambda m: (k_done, m + 1), "v": lambda m: (v_done, m + 1),
               "s": lambda hd, j: (heads.exp_done, NJ * hd + j + 1), "o": lambda j: (x1_done, j + 1),
               "t": lambda k: (t_t_done, k + 1), "g": lambda _: (logits_done, 1), "c": lambda _: (c_done, 2),
               "r": lambda k: (r_t_done, k + 1)}
    freed = [empties[u[0]](*u[1:]) for u in order]
    while len(freed) % len(banks):
        freed.append(freed[-len(banks)])
    ring = Ring(banks, freed)
    c_full, q_full, k_full, v_full = (Tally(sem("l" + n), per) for n, per in
                                      (("c_full", 1), ("q_full", KE), ("k_full", KE), ("v_full", KE)))
    out_full = Tally(sem("out_full"), NJ)
    turned_t = Tally(sem("turned_t"), KD)
    turned_r = Tally(sem("turned_r"), KD, KD)
    gated = Tally(sem("gated"), 1)
    xn_done = Tally(sem("lxn_done"), NJ, NJ)
    sq_done = Tally(sem("sq_done"), NJ, NJ)
    sq2_done = Tally(sem("sq2_done"), NJ)
    xr_done = Tally(sem("xr_done"), NJ, NJ)
    t_done = Tally(sem("t_done"), NJ)
    h_done = Tally(sem("lh_done"), 1)
    rows_done = Tally(sem("lrows_done"), 1)
    norm = Norm(sem, sb, "ln2", ahead=1)
    rms1 = Power(sem, sb, "rms1", ahead=1)
    rms2 = Power(sem, sb, "rms2", ahead=0)
    w_in, consts, padded = sem("lat_w_in"), sem("lat_consts"), sem("padded")
    weights_padded, pool_seen = sem("weights_padded"), sem("pool_seen")

    with nc.Block() as block:

        @block.sync
        def _(sp):
            sp.dma_start(wq0[:, :, :], rows_of(A["L0_ffn_Wq"])).then_inc(w_in, 16)
            sp.dma_start(wdkv[:, :, :], rows_of(A["L0_ffn_Wdkv"])).then_inc(w_in, 16)
            sp.dma_start(wuk0[:, :], A["L0_ffn_Wuk"]).then_inc(w_in, 16)
            sp.dma_start(wuv0[:, :], A["L0_ffn_Wuv"]).then_inc(w_in, 16)
            sp.dma_start(gate[:, :, :], rows_of(A["L0_ffn_gate_w"])).then_inc(w_in, 16)
            sp.dma_start(g1[:, :], column(A["L0_ffn_g1"], 128), allow_slow_non_contiguous=True).then_inc(w_in, 16)
            sp.dma_start(g2[:, :], A["L0_ffn_g2"].partition_broadcast(TR)).then_inc(w_in, 16)
            sp.wait_ge(padded, 1)
            wo_rows = A["L0_ffn_Wo"].rearrange("(g i p) d -> i p g d", i=128 // HP, p=HD)
            for i in range(128 // HP):
                sp.dma_start(wo[HP * i:HP * i + HD], wo_rows[i]).then_inc(w_in, 16)

        @block.gpsimd
        def _(pool):
            pool.memset(wo[:, :, :], 0.0).then_inc(padded, 1)
            for t, x in ((minus_half, -0.5), (ln_eps, LN_EPS), (rms_eps, RMS_EPS), (mask, 0.0), (ident_b, 0.0)):
                pool.memset(t[:, :], x).then_inc(consts, 1)
            pool.wait_ge(weights_padded, 1)
            pool.wait_ge(consts, 5)
            pool.affine_select(out=mask[:, :], in_=mask[:, :], compare_op=ALU.is_ge, fill=NEG, base=0,
                               pattern=[[-1, TR]], channel_multiplier=1).then_inc(consts, 1)
            pool.affine_select(out=ident_b[:, :], in_=ident_b[:, :], compare_op=ALU.not_equal, fill=1.0, base=0,
                               pattern=[[-1, TR]], channel_multiplier=1).then_inc(consts, 1)

            def prepare(at):
                norm.pool_inverse(pool, ln_eps, minus_half, at)
                rms1.pool_inverse(pool, mean_sq[:, :], sq_done, rms_eps, minus_half, at)

            prepare(at_first)
            with pool.Fori(0, B) as b:
                prepare(at_turn(b))
                rms2.pool_inverse(pool, mean_sq2[:, :], sq2_done, rms_eps, minus_half, at_now(b))
                pool.wait_ge(x1_done.sem, x1_done.now(b, NJ))
                pool.sem_inc(pool_seen, 1)
                pool.tensor_tensor(h[:, slot(b)], h[:, slot(b)], rows[:, slot(b)], ALU.add).then_inc(h_done.sem, 1)
                pool.wait_ge(h_done.sem, h_done.now(b, 1))
                pool.wait_ge(t_done.sem, t_done.now(b, NJ))
                pool.sem_inc(pool_seen, 1)
                pool.tensor_tensor(rows[:, slot(b)], t_rows[:, :, :], zero[:, :, :], ALU.add).then_inc(rows_done.sem, 1)

        @block.scalar
        def _(act):
            act.sem_inc(t_t_done.sem, t_t_done.ahead)

            def mean_squares(src, to, at, src_done, done):
                for j in range(NJ):
                    act.wait_ge(src_done.sem, at(src_done, j + 1))
                    act.activation(squares[:, j:j + 1], src(j), ACT.Square, scale=D ** -0.5,
                                   accum_out=to[:, j:j + 1]).then_inc(done.sem, 1)

            def copies(n, dst, full, done, at, scale=None):
                for k in range(KD):
                    act.wait_ge(full.sem, at(full, k + 1))
                    src = ring.bank(at_use(n, k))[:, 0:S]
                    if scale is None:
                        act.activation(dst[:, k], src, ACT.Copy).then_inc(done.sem, 1)
                    else:
                        act.activation(dst[:, k], src, ACT.Identity, scale=scale[:, k:k + 1]).then_inc(done.sem, 1)

            def q_copies(m):
                def copy(act, b):
                    wait(act, q_full, b, m + 1)
                    for i in range(4):
                        r = slice(HP * i, HP * i + HP)
                        ins = act.activation(q_t[r, 4 * (m % KE) + i], ring.bank(at_use("q", m))[r, 0:S], ACT.Copy, scale=HD ** -0.5)
                    ins.then_inc(q_done.sem, 1)
                return copy

            mean_squares(lambda j: rows[:, j:j + 1], mean_sq, at_first, xn_done, sq_done)
            act.wait_ge(w_in, 16 * 11)
            copies("r", r_t, turned_r, r_t_done, at_first, g1)
            act.wait_ge(weights_padded, 9)
            for m in range(KE, 2 * KE):
                q_copies(m)(act, -1)
            heads.act_exps(act, -1, NH)
            heads.act_steps(act, -1)
            extra = {hd: q_copies(m) for hd, m in q_at.items()}
            late = {9: lambda act, b: mean_squares(lambda j: rows[:, slot(b + 1, j)], mean_sq, at_turn(b), xn_done, sq_done),
                    R_AT: lambda act, b: copies("r", r_t, turned_r, r_t_done, at_turn(b), g1),
                    O_AT + 1: lambda act, b: mean_squares(lambda j: rows[:, slot(b, j)], mean_sq2, at_turn(b), x1_done, sq2_done),
                    T_AT: lambda act, b: copies("t", t_t, turned_t, t_t_done, at_now(b))}
            with act.Fori(0, B) as b:
                heads.act_steps(act, b, extra, late)

        @block.tensor
        def _(pe):

            def turn(src, src_done, full, n, at, b=-1):
                pe.wait_ge(src_done.sem, at(src_done, NJ))
                for k in range(KD):
                    u = at_use(n, k)
                    if not isinstance(b, int):
                        ring.claim(pe, b, u)
                    for j in range(NJ):
                        mm = pe.transpose(ring.bank(u)[:, TR * j:TR * j + TR], src[:, j, 128 * k:128 * k + 128],
                                          ident[0:TR, 0:TR])
                    mm.then_inc(full.sem, 1)

            def claim(pe, b, u):
                if not isinstance(b, int):
                    ring.claim(pe, b, u)
                elif order[u][0] == "s":
                    wait(pe, heads.exp_done, b, NJ * order[u][1])

            def project_c(pe, b):
                wait(pe, r_t_done, b, KD)
                u = at_use("c", 0)
                claim(pe, b, u)
                for k in range(KD):
                    mm = pe.matmul(ring.bank(u)[:, 0:S], wdkv[:, k], r_t[:, k], start=k == 0, stop=k == KD - 1)
                mm.then_inc(c_full.sem, 1)

            def project_q(m):
                def project(pe, b):
                    u = at_use("q", m)
                    claim(pe, b, u)
                    m4 = 4 * (m % KE)
                    for k in range(KD):
                        mm = pe.matmul(ring.bank(u)[:, 0:S], wq[:, k, m4:m4 + 4], r_t[:, k], start=k == 0, stop=k == KD - 1)
                    mm.then_inc(q_full.sem, 1)
                return project

            def project_k(m):
                def project(pe, b):
                    wait(pe, c_done, b, 2)
                    u = at_use("k", m)
                    claim(pe, b, u)
                    m4 = 4 * (m % KE)
                    pe.matmul(ring.bank(u)[:, 0:S], wuk[:, m4:m4 + 4], c_t[:, :], start=True, stop=True).then_inc(k_full.sem, 1)
                return project

            def project_v(m):
                def project(pe, b):
                    u = at_use("v", m)
                    claim(pe, b, u)
                    m4 = 4 * (m % KE)
                    for j in range(NJ):
                        mm = pe.matmul(ring.bank(u)[0:TR, 128 * j:128 * j + 128], c_t[:, TR * j:TR * j + TR], wuv[:, m4:m4 + 4],
                                       start=True, stop=True)
                    mm.then_inc(v_full.sem, 1)
                return project

            def result(pe, b):
                wait(pe, heads.heads_out, b, KE)
                for j in range(NJ):
                    u = at_use("o", j)
                    ring.claim(pe, b, u)
                    for k in range(KE):
                        mm = pe.matmul(ring.bank(u)[0:TR, 0:D], o_t[:, k, TR * j:TR * j + TR], wo[:, k], start=k == 0, stop=k == KE - 1)
                    mm.then_inc(out_full.sem, 1)

            def router(pe, b):
                pe.wait_ge(t_t_done.sem, t_t_done.now(b, KD))
                u = at_use("g", 0)
                ring.claim(pe, b, u)
                for j in range(NJ):
                    for k in range(KD):
                        mm = pe.matmul(ring.bank(u)[0:TR, NE * j:NE * j + NE], t_t[:, k, TR * j:TR * j + TR], gate[:, k],
                                       start=k == 0, stop=k == KD - 1)
                mm.then_inc(gated.sem, 1)

            def q(b):
                def part(hd, j):
                    if j == 0 and hd % 4 == 0:
                        wait(pe, q_done, b, hd // 4 + 1)
                        wait(pe, k_done, b, hd // 4 + 1)
                    return q_t[:, hd % NH, TR * j:TR * j + TR]
                return part

            def values(b):
                def part(hd, kt):
                    if hd % 4 == 0 and kt == 0:
                        wait(pe, v_done, b, hd // 4 + 1)
                    return v[:, kt, HP * (hd % NH):HP * (hd % NH) + HP]
                return part

            keys = lambda hd, n: k_t[:, hd % NH // 4, 0:n]
            masks = (ident_b[:, :], mask[:, :])
            turn(xr, xr_done, turned_r, "r", at_first)
            pe.wait_ge(consts, 7)
            pe.wait_ge(weights_padded, 8)
            pe.wait_ge(w_in, 16 * 11)
            project_c(pe, -1)
            wait(pe, c_done, -1, 2)
            for m in range(KE, 2 * KE):
                for project, done in ((project_q, q_done), (project_k, k_done), (project_v, v_done)):
                    project(m)(pe, -1)
                    wait(pe, done, -1, m + 1)
            heads.pe_scores(pe, -1, NH, claim, q(-1), keys, masks)
            heads.pe_steps(pe, -1, claim, q(-1), keys, values(-1), ident, masks)
            wait(pe, heads.exp_done, -1, NJ * (NH + LEAD + 1))
            extra = {}
            for hd in range(LEAD, NH + LEAD):
                extra[hd] = join(*[project(at[hd]) for project, at in ((project_q, q_at), (project_k, k_at), (project_v, v_at)) if hd in at])
            late = {R_AT: lambda pe, b: turn(xr, xr_done, turned_r, "r", at_turn(b), b), C_AT: project_c, O_AT: result,
                    T_AT: lambda pe, b: turn(t_rows, t_done, turned_t, "t", at_now(b), b), G_AT: router}
            with pe.Fori(0, B) as b:
                heads.pe_steps(pe, b, ring.claim, q(b), keys, values(b), ident, masks, extra, late)

        @block.vector
        def _(dve):
            dve.sem_inc(x1_done.sem, x1_done.ahead)
            dve.sem_inc(logits_done.sem, logits_done.ahead)

            def prepare(tile, row, at):
                norm.dve_stats(dve, tile, at)
                norm.dve_apply(dve, tile, row, at, xn_done)

            def prepare2(row, at):
                dve.wait_ge(rms1.done.sem, at(rms1.done, 1))
                for j in range(NJ):
                    dve.tensor_scalar(xr[:, j:j + 1], row(j), rms1.inv[:, j:j + 1], None, ALU.mult).then_inc(xr_done.sem, 1)

            dve.memset(zero[:, :, :], 0.0).then_inc(weights_padded, 1)
            dve.memset(wq[:, :, :, :], 0.0).then_inc(weights_padded, 1)
            dve.memset(wuk[:, :, :], 0.0).then_inc(weights_padded, 1)
            dve.memset(wuv[:, :, :], 0.0).then_inc(weights_padded, 1)
            prepare(lambda j: h[:, j:j + 1], lambda j: rows[:, j:j + 1], at_first)
            prepare2(lambda j: rows[:, j:j + 1], at_first)
            dve.wait_ge(w_in, 16 * 11)
            dve.wait_ge(weights_padded, 4)
            for dst, src in ((wq[:, 0], wq0[:, 0]), (wq[:, 1], wq0[:, 1]), (wuk[:, :, :], wuk0[:, :]), (wuv[:, :, :], wuv0[:, :])):
                dve.tensor_copy(dst[:, :, 0:HD], src.rearrange("p (n e) -> p n e", e=HD)).then_inc(weights_padded, 1)
            dve.memset(q_t[:, :, :], 0.0).then_inc(weights_padded, 1)

            def c_copy(dve, b):
                wait(dve, c_full, b, 2)
                dve.tensor_copy(c_t[:, :], ring.bank(at_use("c", 0))[:, 0:S]).then_inc(c_done.sem, 1)

            def k_copy(m):
                def copy(dve, b):
                    wait(dve, k_full, b, m + 1)
                    dve.tensor_copy(k_t[:, m % KE], ring.bank(at_use("k", m))[:, 0:S]).then_inc(k_done.sem, 1)
                return copy

            def v_copy(m):
                def copy(dve, b):
                    wait(dve, v_full, b, m + 1)
                    dve.tensor_copy(v[:, :, 128 * (m % KE):128 * (m % KE) + 128],
                                    ring.bank(at_use("v", m))[0:TR, 0:NJ * 128].rearrange("p (j n) -> p j n", j=NJ))\
                       .then_inc(v_done.sem, 1)
                return copy

            def add(dve, b):
                for j in range(NJ):
                    dve.wait_ge(out_full.sem, out_full.now(b, j + 1))
                    to = rows[:, slot(b, j)]
                    dve.tensor_tensor(to, ring.bank(at_use("o", j))[0:TR, 0:D].unsqueeze(1), to, ALU.add).then_inc(x1_done.sem, 1)

            def routed_rows(dve, b):
                dve.wait_ge(rms2.done.sem, rms2.done.now(b, 1))
                for j in range(NJ):
                    dve.scalar_tensor_tensor(out=t_rows[:, j:j + 1], in0=rows[:, slot(b, j)], scalar=rms2.inv[:, j:j + 1],
                                             in1=g2[:, :].unsqueeze(1), op0=ALU.mult, op1=ALU.mult).then_inc(t_done.sem, 1)

            def logits_copy(dve, b):
                dve.wait_ge(gated.sem, gated.now(b, 1))
                dve.tensor_copy(logits[:, slot(b)], ring.bank(at_use("g", 0))[0:TR, 0:NJ * NE].rearrange("p (j e) -> p j e", e=NE))\
                   .then_inc(logits_done.sem, 1)

            next_tile = lambda b: lambda j: h[:, slot(b + 1, j)]
            next_row = lambda b: lambda j: rows[:, slot(b + 1, j)]
            out = lambda g: (o_t[:, g % KE], None)
            c_copy(dve, -1)
            for m in range(KE, 2 * KE):
                k_copy(m)(dve, -1)
                v_copy(m)(dve, -1)
            heads.dve_first(dve)
            heads.dve_steps(dve, -1, out)
            extra = {}
            for hd in range(LEAD, NH + LEAD):
                extra[hd] = join(*[copy(at[hd]) for copy, at in ((k_copy, k_at), (v_copy, v_at)) if hd in at])
            extra[C_AT + 1] = c_copy
            late = {7: lambda dve, b: norm.dve_stats(dve, next_tile(b), at_turn(b)),
                    8: lambda dve, b: norm.dve_apply(dve, next_tile(b), next_row(b), at_turn(b), xn_done),
                    10: lambda dve, b: prepare2(next_row(b), at_turn(b)),
                    O_AT: add, T_AT: routed_rows, G_AT: logits_copy}
            with dve.Fori(0, B) as b:
                heads.dve_steps(dve, b, out, extra, late)


class Routing:

    def __init__(self, sem, sb, pb, name, n_experts, slots):
        self.ne = n_experts
        shape = [TR, NT, n_experts]
        self.work = sb(name + "_work", shape, F32)
        self.pick = sb(name + "_pick", shape, F32)
        self.first = sb(name + "_first", shape, F32)
        self.second = sb(name + "_second", shape, F32)
        self.top = sb(name + "_top", [TR, 2, NT], F32)
        self.best = sb(name + "_best", [TR, NT], F32)
        self.mask = sb(name + "_mask", shape, F32)
        self.place = sb(name + "_place", shape, F32)
        self.total = sb(name + "_total", [128, NT, n_experts], F32)
        self.until = sb(name + "_until", [128, NT, n_experts], F32)
        self.rank = sb(name + "_rank", [TR, n_experts], F32)
        self.tri = sb(name + "_tri", [TR, TR], F32)
        self.ones = sb(name + "_ones", [128, 128], F32)
        self.slot_f = sb(name + "_slot_f", [TR, 2, NT], F32)
        self.slot = slots
        half = NT // 2 if NT * n_experts > BANK else NT
        self.halves = [slice(a, a + half) for a in range(0, NT, half)]
        self.p_before = [pb(f"{name}_p_before{i}", [128, BANK], F32) for i in range(len(self.halves))]
        self.p_total = [pb(f"{name}_p_total{i}", [128, BANK], F32) for i in range(len(self.halves))]
        self.consts = sem(name + "_consts")
        self.mask_ready, self.counted = sem(name + "_mask_ready"), sem(name + "_counted")
        self.n_counts = 0

    def pool_consts(self, pool, seen):
        pool.iota(self.rank[:, :], pattern=[[-1, self.ne]], base=self.ne, channel_multiplier=0,
                  allow_small_or_imprecise_dtypes=True).then_inc(self.consts, 1)
        pool.memset(self.ones[:, :], 1.0).then_inc(self.consts, 1)
        pool.memset(self.tri[:, :], 1.0).then_inc(seen, 1)
        pool.wait_ge(seen, 1)
        pool.affine_select(out=self.tri[:, :], in_=self.tri[:, :], compare_op=ALU.is_gt, fill=0.0, base=0,
                           pattern=[[1, TR]], channel_multiplier=-1).then_inc(self.consts, 1)

    def dve_top2(self, dve, ch, scores):
        wide = lambda a: a.unsqueeze(2).to_broadcast([TR, NT, self.ne])
        rank = self.rank[:, :].unsqueeze(1).to_broadcast([TR, NT, self.ne])
        for i, (src, to) in enumerate(((scores, self.first), (self.work[:, :, :], self.second))):
            if i:
                ch.link(dve.scalar_tensor_tensor(out=self.work[:, :, :], in0=self.first[:, :, :], scalar=NEG, in1=scores,
                                                 op0=ALU.mult, op1=ALU.add))
            ch.link(dve.tensor_reduce(self.top[:, i], src, AX.X, ALU.max))
            ch.link(dve.tensor_tensor(self.pick[:, :, :], src, wide(self.top[:, i]), ALU.is_ge))
            ch.link(dve.tensor_tensor(self.pick[:, :, :], self.pick[:, :, :], rank, ALU.mult))
            ch.link(dve.tensor_reduce(self.best[:, :], self.pick[:, :, :], AX.X, ALU.max))
            ch.link(dve.tensor_tensor(to[:, :, :], self.pick[:, :, :], wide(self.best[:, :]), ALU.is_equal))

    def pe_counts(self, pe, n):
        pe.wait_ge(self.consts, 3)
        pe.wait_ge(self.mask_ready, n)
        for i, part in enumerate(self.halves):
            w = (part.stop - part.start) * self.ne
            pe.matmul(self.p_before[i][0:TR, 0:w], self.tri[:, :], self.mask[:, part], start=True, stop=True)
            mm = pe.matmul(self.p_total[i][:, 0:w], self.ones[0:TR, :], self.mask[:, part], start=True, stop=True)
        mm.then_inc(self.counted, 1)

    def dve_places(self, dve, ch):
        self.n_counts += 1
        dve.sem_inc(self.mask_ready, 1)
        dve.wait_ge(self.counted, self.n_counts)
        for i, part in enumerate(self.halves):
            w = (part.stop - part.start) * self.ne
            last = dve.tensor_copy(self.total[:, part].rearrange("p t e -> p (t e)"), self.p_total[i][:, 0:w])
        ch.link(last)
        for e in range(self.ne):
            last = dve.tensor_tensor_scan(self.until[:, :, e], self.ones[:, 0:NT], self.total[:, :, e], 0.0, ALU.mult, ALU.add)
        ch.link(last)
        ch.link(dve.tensor_tensor(self.total[:, :, :], self.until[:, :, :], self.total[:, :, :], ALU.subtract))
        for i, part in enumerate(self.halves):
            w = (part.stop - part.start) * self.ne
            last = dve.tensor_tensor(self.place[:, part].rearrange("p t e -> p (t e)"), self.p_before[i][0:TR, 0:w],
                                     self.total[0:TR, part].rearrange("p t e -> p (t e)"), ALU.add)
        ch.link(last)

    def dve_take(self, dve, ch, values, chosen, to):
        ch.link(dve.tensor_tensor(self.pick[:, :, :], values, chosen[:, :, :], ALU.mult))
        ch.link(dve.tensor_reduce(to, self.pick[:, :, :], AX.X, ALU.add))


class Experts:

    def __init__(self, nc, sem, sb, pb, name, tile_rows, turns, per_set, gated, fixed=False):
        self.r, self.n, self.turns, self.per_set, self.gated, self.fixed = tile_rows, 3 * tile_rows, turns, per_set, gated, fixed
        self.ct = f = 2 * per_set
        r, n = self.r, self.n
        self.x = sb(name + "_x", [r, 2, 3, D], F32)
        self.x_t = sb(name + "_x_t", [128, 2, KD, n], F32R)
        shapes = [[KD, 512], [KD, 512], [4, D]] if gated else [[KD, 512], [4, D]]
        self.pieces = range(len(shapes))
        self.raw = [sb(f"{name}_raw{p}", [128, 1024], F32) for p in self.pieces]
        self.w = [sb(f"{name}_w{p}", [128, 2, 2, *shape], F32R) for p, shape in enumerate(shapes)]
        self.act = sb(name + "_act", [128, 2, n], F32)
        self.prod = sb(name + "_prod", [128, 2, n], F32) if gated else self.act
        self.hid = sb(name + "_hid", [128, 2, 4, n], F32R)
        self.y = sb(name + "_y", [r, 2, 3, D], F32) if not fixed else None
        self.p_x = [pb(f"{name}_p_x{k}", [128, BANK], F32) for k in range(2)]
        self.p_g = [pb(f"{name}_p_g{k}", [128, BANK], F32) for k in range(2)]
        self.p_u = [pb(f"{name}_p_u{k}", [128, BANK], F32) for k in range(2)] if gated else None
        self.p_y = [pb(f"{name}_p_y{k}", [128, BANK], F32) for k in range(2)]
        self.x_in = [Tally(sem(f"{name}_x_in{u}"), 16 * f // 2, 16 * (1 - u)) for u in range(2)]
        self.y_out = [Tally(sem(f"{name}_y_out{u}"), 16 * f // 2, 1) for u in range(2)]
        self.raw_in = [Tally(sem(f"{name}_raw_in{p}"), 32, 16) for p in self.pieces]
        self.w_high = [Tally(sem(f"{name}_w_high{p}"), 2, 1) for p in self.pieces]
        self.w_low = [Tally(sem(f"{name}_w_low{p}"), 2, 1) for p in self.pieces]
        self.turned = Tally(sem(name + "_turned"), f, 2)
        self.x_high = Tally(sem(name + "_x_high"), 2 * f, 2)
        self.x_low = Tally(sem(name + "_x_low"), 2 * f, 2)
        self.up_full = Tally(sem(name + "_up_full"), 4 * f)
        self.act_done = Tally(sem(name + "_act_done"), 4 * f, 4)
        self.prod_done = Tally(sem(name + "_prod_done"), 4 * f, 4)
        self.hid_high = Tally(sem(name + "_hid_high"), 4 * f, 4)
        self.hid_low = Tally(sem(name + "_hid_low"), 4 * f, 4)
        self.y_full = Tally(sem(name + "_y_full"), 3 * f, 7)
        self.y_done = Tally(sem(name + "_y_done"), 3 * f, 3)


    def pe_ahead(self, pe):
        pe.sem_inc(self.y_full.sem, self.y_full.ahead)
        pe.sem_inc(self.turned.sem, self.turned.ahead - 1)

    def act_ahead(self, act):
        act.sem_inc(self.act_done.sem, self.act_done.ahead)
        if not self.gated:
            act.sem_inc(self.hid_high.sem, self.hid_high.ahead)

    def dve_ahead(self, dve):
        dve.sem_inc(self.y_done.sem, self.y_done.ahead)
        dve.sem_inc(self.hid_low.sem, self.hid_low.ahead)
        if self.gated:
            dve.sem_inc(self.prod_done.sem, self.prod_done.ahead)
            dve.sem_inc(self.hid_high.sem, self.hid_high.ahead)

    def sp_ahead(self, sp):
        for t in self.y_out:
            sp.sem_inc(t.sem, t.ahead)


    def w_set(self, i):
        return 0 if self.fixed else i // self.per_set

    def w_wait(self, pe, b, s, p):
        t = self.w_low[p]
        pe.wait_ge(t.sem, 1 if self.fixed else t.now(b, s))

    def w_high_part(self, act, b, s, p):
        if b is None:
            act.wait_ge(self.raw_in[p].sem, 16 * (s + 1))
        else:
            act.wait_ge(self.raw_in[p].sem, self.raw_in[p].now(b, 16 * s))
            act.wait_ge(self.y_full.sem, self.y_full.now(b, 3 * self.per_set * (s - 1)))
        split_high(act, self.w[p][:, s % 2, 0].rearrange("p a n -> p (a n)"), self.raw[p][:, :]).then_inc(self.w_high[p].sem, 1)

    def w_low_part(self, dve, b, s, p):
        dve.wait_ge(self.w_high[p].sem, s + 1 if b is None else self.w_high[p].now(b, s))
        flat = lambda part: self.w[p][:, s % 2, part].rearrange("p a n -> p (a n)")
        split_low(dve, flat(1), self.raw[p][:, :], flat(0)).then_inc(self.w_low[p].sem, 1)

    def raw_free(self, eng, b, s, p):
        if b is not None:
            eng.wait_ge(self.w_low[p].sem, self.w_low[p].now(b, s - 1))
        elif s:
            eng.wait_ge(self.w_low[p].sem, s)


    def x_load(self, sp, b, i, src):
        if b is not None:
            sp.wait_ge(self.turned.sem, self.turned.now(b, i - 2))
        u = i % 2
        sp.dma_start(self.x[:, u], src).then_inc(self.x_in[u].sem, 16)

    def x_here(self, b, i):
        return 16 if b is None else b * self.x_in[i % 2].per + 16 * (i // 2 + 1)

    def pe_turn(self, pe, b, i, ident):
        u = i % 2
        pe.wait_ge(self.x_in[u].sem, self.x_here(b, i))
        if b is not None:
            pe.wait_ge(self.x_low.sem, self.x_low.now(b, 2 * (i - 1)))
        for k in range(KD):
            for j in range(3):
                mm = pe.transpose(self.p_x[k][:, self.r * j:self.r * (j + 1)], self.x[:, u, j, k::2], ident[0:self.r, 0:self.r])
        mm.then_inc(self.turned.sem, 1)

    def act_x(self, act, b, i):
        act.wait_ge(self.turned.sem, 2 if b is None else self.turned.now(b, i))
        for k in range(KD):
            split_high(act, self.x_t[:, 0, k], self.p_x[k][:, 0:self.n]).then_inc(self.x_high.sem, 1)

    def dve_x(self, dve, b, i):
        for k in range(KD):
            dve.wait_ge(self.x_high.sem, k + 1 if b is None else self.x_high.now(b, 2 * (i - 1) + k + 1))
            split_low(dve, self.x_t[:, 1, k], self.p_x[k][:, 0:self.n], self.x_t[:, 0, k]).then_inc(self.x_low.sem, 1)


    def pe_up(self, pe, b, i):
        s = self.w_set(i)
        pe.wait_ge(self.x_low.sem, self.x_low.now(b, 2 * i))
        for p in self.pieces[:-1]:
            self.w_wait(pe, b, s, p)
        for c in range(4):
            t = self.prod_done if self.gated else self.act_done
            pe.wait_ge(t.sem, t.now(b, 4 * i + c - 1))
            if not self.gated:
                pe.wait_ge(self.hid_high.sem, self.hid_high.now(b, 4 * i + c - 1))
            for p, to in ((0, self.p_g), (1, self.p_u)) if self.gated else ((0, self.p_g),):
                w = self.w[p]
                for k in range(KD):
                    mm = matmul3(pe, to[c % 2][:, 0:self.n], (w[:, s % 2, 0, k, c::4], w[:, s % 2, 1, k, c::4]),
                                 (self.x_t[:, 0, k], self.x_t[:, 1, k]), k == 0, k == KD - 1)
            mm.then_inc(self.up_full.sem, 1)

    def act_up(self, act, b, i, c):
        act.wait_ge(self.up_full.sem, self.up_full.now(b, 4 * i + c + 1))
        t = self.prod_done if self.gated else self.hid_low
        act.wait_ge(t.sem, t.now(b, 4 * i + c - 1))
        act.activation(self.act[:, c % 2], self.p_g[c % 2][:, 0:self.n], ACT.Silu).then_inc(self.act_done.sem, 1)
        if not self.gated:
            act.wait_ge(self.y_full.sem, self.y_full.now(b, 3 * i))
            act.activation(self.hid[:, 0, c], self.p_g[c % 2][:, 0:self.n], ACT.Silu).then_inc(self.hid_high.sem, 1)

    def dve_up(self, dve, b, i, c):
        if self.gated:
            dve.wait_ge(self.act_done.sem, self.act_done.now(b, 4 * i + c + 1))
            dve.wait_ge(self.y_full.sem, self.y_full.now(b, 3 * i))
            up, gate = self.p_u[c % 2][:, 0:self.n], self.act[:, c % 2]
            dve.tensor_tensor(self.hid[:, 0, c], up, gate, ALU.mult).then_inc(self.hid_high.sem, 1)
            dve.tensor_tensor(self.prod[:, c % 2], up, gate, ALU.mult).then_inc(self.prod_done.sem, 1)
            dve.wait_ge(self.prod_done.sem, self.prod_done.now(b, 4 * i + c + 1))
        dve.wait_ge(self.hid_high.sem, self.hid_high.now(b, 4 * i + c + 1))
        if not self.gated:
            dve.wait_ge(self.y_full.sem, self.y_full.now(b, 3 * i))
        split_low(dve, self.hid[:, 1, c], self.prod[:, c % 2], self.hid[:, 0, c]).then_inc(self.hid_low.sem, 1)

    def act_chunk(self, act, b, i):
        s = i // self.per_set
        now = not self.fixed and i % self.per_set == 0
        for c in range(4):
            if now and c < len(self.pieces):
                self.w_high_part(act, b, s + 1, c)
            self.act_up(act, b, i, c)
        self.act_x(act, b, i + 1)

    def dve_chunk(self, dve, b, i):
        s = i // self.per_set
        now = not self.fixed and i % self.per_set == 0
        for c in range(4):
            self.dve_up(dve, b, i, c)
            if now and c < len(self.pieces):
                self.w_low_part(dve, b, s + 1, c)
        self.dve_x(dve, b, i + 1)


    def pe_down(self, pe, b, i):
        s, w = self.w_set(i), self.w[-1]
        self.w_wait(pe, b, s, self.pieces[-1])
        for j in range(3):
            n = 3 * i + j
            pe.wait_ge(self.y_done.sem, self.y_done.now(b, n - 1))
            at = slice(self.r * j, self.r * (j + 1))
            for c in range(4):
                if j == 0:
                    pe.wait_ge(self.hid_low.sem, self.hid_low.now(b, 4 * i + c + 1))
                mm = matmul3(pe, self.p_y[n % 2][0:self.r, 0:D], (self.hid[:, 0, c, at], self.hid[:, 1, c, at]),
                             (w[:, s % 2, 0, c], w[:, s % 2, 1, c]), c == 0, c == 3)
            mm.then_inc(self.y_full.sem, 1)

    def dve_out(self, dve, b, i):
        for j in range(3):
            n = 3 * i + j
            dve.wait_ge(self.y_full.sem, self.y_full.now(b, n + 1))
            if j == 0:
                t = self.y_out[i % 2]
                dve.wait_ge(t.sem, t.now(b, 16 * (i // 2)))
            dve.tensor_copy(self.y[:, i % 2, j], self.p_y[n % 2][0:self.r, 0:D]).then_inc(self.y_done.sem, 1)

    def dve_add(self, dve, b, i, h, factor):
        for j in range(3):
            n = 3 * i + j
            dve.wait_ge(self.y_full.sem, self.y_full.now(b, n + 1))
            to = h(j)
            dve.scalar_tensor_tensor(out=to, in0=self.p_y[n % 2][0:self.r, 0:D].unsqueeze(1), scalar=factor, in1=to,
                                     op0=ALU.mult, op1=ALU.add).then_inc(self.y_done.sem, 1)

    def y_store(self, eng, b, i, dst):
        eng.wait_ge(self.y_done.sem, self.y_done.now(b, 3 * i + 3))
        eng.dma_start(dst, self.y[:, i % 2]).then_inc(self.y_out[i % 2].sem, 16)


SLOTS0 = 32 * 384
SLOTS1 = 16 * 720


def chunk_rows(dram, b, per_turn, i, r):
    return dram[bass.ds(b * (per_turn * 3 * r) + i * 3 * r, 3 * r)].rearrange("(j p) d -> p j d", p=r)


def pool_scatter(pool, slots, rows, dram, limit, done, done_slots):
    if done_slots:
        pool.wait_ge(done_slots[0], done_slots[1])
    for t in range(NT):
        for i in range(2):
            pool.indirect_dma_start(dram, bass.IndirectOffsetOnAxis(ap=slots[:, i, t:t + 1], axis=0), rows[:, t], None,
                                    bounds_check=limit, oob_is_err=False).then_inc(done, 16)
    pool.wait_ge(done, 16 * 2 * NT)


class Combine:

    def __init__(self, sem, sb, name, slots, weight, ahead):
        self.g = sb(name + "_g", [TR, 2, NJ, D], F32)
        self.slots, self.weight = slots, weight
        self.here = Tally(sem(name + "_here"), 16 * 2 * NJ, 16 * 2 * NJ * ahead)
        self.added = Tally(sem(name + "_added"), 2 * NJ, 2 * NJ * ahead)

    def pool_gather(self, pool, batch, ys, count):
        if count:
            pool.wait_ge(self.added.sem, 2 * NJ * count)
        for i in range(2):
            for j in range(NJ):
                t = NJ * batch + j
                pool.indirect_dma_start(self.g[:, i, j], None, ys, bass.IndirectOffsetOnAxis(ap=self.slots[:, i, t:t + 1], axis=0))\
                    .then_inc(self.here.sem, 16)

    def dve_add(self, dve, at, h, weight):
        dve.wait_ge(self.here.sem, at(self.here, 16 * 2 * NJ))
        for i in range(2):
            if i:
                dve.wait_ge(self.added.sem, at(self.added, NJ))
            for j in range(NJ):
                dve.scalar_tensor_tensor(out=h(j), in0=self.g[:, i, j:j + 1], scalar=weight(i, j), in1=h(j),
                                         op0=ALU.mult, op1=ALU.add).then_inc(self.added.sem, 1)
        dve.wait_ge(self.added.sem, at(self.added, 2 * NJ))


def stage_experts0(nc, A, keep, sem, sb, pb):
    rows, ident, logits = keep["rows"], keep["ident"], keep["logits0"]
    NE, R = 8, 128
    N = 3 * R
    NC = SLOTS0 // N
    MOST = NTOK // N
    assert NC == 2 * NTOK // N + NE
    slots, weight = keep["slots0"], keep["weight0"]
    rt = Routing(sem, sb, pb, "rt0", NE, slots)
    filled = sb("filled", [128, NE, MOST], F32)
    bound = sb("bound", [128, MOST], F32)
    n_chunks = sb("n_chunks", [128, NE], F32)
    chunks_until = sb("chunks_until", [128, NE], F32)
    start = sb("start", [128, NE], F32)
    chunk_id = sb("chunk_id", [128, NC + 2], F32)
    passed = sb("passed", [128, NC + 2, NE], F32)
    of_chunk = sb("of_chunk", [128, NC + 2], F32)
    part_id = sb("part_id", [128, 1], F32)
    w_row = sb("w_row", [128, NC + 2], I32)
    w_row_now = sb("w_row_now", [128, 2], I32)
    xs, ys = keep["xs"], keep["ys"]
    rdve, rseen, iotas = sem("rt0_dve"), sem("rt0_seen"), sem("rt0_iotas")
    gap, gap_exp = sem("gap"), sem("gap_exp")
    slots_done, scattered = sem("slots0_done"), sem("scattered0")

    with nc.Block() as block:

        @block.gpsimd
        def _(pool):
            rt.pool_consts(pool, rseen)
            pool.iota(bound[:, :], pattern=[[N, MOST]], base=0, channel_multiplier=0,
                      allow_small_or_imprecise_dtypes=True).then_inc(iotas, 1)
            pool.iota(chunk_id[:, :], pattern=[[1, NC + 2]], base=0, channel_multiplier=0,
                      allow_small_or_imprecise_dtypes=True).then_inc(iotas, 1)
            pool.iota(part_id[:, :], pattern=[[0, 1]], base=0, channel_multiplier=1,
                      allow_small_or_imprecise_dtypes=True).then_inc(iotas, 1)
            pool_scatter(pool, rt.slot, rows, xs, SLOTS0 - 1, scattered, (slots_done, 1))

        @block.scalar
        def _(act):
            act.wait_ge(gap, 1)
            act.activation(weight[:, 1, 0:NT], weight[:, 1, 0:NT], ACT.Exp).then_inc(gap_exp, 1)

        @block.tensor
        def _(pe):
            rt.pe_counts(pe, 1)

        @block.vector
        def _(dve):
            ch = Chain(dve, rdve)
            ch.link(dve.memset(weight[:, :, NT:], 0.0))
            dve.wait_ge(rt.consts, 3)
            dve.wait_ge(iotas, 3)
            rt.dve_top2(dve, ch, logits[:, 0:NT])
            ch.link(dve.tensor_tensor(weight[:, 1, 0:NT], rt.top[:, 1], rt.top[:, 0], ALU.subtract))
            dve.sem_inc(gap, 1)
            ch.link(dve.tensor_tensor(rt.mask[:, :, :], rt.first[:, :, :], rt.second[:, :, :], ALU.add))
            rt.dve_places(dve, ch)
            ch.link(dve.tensor_tensor(filled[:, :, :], rt.until[:, NT - 1].unsqueeze(2).to_broadcast([128, NE, MOST]),
                                      bound[:, :].unsqueeze(1).to_broadcast([128, NE, MOST]), ALU.is_gt))
            ch.link(dve.tensor_reduce(n_chunks[:, :], filled[:, :, :], AX.X, ALU.add))
            ch.link(dve.tensor_tensor_scan(chunks_until[:, :], rt.ones[:, 0:NE], n_chunks[:, :], 0.0, ALU.mult, ALU.add))
            ch.link(dve.tensor_tensor(start[:, :], chunks_until[:, :], n_chunks[:, :], ALU.subtract))
            ch.link(dve.tensor_scalar(start[:, :], start[:, :], float(N), None, ALU.mult))
            ch.link(dve.tensor_tensor(rt.place[:, :, :], rt.place[:, :, :],
                                      start[0:TR].unsqueeze(1).to_broadcast([TR, NT, NE]), ALU.add))
            for i, chosen in enumerate((rt.first, rt.second)):
                rt.dve_take(dve, ch, rt.place[:, :, :], chosen, rt.slot_f[:, i])
            dve.tensor_copy(rt.slot[:, :, :], rt.slot_f[:, :, :]).then_inc(slots_done, 1)
            ch.link(dve.tensor_tensor(passed[:, :, :], chunk_id[:, :].unsqueeze(2).to_broadcast([128, NC + 2, NE]),
                                      chunks_until[:, :].unsqueeze(1).to_broadcast([128, NC + 2, NE]), ALU.is_ge))
            ch.link(dve.tensor_reduce(of_chunk[:, :], passed[:, :, :], AX.X, ALU.add))
            ch.link(dve.tensor_scalar(of_chunk[:, :], of_chunk[:, :], float(NE - 1), 128.0, ALU.min, ALU.mult))
            ch.link(dve.tensor_scalar(w_row[:, :], of_chunk[:, :], part_id[:, 0:1], None, ALU.add))
            dve.wait_ge(gap_exp, 1)
            ch.link(dve.tensor_scalar(weight[:, 0, 0:NT], weight[:, 1, 0:NT], 1.0, None, ALU.add))
            ch.link(dve.reciprocal(weight[:, 0, 0:NT], weight[:, 0, 0:NT]))
            ch.link(dve.tensor_tensor(weight[:, 1, 0:NT], weight[:, 1, 0:NT], weight[:, 0, 0:NT], ALU.mult))

    with ExitStack() as inner:
        sb2 = lambda name, shape, dt: inner.enter_context(nc.sbuf_tensor(name, shape, dt))
        pb2 = lambda name, shape, dt: inner.enter_context(nc.psum_tensor(name, shape, dt))
        ex = Experts(nc, sem, sb2, pb2, "ex0", R, NC // 2, 1, False)
        row_copied = Tally(sem("row_copied"), 2, 1)
        weights = [A["L0_ffn_w1"].rearrange("e (p k) n -> (e p) (k n)", k=KD),
                   A["L0_ffn_w2"].rearrange("e (p c) n -> (e p) (c n)", c=4)]

        with nc.Block() as block:

            @block.sync
            def _(sp):
                ex.sp_ahead(sp)
                ex.x_load(sp, None, 0, xs[0:N].rearrange("(j p) d -> p j d", p=R))
                with sp.Fori(0, ex.turns) as b:
                    for i in range(2):
                        ex.x_load(sp, b, i + 1, chunk_rows(xs, b, 2, i + 1, R))
                    for i in range(2):
                        ex.y_store(sp, b, i, chunk_rows(ys, b, 2, i, R))
                for u in range(2):
                    sp.wait_ge(ex.y_out[u].sem, ex.y_out[u].now(ex.turns, 0))

            @block.gpsimd
            def _(pool):
                def load(b, s):
                    u = s % 2
                    if b is None:
                        pool.tensor_copy(w_row_now[:, 0:1], w_row[:, 0:1]).then_inc(row_copied.sem, 1)
                        pool.wait_ge(row_copied.sem, 1)
                    else:
                        pool.tensor_copy(w_row_now[:, u:u + 1], w_row[:, bass.ds(b * 2 + s, 1)]).then_inc(row_copied.sem, 1)
                        pool.wait_ge(row_copied.sem, row_copied.now(b, s))
                    for p in ex.pieces:
                        ex.raw_free(pool, b, s, p)
                        if b is not None:
                            pool.sem_inc(rseen, 1)
                        pool.indirect_dma_start(ex.raw[p][:, :], None, weights[p],
                                                bass.IndirectOffsetOnAxis(ap=w_row_now[:, u:u + 1], axis=0))\
                            .then_inc(ex.raw_in[p].sem, 16)

                load(None, 0)
                with pool.Fori(0, ex.turns) as b:
                    for s in range(1, 3):
                        load(b, s)
                for p in ex.pieces:
                    pool.wait_ge(ex.raw_in[p].sem, ex.raw_in[p].now(ex.turns, 0))

            @block.scalar
            def _(act):
                ex.act_ahead(act)
                for p in ex.pieces:
                    ex.w_high_part(act, None, 0, p)
                ex.act_x(act, None, 0)
                with act.Fori(0, ex.turns) as b:
                    for i in range(2):
                        ex.act_chunk(act, b, i)

            @block.tensor
            def _(pe):
                ex.pe_ahead(pe)
                ex.pe_turn(pe, None, 0, ident)
                with pe.Fori(0, ex.turns) as b:
                    for i in range(2):
                        ex.pe_up(pe, b, i)
                        ex.pe_turn(pe, b, i + 1, ident)
                        ex.pe_down(pe, b, i)

            @block.vector
            def _(dve):
                ex.dve_ahead(dve)
                for p in ex.pieces:
                    ex.w_low_part(dve, None, 0, p)
                ex.dve_x(dve, None, 0)
                with dve.Fori(0, ex.turns) as b:
                    for i in range(2):
                        ex.dve_chunk(dve, b, i)
                        ex.dve_out(dve, b, i)


def stage_distance(nc, A, keep, sem, sb, pb):
    h, rows, ident, logits = keep["h"], keep["rows"], keep["ident"], keep["logits1"]
    R, NE = 32, 16
    u3 = sb("u3", [128, KD, 3, R], F32)
    gate = sb("gate1", [128, KD, NE], F32)
    minus_half = sb("minus_half5", [TR, NJ], F32)
    eps = sb("ln_eps5", [TR, NJ], F32)
    zero = sb("zero5", [TR, NJ, D], F32)
    xn = sb("dxn", [TR, NJ, D], F32)
    xc = sb("dxc", [TR, NJ, D], F32)
    x_t = sb("dx_t", [128, KD, S], F32)
    c_t = sb("dc_t", [128, KD, S], F32)
    q_t = sb("dq_t", [3 * R, S], F32)
    k_t = sb("dk_t", [3 * R, S], F32)
    prob = sb("dprob", [TR, NJ, S], F32)
    prob_t = sb("dprob_t", [TR, NJ, S], F32)
    neg_max = sb("dneg_max", [TR, NJ], F32)
    row_sum = sb("drow_sum", [TR, NJ], F32)
    inv_sum = sb("dinv_sum", [TR, NJ], F32)
    p_s = [pb(f"dp_s{j}", [TR, BANK], F32) for j in range(NJ)]
    p_t = [pb(f"dp_t{j}", [TR, BANK], F32) for j in range(NJ)]
    p_x = [pb(f"dp_x{k}", [128, BANK], F32) for k in range(KD)]

    cb = Combine(sem, sb, "cb0", keep["slots0"], keep["weight0"], ahead=2)
    norm = Norm(sem, sb, "ln5", ahead=2)
    norm_c = Norm(sem, sb, "ln6", ahead=0)
    xn_done, xc_done = Tally(sem("dxn_done"), NJ, 2 * NJ), Tally(sem("dxc_done"), NJ)
    turned_x, turned_c = Tally(sem("dturned_x"), 1, 1), Tally(sem("dturned_c"), 1, 1)
    kept_x, kept_c = Tally(sem("dkept_x"), 1, 2), Tally(sem("dkept_c"), 1, 1)
    x_t_done, c_t_done = Tally(sem("dx_t_done"), KD, KD), Tally(sem("dc_t_done"), KD, KD)
    y_full, y_done = Tally(sem("dy_full"), 1, 1), Tally(sem("dy_done"), 4, 4)
    scored, max_done, exp_done = (Tally(sem("d" + n), NJ, NJ) for n in ("scored", "max_done", "exp_done"))
    inv_done, h_done = Tally(sem("dinv_done"), 1), Tally(sem("dh_done"), NJ)
    turned_p, p_t_done = Tally(sem("dturned_p"), 1, 1), Tally(sem("dp_t_done"), NJ, NJ)
    weighted = Tally(sem("dweighted"), NJ, NJ)
    gated, logits_done = Tally(sem("dgated"), 1), Tally(sem("dlogits_done"), 1, 1)
    w_in, consts, pool_seen = sem("dist_w_in"), sem("dist_consts"), sem("dpool_seen")

    with nc.Block() as block:

        @block.sync
        def _(sp):
            for i in range(3):
                sp.dma_start(u3[:, :, i], rows_of(A["L1_attn_U"])).then_inc(w_in, 16)
            sp.dma_start(gate[:, :, :], rows_of(A["L1_ffn_gate_w"])).then_inc(w_in, 16)

        @block.gpsimd
        def _(pool):
            pool.memset(minus_half[:, :], -0.5).then_inc(consts, 1)
            pool.memset(eps[:, :], LN_EPS).then_inc(consts, 1)
            pool.memset(zero[:, :, :], 0.0).then_inc(consts, 1)
            pool.wait_ge(consts, 5)
            pool.sem_inc(kept_c.sem, kept_c.ahead)

            def keep_rows(src, src_done, to, done, at):
                pool.wait_ge(src_done.sem, at(src_done, NJ))
                pool.sem_inc(pool_seen, 1)
                pool.tensor_tensor(to, src[:, :, :], zero[:, :, :], ALU.add).then_inc(done.sem, 1)

            cb.pool_gather(pool, 0, keep["ys"], 0)
            for b, at in ((0, at_first), (1, at_second)):
                norm.pool_inverse(pool, eps, minus_half, at)
                keep_rows(xn, xn_done, rows[:, slot(b)], kept_x, at)
                cb.pool_gather(pool, b + 1, keep["ys"], b + 1)
            for b in range(B):
                if b + 1 < B:
                    norm.pool_inverse(pool, eps, minus_half, at_now(b))
                norm_c.pool_inverse(pool, eps, minus_half, at_now(b))
                if b + 2 < B:
                    cb.pool_gather(pool, min(b + 3, B - 1), keep["ys"], b + 3)
                if b + 1 < B:
                    keep_rows(xn, xn_done, rows[:, slot(b + 2)], kept_x, at_now(b))
                keep_rows(xc, xc_done, rows[:, slot(b)], kept_c, at_now(b))

        @block.scalar
        def _(act):
            act.sem_inc(c_t_done.sem, c_t_done.ahead)
            act.sem_inc(logits_done.sem, logits_done.ahead)

            def project(at):
                act.wait_ge(turned_x.sem, at(turned_x, 1))
                for k in range(KD):
                    act.activation(x_t[:, k], p_x[k][:, 0:S], ACT.Copy).then_inc(x_t_done.sem, 1)
                act.wait_ge(y_full.sem, at(y_full, 1))
                act.activation(q_t[0:R, :], p_x[0][0:R, 0:S], ACT.Copy, scale=2.0).then_inc(y_done.sem, 1)
                act.activation(k_t[0:R, :], p_x[0][0:R, 0:S], ACT.Copy).then_inc(y_done.sem, 1)
                act.activation(q_t[R:2 * R, :], p_x[0][R:2 * R, 0:S], ACT.Square).then_inc(y_done.sem, 1)
                act.activation(k_t[2 * R:3 * R, :], p_x[0][2 * R:3 * R, 0:S], ACT.Square).then_inc(y_done.sem, 1)

            def exps(at):
                for j in range(NJ):
                    act.wait_ge(max_done.sem, at(max_done, j + 1))
                    act.activation(prob[:, j], p_s[j][:, 0:S], ACT.Exp, bias=neg_max[:, j:j + 1],
                                   accum_out=row_sum[:, j:j + 1]).then_inc(exp_done.sem, 1)

            def keep_turned(at):
                act.wait_ge(turned_p.sem, at(turned_p, 1))
                for j in range(NJ):
                    act.activation(prob_t[:, j], p_t[j][:, 0:S], ACT.Copy).then_inc(p_t_done.sem, 1)

            project(at_first)
            exps(at_first)
            keep_turned(at_first)

            def apply_and_route(b, last=False):
                if not last:
                    project(at_turn(b))
                    act.wait_ge(inv_done.sem, inv_done.now(b, 1))
                    exps(at_turn(b))
                    keep_turned(at_turn(b))
                act.wait_ge(turned_c.sem, turned_c.now(b, 1))
                for k in range(KD):
                    act.activation(c_t[:, k], p_x[k][:, 0:S], ACT.Copy).then_inc(c_t_done.sem, 1)
                act.wait_ge(gated.sem, gated.now(b, 1))
                act.activation(logits[:, slot(b)], p_x[1][0:TR, S:S + NJ * NE].rearrange("p (j e) -> p j e", e=NE), ACT.Copy)\
                   .then_inc(logits_done.sem, 1)

            with act.Fori(0, B - 1) as b:
                apply_and_route(b)
            apply_and_route(B - 1, last=True)

        @block.tensor
        def _(pe):
            pe.sem_inc(turned_c.sem, turned_c.ahead)
            pe.sem_inc(weighted.sem, weighted.ahead)

            def turn(src, src_done, done, at):
                pe.wait_ge(src_done.sem, at(src_done, NJ))
                for k in range(KD):
                    for j in range(NJ):
                        mm = pe.transpose(p_x[k][:, TR * j:TR * j + TR], src[:, j, 128 * k:128 * k + 128], ident[0:TR, 0:TR])
                mm.then_inc(done.sem, 1)

            def project(at):
                pe.wait_ge(x_t_done.sem, at(x_t_done, KD))
                for k in range(KD):
                    mm = pe.matmul(p_x[0][0:3 * R, 0:S], u3[:, k], x_t[:, k], start=k == 0, stop=k == KD - 1)
                mm.then_inc(y_full.sem, 1)

            def scores(at):
                pe.wait_ge(y_done.sem, at(y_done, 4))
                for j in range(NJ):
                    pe.matmul(p_s[j][:, 0:S], q_t[:, TR * j:TR * j + TR], k_t[:, :], start=True, stop=True)\
                      .then_inc(scored.sem, 1)

            pe.wait_ge(consts, 5)
            pe.wait_ge(w_in, 16 * 4)
            def turn_probs(at):
                pe.wait_ge(exp_done.sem, at(exp_done, NJ))
                for j in range(NJ):
                    for kt in range(NJ):
                        mm = pe.transpose(p_t[kt][:, TR * j:TR * j + TR], prob[:, j, TR * kt:TR * kt + TR], ident[0:TR, 0:TR])
                mm.then_inc(turned_p.sem, 1)

            def weigh(b, j):
                for kt in range(NJ):
                    mm = pe.matmul(p_t[j][:, 0:D].unsqueeze(1), prob_t[:, kt, TR * j:TR * j + TR], rows[:, slot(b, kt)],
                                   start=kt == 0, stop=kt == NJ - 1)
                mm.then_inc(weighted.sem, 1)

            turn(xn, xn_done, turned_x, at_first)
            project(at_first)
            scores(at_first)
            turn_probs(at_first)

            def apply_and_route(b, last=False):
                pe.wait_ge(kept_x.sem, kept_x.now(b, -1))
                pe.wait_ge(p_t_done.sem, p_t_done.before(b, NJ))
                weigh(b, 0)
                pe.wait_ge(c_t_done.sem, c_t_done.before(b, KD))
                pe.wait_ge(logits_done.sem, logits_done.before(b, 1))
                if not last:
                    turn(xn, xn_done, turned_x, lambda tally, n: tally.before(b, n))
                weigh(b, 1)
                if not last:
                    project(at_turn(b))
                    scores(at_turn(b))
                weigh(b, 2)
                if not last:
                    pe.wait_ge(h_done.sem, h_done.now(b, NJ))
                    turn_probs(at_turn(b))
                turn(xc, xc_done, turned_c, at_now(b))
                pe.wait_ge(c_t_done.sem, c_t_done.now(b, KD))
                for j in range(NJ):
                    for k in range(KD):
                        mm = pe.matmul(p_x[1][0:TR, S + NE * j:S + NE * j + NE], c_t[:, k, TR * j:TR * j + TR], gate[:, k],
                                       start=k == 0, stop=k == KD - 1)
                mm.then_inc(gated.sem, 1)

            with pe.Fori(0, B - 1) as b:
                apply_and_route(b)
            apply_and_route(B - 1, last=True)

        @block.vector
        def _(dve):
            def maxima(at):
                for j in range(NJ):
                    dve.wait_ge(scored.sem, at(scored, j + 1))
                    dve.tensor_reduce(neg_max[:, j:j + 1], p_s[j][:, 0:S], AX.X, ALU.max, negate=True)\
                       .then_inc(max_done.sem, 1)

            dve.memset(q_t[2 * R:3 * R, :], -1.0).then_inc(consts, 1)
            dve.memset(k_t[R:2 * R, :], -1.0).then_inc(consts, 1)
            def stats_x(b, at):
                cb.dve_add(dve, at, lambda j: h[:, slot(b, j)], lambda i, j: cb.weight[:, i, slot(b, j)])
                dve.sem_inc(norm.stats_seen, 1)
                norm.dve_stats(dve, lambda j: h[:, slot(b, j)], at)

            def apply_x(b, at):
                norm.dve_apply(dve, lambda j: h[:, slot(b, j)], lambda j: xn[:, j:j + 1], at, xn_done)

            stats_x(0, at_first)
            apply_x(0, at_first)
            maxima(at_first)
            stats_x(1, at_second)
            dve.wait_ge(turned_x.sem, 1)
            dve.wait_ge(kept_x.sem, 1)
            apply_x(1, at_second)

            def apply_and_route(b, last=False):
                dve.wait_ge(exp_done.sem, exp_done.before(b, NJ))
                dve.reciprocal(inv_sum[:, :], row_sum[:, :]).then_inc(inv_done.sem, 1)
                dve.wait_ge(inv_done.sem, inv_done.now(b, 1))
                for j in range(NJ):
                    if j == NJ - 1 and not last:
                        stats_x(b + 2, at_now(b))
                    dve.wait_ge(weighted.sem, weighted.now(b, j + 1))
                    to = h[:, slot(b, j)]
                    dve.scalar_tensor_tensor(out=to, in0=p_t[j][:, 0:D].unsqueeze(1), scalar=inv_sum[:, j:j + 1], in1=to,
                                             op0=ALU.mult, op1=ALU.add).then_inc(h_done.sem, 1)
                if not last:
                    maxima(at_turn(b))
                dve.wait_ge(h_done.sem, h_done.now(b, NJ))
                dve.sem_inc(norm_c.stats_seen, 1)
                norm_c.dve_stats(dve, lambda j: h[:, slot(b, j)], at_now(b))
                if not last:
                    dve.wait_ge(turned_x.sem, turned_x.now(b, 1))
                    dve.wait_ge(kept_x.sem, kept_x.before(b, 1))
                    apply_x(b + 2, at_now(b))
                dve.wait_ge(turned_c.sem, turned_c.before(b, 1))
                dve.wait_ge(kept_c.sem, kept_c.before(b, 1))
                norm_c.dve_apply(dve, lambda j: h[:, slot(b, j)], lambda j: xc[:, j:j + 1], at_now(b), xc_done)

            with dve.Fori(0, B - 1) as b:
                apply_and_route(b)
            apply_and_route(B - 1, last=True)


CAP = 720
LOWEST = -3.4028234663852886e38


def shared_expert(nc, A, keep, sem, e, pool_work, slots=None, weight=None):
    h, rows, ident = keep["h"], keep["rows"], keep["ident"]
    with ExitStack() as inner:
        sb = lambda name, shape, dt: inner.enter_context(nc.sbuf_tensor(name, shape, dt))
        pb = lambda name, shape, dt: inner.enter_context(nc.psum_tensor(name, shape, dt))
        ex = Experts(nc, sem, sb, pb, f"sh{e}", TR, B // 2, 1, True, fixed=True)
        cb = Combine(sem, sb, "cb1", slots, weight, 0) if slots is not None else None
        out_stored = sem(f"out_stored{e}")
        out = keep["out"].rearrange("b (j p) d -> p (b j) d", p=TR)

        with nc.Block() as block:

            @block.sync
            def _(sp):
                ex.x_load(sp, None, 0, rows[:, 0:NJ])
                for p, (name, k) in enumerate((("sw1", KD), ("sw3", KD), ("sw2", 4))):
                    sp.dma_start(ex.raw[p][:, :], A["L1_ffn_" + name][e].rearrange("(p k) n -> p (k n)", k=k)).then_inc(ex.raw_in[p].sem, 16)
                with sp.Fori(0, ex.turns) as b:
                    for i in range(2):
                        ex.x_load(sp, b, i + 1, rows[:, slot(b * 2 + i + 1)])
                    if cb:
                        for i in range(2):
                            sp.wait_ge(cb.added.sem, b * (4 * NJ) + 2 * NJ * (i + 1))
                            sp.dma_start(out[:, slot(b * 2 + i)], h[:, slot(b * 2 + i)]).then_inc(out_stored, 16)
                if cb:
                    sp.wait_ge(out_stored, 16 * B)

            @block.gpsimd
            def _(pool):
                if cb:
                    for b in range(B):
                        cb.pool_gather(pool, b, keep["ys"][0:SLOTS1], b)
                else:
                    pool_work(pool)

            @block.scalar
            def _(act):
                ex.act_ahead(act)
                for p in ex.pieces:
                    ex.w_high_part(act, None, 0, p)
                ex.act_x(act, None, 0)
                with act.Fori(0, ex.turns) as b:
                    for i in range(2):
                        ex.act_chunk(act, b, i)

            @block.tensor
            def _(pe):
                ex.pe_ahead(pe)
                ex.pe_turn(pe, None, 0, ident)
                with pe.Fori(0, ex.turns) as b:
                    for i in range(2):
                        ex.pe_up(pe, b, i)
                        ex.pe_turn(pe, b, i + 1, ident)
                        ex.pe_down(pe, b, i)

            @block.vector
            def _(dve):
                ex.dve_ahead(dve)
                for p in ex.pieces:
                    ex.w_low_part(dve, None, 0, p)
                ex.dve_x(dve, None, 0)
                with dve.Fori(0, ex.turns) as b:
                    for i in range(2):
                        ex.dve_chunk(dve, b, i)
                        ex.dve_add(dve, b, i, lambda j: h[:, slot(b * 2 + i, j)], 0.5)
                        if cb:
                            dve.wait_ge(ex.y_done.sem, ex.y_done.now(b, 3 * i + 3))
                            at = lambda tally, n: b * (2 * tally.per) + (tally.per * i + n)
                            cb.dve_add(dve, at, lambda j: h[:, slot(b * 2 + i, j)], lambda c, j: weight[:, c, slot(b * 2 + i, j)])


def stage_experts1(nc, A, keep, sem, sb, pb):
    rows, ident, logits = keep["rows"], keep["ident"], keep["logits1"]
    xs, ys = keep["xs"], keep["ys"]
    NE, R = 16, 120
    N = 3 * R
    assert NE * CAP == SLOTS1 and CAP % N == 0
    shape = [TR, NT, NE]
    slots = sb("slots1", [TR, 2, NT], I32)
    weight = sb("weight1", [TR, 2, NT], F32)
    gather_slot = sb("gather_slot", [TR, 2, NT], I32)
    route_sem = [sem(n) for n in ("rt1_dve", "rt1_seen", "rt1_in", "shifted", "exp1_done", "slots1_done", "scattered1")]
    rdve, rseen, b_in, shifted, exp_done, slots_done, scattered = route_sem
    steps = 31

    with ExitStack() as inner:
        sb2 = lambda name, shape, dt: inner.enter_context(nc.sbuf_tensor(name, shape, dt))
        pb2 = lambda name, shape, dt: inner.enter_context(nc.psum_tensor(name, shape, dt))
        rt = Routing(sem, sb2, pb2, "rt1", NE, slots)
        gate_b = sb2("gate_b", [TR, NE], F32)
        score = sb2("score", shape, F32)
        token_max = sb2("token_max", [TR, NT], F32)
        own = sb2("own", shape, F32)
        above = sb2("above", shape, F32)
        equal = sb2("equal", shape, F32)
        count = sb2("count", [TR, NE], F32)
        limit = sb2("limit", [TR, NE], I32)
        trial = sb2("trial", [TR, NE], I32)
        raised = sb2("raised", [TR, NE], I32)
        bit_f = sb2("bit_f", [TR, NE], F32)
        tried_f = sb2("tried_f", [TR, NE], F32)
        bit = sb2("bit", [TR, NE], I32)
        n_above = sb2("n_above", [TR, NE], F32)
        expert_slot = sb2("expert_slot", [TR, NE], F32)
        p_count = pb2("p_count", [TR, BANK], F32)
        summed = Tally(sem("summed"), 1, 1)
        totalled = Tally(sem("totalled"), 1, 1)
        search = LoopChain(None, sem("search"), 7)

        with nc.Block() as block:

            @block.sync
            def _(sp):
                sp.dma_start(gate_b[:, :], A["L1_ffn_gate_b"].partition_broadcast(TR)).then_inc(b_in, 16)

            @block.gpsimd
            def _(pool):
                rt.pool_consts(pool, rseen)
                pool.iota(expert_slot[:, :], pattern=[[CAP, NE]], base=-SLOTS1, channel_multiplier=0,
                          allow_small_or_imprecise_dtypes=True).then_inc(rt.consts, 1)

            @block.scalar
            def _(act):
                act.wait_ge(shifted, 1)
                act.activation(score[:, :, :], score[:, :, :], ACT.Exp).then_inc(exp_done, 1)

            @block.tensor
            def _(pe):
                def total(value):
                    pe.wait_ge(summed.sem, value)
                    pe.matmul(p_count[:, 0:NE], rt.ones[0:TR, 0:TR], count[:, :], start=True, stop=True).then_inc(totalled.sem, 1)

                pe.wait_ge(rt.consts, 4)
                total(1)
                with pe.Fori(0, steps) as b:
                    total(summed.now(b, 1))
                rt.pe_counts(pe, 1)
                rt.pe_counts(pe, 2)

            @block.vector
            def _(dve):
                ch = Chain(dve, rdve)
                wide = lambda a: a.unsqueeze(2).to_broadcast(shape)
                each = lambda a: a.unsqueeze(1).to_broadcast(shape)
                lg = logits[:, 0:NT]
                ch.link(dve.tensor_reduce(token_max[:, :], lg, AX.X, ALU.max))
                ch.link(dve.tensor_tensor(score[:, :, :], lg, wide(token_max[:, :]), ALU.subtract))
                dve.sem_inc(shifted, 1)
                dve.wait_ge(exp_done, 1)
                ch.link(dve.tensor_reduce(token_max[:, :], score[:, :, :], AX.X, ALU.add))
                ch.link(dve.reciprocal(token_max[:, :], token_max[:, :]))
                ch.link(dve.tensor_tensor(score[:, :, :], score[:, :, :], wide(token_max[:, :]), ALU.mult))
                dve.wait_ge(b_in, 16)
                ch.link(dve.tensor_tensor(score[:, :, :], score[:, :, :], each(gate_b[:, :]), ALU.add))
                dve.wait_ge(rt.consts, 4)
                rt.dve_top2(dve, ch, score[:, :, :])
                ch.link(dve.tensor_tensor(rt.mask[:, :, :], rt.first[:, :, :], rt.second[:, :, :], ALU.add))
                ch.link(dve.tensor_scalar(own[:, :, :], rt.mask[:, :, :], 1.0, -LOWEST, ALU.subtract, ALU.mult))
                ch.link(dve.tensor_tensor(rt.work[:, :, :], lg, rt.mask[:, :, :], ALU.mult))
                ch.link(dve.tensor_tensor(own[:, :, :], own[:, :, :], rt.work[:, :, :], ALU.add))

                def tokens_reaching(threshold, link):
                    link(dve.tensor_tensor(above[:, :, :], own[:, :, :], each(threshold), ALU.is_ge))
                    dve.tensor_reduce(count[:, :], above[:, :, :].rearrange("p t e -> p e t"), AX.X, ALU.add)\
                       .then_inc(summed.sem, 1)

                ch.link(dve.memset(bit_f[:, :], 0.0))
                tokens_reaching(bit_f[:, :], ch.link)
                dve.wait_ge(totalled.sem, 1)
                ch.link(dve.tensor_scalar(n_above[:, :], p_count[:, 0:NE], float(CAP), 1.0, ALU.is_ge, ALU.subtract))
                dve.tensor_copy(limit[:, :], n_above[:, :])
                ch.link(dve.memset(bit_f[:, :], float(2 ** (steps - 1))))
                ch.link(dve.tensor_copy(bit[:, :], bit_f[:, :]))
                with dve.Fori(0, steps) as b:
                    search.eng = dve
                    search.start(b)
                    search.link(dve.tensor_tensor(trial[:, :], limit[:, :], bit[:, :], ALU.bitwise_xor))
                    tokens_reaching(trial[:, :].bitcast(F32), search.link)
                    search.link(dve.tensor_copy(tried_f[:, :], bit_f[:, :]))
                    search.link(dve.tensor_scalar(bit_f[:, :], bit_f[:, :], 0.5, None, ALU.mult))
                    search.link(dve.tensor_copy(bit[:, :], bit_f[:, :]))
                    dve.wait_ge(totalled.sem, totalled.now(b, 1))
                    search.link(dve.scalar_tensor_tensor(out=raised[:, :], in0=p_count[:, 0:NE], scalar=float(CAP), in1=tried_f[:, :],
                                                         op0=ALU.is_ge, op1=ALU.mult))
                    search.link(dve.tensor_tensor(limit[:, :], limit[:, :], raised[:, :], ALU.bitwise_xor))
                    search.end()

                threshold = each(limit[:, :].bitcast(F32))
                ch.link(dve.tensor_tensor(equal[:, :, :], own[:, :, :], threshold, ALU.is_equal))
                ch.link(dve.tensor_tensor(equal[:, :, :], equal[:, :, :], rt.mask[:, :, :], ALU.mult))
                ch.link(dve.tensor_tensor(rt.mask[:, :, :], own[:, :, :], threshold, ALU.is_gt))
                rt.dve_places(dve, ch)
                ch.link(dve.tensor_copy(above[:, :, :], rt.mask[:, :, :]))
                ch.link(dve.tensor_tensor(score[:, :, :], rt.place[:, :, :], above[:, :, :], ALU.mult))
                ch.link(dve.tensor_copy(n_above[:, :], rt.until[0:TR, NT - 1]))
                ch.link(dve.tensor_copy(rt.mask[:, :, :], equal[:, :, :]))
                rt.dve_places(dve, ch)
                ch.link(dve.tensor_tensor(rt.place[:, :, :], rt.place[:, :, :], each(n_above[:, :]), ALU.add))
                ch.link(dve.scalar_tensor_tensor(out=equal[:, :, :], in0=rt.place[:, :, :], scalar=float(CAP), in1=equal[:, :, :],
                                                 op0=ALU.is_lt, op1=ALU.mult))
                ch.link(dve.tensor_tensor(rt.place[:, :, :], rt.place[:, :, :], equal[:, :, :], ALU.mult))
                ch.link(dve.tensor_tensor(rt.place[:, :, :], rt.place[:, :, :], score[:, :, :], ALU.add))
                ch.link(dve.tensor_tensor(above[:, :, :], above[:, :, :], equal[:, :, :], ALU.add))
                ch.link(dve.tensor_tensor(rt.place[:, :, :], rt.place[:, :, :], each(expert_slot[:, :]), ALU.add))
                ch.link(dve.tensor_tensor(rt.place[:, :, :], rt.place[:, :, :], above[:, :, :], ALU.mult))
                ch.link(dve.tensor_scalar(rt.place[:, :, :], rt.place[:, :, :], float(SLOTS1), None, ALU.add))
                ch.link(dve.tensor_tensor(above[:, :, :], above[:, :, :], lg, ALU.mult))
                for i, chosen in enumerate((rt.first, rt.second)):
                    rt.dve_take(dve, ch, rt.place[:, :, :], chosen, rt.slot_f[:, i])
                    rt.dve_take(dve, ch, above[:, :, :], chosen, weight[:, i])
                ch.link(dve.tensor_copy(rt.slot[:, :, :], rt.slot_f[:, :, :]))
                ch.link(dve.tensor_scalar(gather_slot[:, :, :], rt.slot_f[:, :, :], float(SLOTS1 - 1), None, ALU.min))

    shared_expert(nc, A, keep, sem, 0, lambda pool: pool_scatter(pool, slots, rows, xs, SLOTS1 - 1, scattered, None))

    with ExitStack() as inner:
        sb2 = lambda name, shape, dt: inner.enter_context(nc.sbuf_tensor(name, shape, dt))
        pb2 = lambda name, shape, dt: inner.enter_context(nc.psum_tensor(name, shape, dt))
        ex = Experts(nc, sem, sb2, pb2, "ex1", R, NE // 2, CAP // N, True)

        with nc.Block() as block:

            @block.sync
            def _(sp):
                ex.sp_ahead(sp)
                ex.x_load(sp, None, 0, xs[0:N].rearrange("(j p) d -> p j d", p=R))
                with sp.Fori(0, ex.turns) as b:
                    ex.x_load(sp, b, 1, chunk_rows(xs, b, 4, 1, R))
                    for i in range(4):
                        if i < 3:
                            ex.x_load(sp, b, i + 2, chunk_rows(xs, b, 4, i + 2, R))
                        ex.y_store(sp, b, i, chunk_rows(ys, b, 4, i, R))
                for u in range(2):
                    sp.wait_ge(ex.y_out[u].sem, ex.y_out[u].now(ex.turns, 0))

            @block.gpsimd
            def _(pool):
                def load(b, s, e):
                    for p, (name, k) in enumerate((("ew1", KD), ("ew3", KD), ("ew2", 4))):
                        ex.raw_free(pool, b, s, p)
                        pool.sem_inc(rseen, 1)
                        pool.dma_start(ex.raw[p][:, :].unsqueeze(1),
                                       A["L1_ffn_" + name][e].rearrange("e (p k) n -> p e (k n)", k=k)).then_inc(ex.raw_in[p].sem, 16)

                load(None, 0, slice(0, 1))
                with pool.Fori(0, ex.turns - 1) as b:
                    for s in range(1, 3):
                        load(b, s, bass.ds(b * 2 + s, 1))
                load(ex.turns - 1, 1, slice(NE - 1, NE))
                load(ex.turns - 1, 2, slice(0, 1))
                for p in ex.pieces:
                    pool.wait_ge(ex.raw_in[p].sem, ex.raw_in[p].now(ex.turns, 0))

            @block.scalar
            def _(act):
                ex.act_ahead(act)
                for p in ex.pieces:
                    ex.w_high_part(act, None, 0, p)
                ex.act_x(act, None, 0)
                with act.Fori(0, ex.turns) as b:
                    for i in range(4):
                        ex.act_chunk(act, b, i)

            @block.tensor
            def _(pe):
                ex.pe_ahead(pe)
                ex.pe_turn(pe, None, 0, ident)
                with pe.Fori(0, ex.turns) as b:
                    for i in range(4):
                        ex.pe_up(pe, b, i)
                        ex.pe_turn(pe, b, i + 1, ident)
                        ex.pe_down(pe, b, i)

            @block.vector
            def _(dve):
                ex.dve_ahead(dve)
                for p in ex.pieces:
                    ex.w_low_part(dve, None, 0, p)
                ex.dve_x(dve, None, 0)
                with dve.Fori(0, ex.turns) as b:
                    for i in range(4):
                        ex.dve_chunk(dve, b, i)
                        ex.dve_out(dve, b, i)

    shared_expert(nc, A, keep, sem, 1, None, gather_slot, weight)


STAGES = (stage_front, stage_attention, stage_latent, stage_experts0, stage_distance, stage_experts1)


def build(nc, A, out):
    with ExitStack() as whole:
        def sem(name):
            return whole.enter_context(nc.semaphore(name))

        def big(name):
            return whole.enter_context(nc.sbuf_tensor(name, [TR, NT + NJ, D], F32))

        keep = {
            "ident": whole.enter_context(nc.sbuf_tensor("ident", [128, 128], F32)),
            "logits0": whole.enter_context(nc.sbuf_tensor("logits0", [TR, NT + NJ, 8], F32)),
            "logits1": whole.enter_context(nc.sbuf_tensor("logits1", [TR, NT + NJ, 16], F32)),
            "slots0": whole.enter_context(nc.sbuf_tensor("slots0", [TR, 2, NT], I32)),
            "weight0": whole.enter_context(nc.sbuf_tensor("weight0", [TR, 2, NT + NJ], F32)),
            "ident_done": sem("ident_done"),
            "h0": nc.dram_tensor("h0", [NTOK, D], F32).ap(),
            "xs": nc.dram_tensor("xs", [SLOTS0 + 512, D], F32).ap(),
            "ys": nc.dram_tensor("ys", [SLOTS0, D], F32).ap(),
            "out": out,
        }
        for stage in STAGES:
            if stage is stage_attention:
                keep["h"] = big("h")
            if stage is stage_latent:
                keep["rows"] = big("rows")
            with ExitStack() as here:
                stage_sems = []

                def stage_sem(name):
                    stage_sems.append(nc.alloc_semaphore(name=name))
                    return stage_sems[-1]

                sb = lambda name, shape, dt: here.enter_context(nc.sbuf_tensor(name, shape, dt))
                pb = lambda name, shape, dt: here.enter_context(nc.psum_tensor(name, shape, dt))
                stage(nc, A, keep, stage_sem, sb, pb)
            nc.clear_and_free_semaphores(stage_sems)
            nc.all_engine_barrier()


_INS = ['x', 'x_txt', 'L0_tok_Wa', 'L0_tok_ba', 'L0_tok_Wd1', 'L0_tok_bd1', 'L0_tok_Wd2', 'L0_tok_bd2', 'L0_tok_Wd3',
        'L0_tok_bd3', 'L0_txt_weight', 'L0_txt_lora_A', 'L0_txt_lora_B', 'L0_attn_Wq', 'L0_attn_bq', 'L0_attn_Wk',
        'L0_attn_bk', 'L0_attn_Wv', 'L0_attn_bv', 'L0_attn_Wo', 'L0_attn_bo', 'L0_ffn_g1', 'L0_ffn_Wq', 'L0_ffn_Wdkv',
        'L0_ffn_Wuk', 'L0_ffn_Wuv', 'L0_ffn_Wo', 'L0_ffn_g2', 'L0_ffn_gate_w', 'L0_ffn_w1', 'L0_ffn_w2', 'L1_attn_U',
        'L1_ffn_gate_w', 'L1_ffn_gate_b', 'L1_ffn_ew1', 'L1_ffn_ew3', 'L1_ffn_ew2', 'L1_ffn_sw1', 'L1_ffn_sw3',
        'L1_ffn_sw2']


def kernel(**inputs):
    from concourse import bacc
    from concourse.bass_utils import run_bass_kernel_spmd

    nc = bacc.Bacc("TRN2", target_bir_lowering=False, num_devices=1)
    arrays, A = {}, {}
    for name in _INS:
        a = np.ascontiguousarray(inputs[name])
        arrays[f"in_{name}"] = a
        A[name] = nc.dram_tensor(f"in_{name}", a.shape, mybir.dt.from_np(a.dtype), kind="ExternalInput").ap()
    out = nc.dram_tensor("out_h", (B, S, D), F32, kind="ExternalOutput").ap()
    build(nc, A, out)
    return run_bass_kernel_spmd(nc, [arrays], core_ids=[0]).results[0]["out_h"]
```
